# Optimizing a Trainium2 kernel written in Bass

```python
import numpy as np
import jax
import jax.numpy as jnp

def _softmax(x, axis=-1):
    return jax.nn.softmax(x, axis=axis)

def _gelu(x):
    return jax.nn.gelu(x, approximate=True)

def _silu(x):
    return jax.nn.silu(x)

def _sigmoid(x):
    return jax.nn.sigmoid(x)

def _layernorm(x, axis=-1, eps=1e-05):
    m = jnp.mean(x, axis=axis, keepdims=True)
    v = jnp.var(x, axis=axis, keepdims=True)
    return (x - m) / jnp.sqrt(v + eps)

def _scatter_add(tgt, idx, src, axis=0):
    return tgt.at[idx].add(src)

def _segment_sum(src, seg, n):
    return jax.ops.segment_sum(src, seg, n)
kernel_name = 'mk_xattn_ffn_d1_seqx_r4_a789c2'

def setup_inputs(seed: int=0):
    np.random.seed(seed)
    _w = jnp.asarray

    def _rec_inputs():
        import jax
        import jax.numpy as jnp
        _rk = jax.random.key(seed)
        x = -0.0002928 + 1 * jax.random.normal(jax.random.fold_in(_rk, 1), (4, 512, 256), jnp.float32)
        _lenS = 512 - jax.random.randint(jax.random.fold_in(_rk, 7), (4,), 0, max(1, 512 // 4) + 1, jnp.int32)
        _lenS2 = 512 - jax.random.randint(jax.random.fold_in(_rk, 8), (4,), 0, max(1, 512 // 4) + 1, jnp.int32)
        _ctx_1024P = jax.random.normal(jax.random.fold_in(_rk, 11), (4, 16, 256), jnp.float32)
        _ctx_1024c = jax.random.dirichlet(jax.random.fold_in(_rk, 511), 0.3 * jnp.ones((16,), jnp.float32), (4, 512))
        _ctx_1024t = jnp.einsum('bsk,bkd->bsd', _ctx_1024c, _ctx_1024P)
        _ctx_1024t = _ctx_1024t * jax.lax.rsqrt(jnp.mean(jnp.square(_ctx_1024t)) + 1e-12) * 0.953939
        ctx_1024 = -1.39393e-06 + 0.999914 * (_ctx_1024t + 0.3 * jax.random.normal(jax.random.fold_in(_rk, 611), (4, 512, 256), jnp.float32))
        return (x, ctx_1024)
    x, ctx_1024 = _rec_inputs()

    def _L0_xattn_setup():
        import jax, jax.numpy as jnp
        import numpy as np
        import math
        D_MODEL = 256
        NUM_HEADS = 16
        D_K = D_MODEL // NUM_HEADS

        def _attention(q, k, v, Wq, bq, Wo, bo):
            B, S, _ = q.shape

            def proj(x):
                y = jnp.einsum('bsd,de->bse', x, Wq) + bq
                return y.reshape(B, S, NUM_HEADS, D_K).transpose(0, 2, 1, 3)
            qh, kh, vh = (proj(q), proj(k), proj(v))
            scores = jnp.einsum('bhsd,bhtd->bhst', qh, kh) / math.sqrt(D_K)
            attn = jax.nn.softmax(scores, axis=-1)
            out = jnp.einsum('bhst,bhtd->bhsd', attn, vh)
            out = out.transpose(0, 2, 1, 3).reshape(B, S, D_MODEL)
            return jnp.einsum('bsd,de->bse', out, Wo) + bo
        key = jax.random.key(seed)
        ks = jax.random.split(key, 7)
        B, S = (2, 512)
        scale = 1.0 / math.sqrt(D_MODEL)
        inp = {'q': jax.random.normal(ks[0], (B, S, D_MODEL), dtype=jnp.float32), 'k': jax.random.normal(ks[1], (B, S, D_MODEL), dtype=jnp.float32), 'v': jax.random.normal(ks[2], (B, S, D_MODEL), dtype=jnp.float32), 'Wq': jax.random.normal(ks[3], (D_MODEL, D_MODEL), dtype=jnp.float32) * scale, 'bq': jnp.zeros((D_MODEL,), dtype=jnp.float32), 'Wo': jax.random.normal(ks[4], (D_MODEL, D_MODEL), dtype=jnp.float32) * scale, 'bo': jnp.zeros((D_MODEL,), dtype=jnp.float32)}
        return inp
    _L0_xattn_all = _L0_xattn_setup()
    _L0_xattn_in = {k: v for k, v in _L0_xattn_all.items() if k in ('Wq', 'bq', 'Wo', 'bo')}
    del _L0_xattn_all

    def _L0_ffn_setup():
        import jax, jax.numpy as jnp
        import numpy as np
        from jax import lax
        D = 256
        H = 352
        E = 8
        K = 2
        ROUTER_SCALE = 1.0

        def _expert(x, w1, b1, w3, b3, w2, b2):
            h = jax.nn.silu((x @ w1 + b1) * (x @ w3 + b3))
            return h @ w2 + b2
        key = jax.random.key(seed)
        ks = jax.random.split(key, 16)
        s = 0.02
        inp = {'x': jax.random.normal(ks[0], (2, 512, D), dtype=jnp.float32), 'gate_w': jax.random.normal(ks[1], (E, D), dtype=jnp.float32) * s, 'gate_b': jax.random.normal(ks[2], (E,), dtype=jnp.float32) * s, 'w1': jax.random.normal(ks[3], (E, D, H), dtype=jnp.float32) * s, 'b1': jax.random.normal(ks[4], (E, H), dtype=jnp.float32) * s, 'w3': jax.random.normal(ks[5], (E, D, H), dtype=jnp.float32) * s, 'b3': jax.random.normal(ks[6], (E, H), dtype=jnp.float32) * s, 'w2': jax.random.normal(ks[7], (E, H, D), dtype=jnp.float32) * s, 'b2': jax.random.normal(ks[8], (E, D), dtype=jnp.float32) * s, 'sw1': jax.random.normal(ks[9], (D, H), dtype=jnp.float32) * s, 'sb1': jax.random.normal(ks[10], (H,), dtype=jnp.float32) * s, 'sw3': jax.random.normal(ks[11], (D, H), dtype=jnp.float32) * s, 'sb3': jax.random.normal(ks[12], (H,), dtype=jnp.float32) * s, 'sw2': jax.random.normal(ks[13], (H, D), dtype=jnp.float32) * s, 'sb2': jax.random.normal(ks[14], (D,), dtype=jnp.float32) * s}
        return inp
    _L0_ffn_all = _L0_ffn_setup()
    _L0_ffn_in = {k: v for k, v in _L0_ffn_all.items() if k in ('gate_w', 'gate_b', 'w1', 'b1', 'w3', 'b3', 'w2', 'b2', 'sw1', 'sb1', 'sw3', 'sb3', 'sw2', 'sb2')}
    del _L0_ffn_all
    return {'x': x, 'ctx_1024': ctx_1024, 'L0_xattn_Wq': _L0_xattn_in['Wq'], 'L0_xattn_bq': _L0_xattn_in['bq'], 'L0_xattn_Wo': _L0_xattn_in['Wo'], 'L0_xattn_bo': _L0_xattn_in['bo'], 'L0_ffn_gate_w': _L0_ffn_in['gate_w'], 'L0_ffn_gate_b': _L0_ffn_in['gate_b'], 'L0_ffn_w1': _L0_ffn_in['w1'], 'L0_ffn_b1': _L0_ffn_in['b1'], 'L0_ffn_w3': _L0_ffn_in['w3'], 'L0_ffn_b3': _L0_ffn_in['b3'], 'L0_ffn_w2': _L0_ffn_in['w2'], 'L0_ffn_b2': _L0_ffn_in['b2'], 'L0_ffn_sw1': _L0_ffn_in['sw1'], 'L0_ffn_sb1': _L0_ffn_in['sb1'], 'L0_ffn_sw3': _L0_ffn_in['sw3'], 'L0_ffn_sb3': _L0_ffn_in['sb3'], 'L0_ffn_sw2': _L0_ffn_in['sw2'], 'L0_ffn_sb2': _L0_ffn_in['sb2']}

def reference(x, ctx_1024, L0_xattn_Wq, L0_xattn_bq, L0_xattn_Wo, L0_xattn_bo, L0_ffn_gate_w, L0_ffn_gate_b, L0_ffn_w1, L0_ffn_b1, L0_ffn_w3, L0_ffn_b3, L0_ffn_w2, L0_ffn_b2, L0_ffn_sw1, L0_ffn_sb1, L0_ffn_sw3, L0_ffn_sb3, L0_ffn_sw2, L0_ffn_sb2):
    import jax
    import jax.numpy as jnp

    def _L0_xattn_ref(q, k, v, Wq, bq, Wo, bo):
        import jax, jax.numpy as jnp
        import numpy as np
        import math
        D_MODEL = 256
        NUM_HEADS = 16
        D_K = D_MODEL // NUM_HEADS

        def _attention(q, k, v, Wq, bq, Wo, bo):
            B, S, _ = q.shape

            def proj(x):
                y = jnp.einsum('bsd,de->bse', x, Wq) + bq
                return y.reshape(B, S, NUM_HEADS, D_K).transpose(0, 2, 1, 3)
            qh, kh, vh = (proj(q), proj(k), proj(v))
            scores = jnp.einsum('bhsd,bhtd->bhst', qh, kh) / math.sqrt(D_K)
            attn = jax.nn.softmax(scores, axis=-1)
            out = jnp.einsum('bhst,bhtd->bhsd', attn, vh)
            out = out.transpose(0, 2, 1, 3).reshape(B, S, D_MODEL)
            return jnp.einsum('bsd,de->bse', out, Wo) + bo
        return _attention(q, k, v, Wq, bq, Wo, bo)

    def _L0_ffn_ref(x, gate_w, gate_b, w1, b1, w3, b3, w2, b2, sw1, sb1, sw3, sb3, sw2, sb2):
        import jax, jax.numpy as jnp
        import numpy as np
        from jax import lax
        D = 256
        H = 352
        E = 8
        K = 2
        ROUTER_SCALE = 1.0

        def _expert(x, w1, b1, w3, b3, w2, b2):
            h = jax.nn.silu((x @ w1 + b1) * (x @ w3 + b3))
            return h @ w2 + b2
        shape = x.shape
        xf = x.reshape(-1, D)
        T = xf.shape[0]
        scores = jax.nn.softmax(xf @ gate_w.T, axis=-1)
        biased = scores + gate_b
        _, idx = lax.top_k(biased, K)
        w = jnp.take_along_axis(scores, idx, axis=-1) * ROUTER_SCALE
        rw = jnp.zeros((T, E), dtype=xf.dtype).at[jnp.arange(T)[:, None], idx].add(w)
        h = jax.nn.silu((jnp.einsum('td,edh->teh', xf, w1) + b1) * (jnp.einsum('td,edh->teh', xf, w3) + b3))
        oe = jnp.einsum('teh,ehd->ted', h, w2) + b2
        y = jnp.einsum('te,ted->td', rw, oe)
        z = _expert(xf, sw1, sb1, sw3, sb3, sw2, sb2)
        return (y + z).reshape(shape)
    x = x + _L0_xattn_ref(_layernorm(x, axis=-1), ctx_1024, ctx_1024, L0_xattn_Wq, L0_xattn_bq, L0_xattn_Wo, L0_xattn_bo)
    x = x + _L0_ffn_ref(_layernorm(x, axis=-1), L0_ffn_gate_w, L0_ffn_gate_b, L0_ffn_w1, L0_ffn_b1, L0_ffn_w3, L0_ffn_b3, L0_ffn_w2, L0_ffn_b2, L0_ffn_sw1, L0_ffn_sb1, L0_ffn_sw3, L0_ffn_sb3, L0_ffn_sw2, L0_ffn_sb2)
    return x

_drawn_inputs = setup_inputs


def setup_inputs(seed=0):
    import zlib

    import numpy as np

    out = dict(_drawn_inputs(seed))
    spreads = {'L0_xattn_bq': (0.0, 0.1), 'L0_xattn_bo': (0.0, 0.1)}
    factors = {'L0_ffn_gate_w': 8.0,
     'L0_ffn_gate_b': 8.0,
     'L0_ffn_w1': 8.0,
     'L0_ffn_b1': 8.0,
     'L0_ffn_w3': 8.0,
     'L0_ffn_b3': 8.0,
     'L0_ffn_w2': 8.0,
     'L0_ffn_b2': 40.143,
     'L0_ffn_sw1': 3.433,
     'L0_ffn_sb1': 31.05,
     'L0_ffn_sw3': 3.378,
     'L0_ffn_sb3': 32.406,
     'L0_ffn_sw2': 3.381,
     'L0_ffn_sb2': 27.272}
    for name, (base, spread) in spreads.items():
        noise = np.random.default_rng([zlib.crc32(name.encode()), seed]).standard_normal(out[name].shape)
        drawn = base * np.exp(spread * noise) if base else spread * noise
        out[name] = jnp.asarray(drawn.astype(out[name].dtype))
    for name, factor in factors.items():
        out[name] = (out[name] * factor).astype(out[name].dtype)
    return out
```

```python
from contextlib import ExitStack

import concourse.bass as bass
from concourse import mybir

ALU = mybir.AluOpType
ACT = mybir.ActivationFunctionType
AX_X = mybir.AxisListType.X
F32 = mybir.dt.float32
BF16 = mybir.dt.bfloat16
I32 = mybir.dt.int32

P = 128
EPS = 1e-5
TOP_K = 2


def xattn_moe_kernel(nc, x, ctx_in, wq, bq, wo, bo, gate_wt, gate_b, w1, b1, w3, b3, w2, b2,
                     sw1, sb1, sw3, sb3, sw2, sb2, out):
    B, S, D = x.shape
    T = B * S
    NT = T // P
    TB = S // P
    DK = 16
    H = D // DK
    GH = 4
    NG = H // GH
    KC = D // P
    E, _, F = w1.shape
    FC = -(-F // P)
    FL = F - (FC - 1) * P
    MAX_BLOCKS = (T * TOP_K + E * (P - 1)) // P
    assert S == 512 and D == 256 and H == 16 and FL % 32 == 0 and FL < P
    SCALE = float(DK) ** -0.5

    x_v = x.rearrange("b (j p) d -> b p j d", p=P)
    ctx_v = ctx_in.rearrange("b (j p) d -> b p j d", p=P)
    out_v = out.rearrange("b (j p) d -> (b j) p d", p=P)

    q_dram = nc.dram_tensor("q_parts", (B, NG, 3, DK, GH, S), BF16).ap()
    k_dram = nc.dram_tensor("k_parts", (B, NG, 3, DK, GH, S), BF16).ap()
    xs_dram = nc.dram_tensor("slot_rows", (MAX_BLOCKS * P, D), F32).ap()
    os_dram = nc.dram_tensor("slot_results", (MAX_BLOCKS * P, D), F32).ap()

    with ExitStack() as stack:
        def sb(name, shape, dt=F32):
            return stack.enter_context(nc.sbuf_tensor(name, shape, dt))

        def sem(name):
            return stack.enter_context(nc.semaphore(name))

        xres = sb("xres", [P, NT, D])
        xn = sb("xn", [P, NT, D])
        wq_sb = sb("wq_sb", [P, KC, D])
        bq_sb = sb("bq_sb", [P, KC])
        bqs_sb = sb("bqs_sb", [P, KC])
        wo_sb = sb("wo_sb", [P, NG, D])
        ident = sb("ident", [P, P])
        ident_b = sb("ident_b", [P, P], BF16)
        stats = sb("stats", [P, TB, 6])
        mv = sb("mv", [P, TB, 2])
        var = sb("var", [P, TB])
        lnv = sb("lnv", [P, TB])
        y0 = sb("y0", [P, TB])
        newt = sb("newt", [P, TB])
        rstd = sb("rstd", [P, TB])
        aT = sb("aT", [P, NG, S])
        tA = sb("tA", [P, S // 32, 32])
        tB = sb("tB", [P, S // 32, 32])
        rsum = sb("rsum", [P, S // 32])
        nmax = sb("nmax", [P, 2, GH * TB])
        mparts = sb("mparts", [P, 2, GH * TB], BF16)
        mT = sb("mT", [2 * GH * TB, P], BF16)
        sw13_sb = sb("sw13_sb", [P, KC, 2 * F])
        sw2_sb = sb("sw2_sb", [P, FC, D])
        sb13_sb = sb("sb13_sb", [P, FC, 2])
        gw_sb = sb("gw_sb", [P, KC, E])
        gb_sb = sb("gb_sb", [P, E])

        W13_N, W2_N, B13_N = E * KC * 2 * F, E * FC * D, E * 2 * F
        QK_N, V_N, PR_N, VG_N = NG * GH * S // 2, NT * D, 8 * S, 2 * TB * GH * 32
        arena = sb("arena", [P, max(W13_N + W2_N + B13_N, 2 * QK_N + V_N + PR_N + VG_N)])
        q_st = arena[:, 0:QK_N].bitcast(BF16).rearrange("p (g h s) -> p g h s", g=NG, h=GH)
        k_st = arena[:, QK_N:2 * QK_N].bitcast(BF16).rearrange("p (g h s) -> p g h s", g=NG, h=GH)
        o = 2 * QK_N
        v_all = arena[:, o:o + V_N].rearrange("p (j h d) -> p j h d", j=NT, h=H)
        o += V_N
        probs = arena[:, o:o + PR_N].rearrange("p (r s) -> p r s", r=8)
        o += PR_N
        v_grp = arena[:, o:o + VG_N].rearrange("p (r j h d) -> p r j h d", r=2, j=TB, h=GH)
        w13_sb = arena[:, 0:W13_N].rearrange("p (e k f) -> p e k f", e=E, k=KC)
        w2_sb = arena[:, W13_N:W13_N + W2_N].rearrange("p (e c d) -> p e c d", e=E, c=FC)
        b13_sb = arena[:, W13_N + W2_N:W13_N + W2_N + B13_N].rearrange("p (e f) -> p e f", e=E)

        PB = [("cst", 2 * TB * D), ("xT", KC * S), ("cT", KC * S), ("kf", KC * S), ("qf", KC * S),
              ("qparts", 3 * KC * S // 2), ("kparts", 3 * KC * S // 2)]
        FB = [("x2T", KC * T), ("lgT", S), ("sa", 2 * S), ("sz", 2 * S), ("shT", FC * S)]
        EB = [("xb", 2 * D), ("xbT", 2 * D), ("ez", 2 * F), ("eh", 2 * F),
              ("ehT", 2 * FC * P), ("eo", 2 * D)]
        assert sum(n for _, n in EB) <= KC * T
        work = sb("work", [P, max(sum(n for _, n in PB), sum(n for _, n in FB))])

        def carve(parts):
            at, got = 0, {}
            for name, n in parts:
                got[name] = work[:, at:at + n]
                at += n
            return got

        pb, fb, eb = carve(PB), carve(FB), carve(EB)
        cst = pb["cst"].rearrange("p (r j d) -> p r j d", r=2, j=TB)
        xT = pb["xT"].rearrange("p (k s) -> p k s", k=KC)
        cT = pb["cT"].rearrange("p (k s) -> p k s", k=KC)
        kf = pb["kf"].rearrange("p (k s) -> p k s", k=KC)
        qf = pb["qf"].rearrange("p (k s) -> p k s", k=KC)
        qparts = pb["qparts"].bitcast(BF16).rearrange("p (t k s) -> p t k s", t=3, k=KC)
        kparts = pb["kparts"].bitcast(BF16).rearrange("p (t k s) -> p t k s", t=3, k=KC)
        x2T = fb["x2T"].rearrange("p (k t) -> p k t", k=KC)
        lgT = fb["lgT"]
        sh_a = fb["sa"].rearrange("p (r s) -> p r s", r=2)
        sh_z = fb["sz"].rearrange("p (r s) -> p r s", r=2)
        sh_hT = fb["shT"].rearrange("p (c s) -> p c s", c=FC)
        xb = eb["xb"].rearrange("p (r d) -> p r d", r=2)
        xbT = eb["xbT"].rearrange("p (r k s) -> p r k s", r=2, k=KC)
        e_a, e_c = fb["sa"][:, 0:F], fb["sa"][:, F:2 * F]
        e_z = eb["ez"].rearrange("p (r f) -> p r f", r=2)
        e_h = eb["eh"].rearrange("p (r f) -> p r f", r=2)
        e_hT = eb["ehT"].rearrange("p (r c s) -> p r c s", r=2, c=FC)
        e_o = eb["eo"].rearrange("p (r d) -> p r d", r=2)
        gath = fb["x2T"][:, 0:4 * TOP_K * D].rearrange("p (r k d) -> p r k d", r=4, k=TOP_K)

        lg = sb("lg", [P, NT, E])
        lsh = sb("lsh", [P, NT, E])
        lex = sb("lex", [P, NT, E])
        sco = sb("sco", [P, NT, E])
        bia = sb("bia", [P, NT, E])
        cand = sb("cand", [P, NT, E])
        oneh = sb("oneh", [P, TOP_K, NT, E])
        rt1 = sb("rt1", [P, NT])
        rt2 = sb("rt2", [P, NT])
        rw = sb("rw", [P, TOP_K, NT])
        selb = sb("selb", [P, NT, E], BF16)
        tri = sb("tri", [P, P], BF16)
        ones_b = sb("ones_b", [P, P], BF16)
        cum = sb("cum", [P, NT + 1, E])
        iota_e = sb("iota_e", [P, E])
        iota_n = sb("iota_n", [P, MAX_BLOCKS])
        iota_c = sb("iota_c", [P, NT])
        cmpc = sb("cmpc", [P, E, NT])
        nblk = sb("nblk", [P, E])
        bend = sb("bend", [P, E + 1])
        off = sb("off", [P, E])
        cmpn = sb("cmpn", [P, MAX_BLOCKS, E])
        blkf = sb("blkf", [P, MAX_BLOCKS])
        blk = sb("blk", [P, MAX_BLOCKS], I32)
        slotf = sb("slotf", [P, TOP_K, NT])
        slot = sb("slot", [P, TOP_K, NT], I32)
        zrow = sb("zrow", [P, D])

        ps = stack.enter_context(nc.psum_tensor("ps", [P, 8, 512], F32))
        stack.enter_context(nc.allow_non_contiguous_dma(reason="a few bias vectors, one value per partition"))

        s_const = sem("s_const")
        s_wq = sem("s_wq")
        s_bq = sem("s_bq")
        s_wo = sem("s_wo")
        s_sw = sem("s_sw")
        s_zero = sem("s_zero")
        s_ew = sem("s_ew")
        s_x = [sem(f"s_x{b}") for b in range(B)]
        s_c = [sem(f"s_c{r}") for r in range(2)]
        s_dve = sem("s_dve")
        s_act = sem("s_act")
        s_pool = sem("s_pool")
        s_var = sem("s_var")
        s_y0 = sem("s_y0")
        s_xn = sem("s_xn")
        s_cTp = sem("s_cTp")
        s_xTp = sem("s_xTp")
        s_cT = sem("s_cT")
        s_xT = sem("s_xT")
        s_kp = sem("s_kp")
        s_qp = sem("s_qp")
        s_kf = sem("s_kf")
        s_qf = sem("s_qf")
        s_vp = sem("s_vp")
        s_v = sem("s_v")
        s_ks = sem("s_ks")
        s_qs = sem("s_qs")
        s_kd = sem("s_kd")
        s_qd = sem("s_qd")
        s_st = [sem(f"s_st{g}") for g in range(NG)]
        s_mrow = [sem(f"s_mrow{g}") for g in range(NG)]
        s_ones = sem("s_ones")
        s_rp = sem("s_rp")
        s_rc = sem("s_rc")
        s_mp = sem("s_mp")
        s_mT = sem("s_mT")
        s_s2 = sem("s_s2")
        s_exp = sem("s_exp")
        s_pv = sem("s_pv")
        s_pvc = sem("s_pvc")
        s_vg = sem("s_vg")
        s_norm = sem("s_norm")
        s_gTp = sem("s_gTp")
        s_gT = sem("s_gT")
        s_gp = sem("s_gp")
        s_ge = sem("s_ge")
        s_glp = sem("s_glp")
        s_gl = sem("s_gl")
        s_lsh = sem("s_lsh")
        s_lex = sem("s_lex")
        s_sel = sem("s_sel")
        s_cnt = sem("s_cnt")
        s_route = sem("s_route")
        s_scat = sem("s_scat")
        s_up1 = sem("s_up1")
        s_a1 = sem("s_a1")
        s_z1 = sem("s_z1")
        s_h1 = sem("s_h1")
        s_dn1 = sem("s_dn1")
        s_y1 = sem("s_y1")
        s_xb = [sem(f"s_xb{r}") for r in range(2)]
        s_xbp = sem("s_xbp")
        s_xbe = sem("s_xbe")
        s_up = sem("s_up")
        s_upc = sem("s_upc")
        s_z = sem("s_z")
        s_h = sem("s_h")
        s_hp = sem("s_hp")
        s_hT = sem("s_hT")
        s_o = sem("s_o")
        s_oe = sem("s_oe")
        s_os = [sem(f"s_os{r}") for r in range(2)]
        s_g = [sem(f"s_g{r}") for r in range(4)]
        s_fin = sem("s_fin")
        s_out = sem("s_out")

        def loop(eng, lo, hi, body):
            with eng.Fori(lo, hi) as i:
                body(i)

        def pairs(eng, n, body):
            with eng.Fori(0, n // 2) as r:
                for par in range(2):
                    body(2 * r + par, par, r)

        PRE = 2 * GH * TB + 1
        PER = NG * (GH * TB + 1)
        BR, BS2, BPV = 0, 3, 7

        def ring_base(b):
            return PRE + PER + (PER + TB) * (b - 1) if not isinstance(b, int) or b else PRE

        def step_units(g, with_wo, with_s1, with_m):
            units = []
            for t in range(TB):
                if t == 1 and with_m:
                    units.append(("m", 0))
                if with_s1:
                    units += [("s1", t * TB + c) for c in range(TB)]
            if g == 0 and with_wo:
                units += [("wo", j) for j in range(TB)]
            return units

        def kinds(b, g):
            first, last = isinstance(b, int) and b == 0, isinstance(b, int) and b == B - 1
            return not first, not (last and g >= NG - 2), not (last and g == NG - 1)

        def batch_units(b):
            at, offs = 0, []
            for g in range(NG):
                offs.append(at)
                at += len(step_units(g, *kinds(b, g)))
            return offs, at

        def bank_of(b, k):
            return (ring_base(b if isinstance(b, int) and b == 0 else 1) + k) % 3

        RING_END = ring_base(B - 1) + batch_units(B - 1)[1]

        block = stack.enter_context(nc.Block())

        @block.sync
        def _(sp):
            sp.dma_start(wq_sb[:, :, :], wq.rearrange("(k p) e -> p k e", p=P)).then_inc(s_wq, 16)
            sp.dma_start(bq_sb[:, :], bq.rearrange("(k p) -> p k", p=P)).then_inc(s_bq, 16)
            sp.wait_ge(s_const, 3)

            def load(b, r, n):
                if n:
                    sp.wait_ge(s_cTp, 2 * (b - 1))
                sp.dma_start(cst[:, r, :, :], ctx_v[b]).then_inc(s_c[r], 16)

            sp.sem_inc(s_kd, 16 * 12)
            sp.sem_inc(s_qd, 16 * 12)
            for r in range(2):
                sp.sem_inc(s_os[r], 16)
            for b in range(B):
                if b < 2:
                    load(b, b, 0)
                sp.dma_start(xres[:, TB * b:TB * b + TB, :], x_v[b]).then_inc(s_x[b], 16)
            for g in range(NG):
                for j in range(GH):
                    h = GH * g + j
                    sp.dma_start(wo_sb[32 * j:32 * j + DK, g, :], wo[DK * h:DK * h + DK, :]).then_inc(s_wo, 16)
            sp.dma_start(wo_sb[DK:DK + 1, 0, :], bo.rearrange("(a d) -> a d", a=1)).then_inc(s_wo, 16)
            sp.dma_start(sw13_sb[:, :, 0:F], sw1.rearrange("(k p) f -> p k f", p=P)).then_inc(s_sw, 16)
            sp.dma_start(sw13_sb[:, :, F:2 * F], sw3.rearrange("(k p) f -> p k f", p=P)).then_inc(s_sw, 16)
            sp.dma_start(sw2_sb[:, 0:FC - 1, :], sw2[0:(FC - 1) * P, :].rearrange("(c p) d -> p c d", p=P)).then_inc(s_sw, 16)
            sp.dma_start(sw2_sb[0:FL, FC - 1, :], sw2[(FC - 1) * P:F, :]).then_inc(s_sw, 16)
            sp.dma_start(sw2_sb[FL:FL + 1, FC - 1, :], sb2.rearrange("(a d) -> a d", a=1)).then_inc(s_sw, 16)
            for n, bias in enumerate((sb1, sb3)):
                sp.dma_start(sb13_sb[:, 0:FC - 1, n], bias[0:(FC - 1) * P].rearrange("(c p) -> p c", p=P)).then_inc(s_sw, 16)
                sp.dma_start(sb13_sb[0:FL, FC - 1, n:n + 1], bias[(FC - 1) * P:F].rearrange("(p a) -> p a", a=1)).then_inc(s_sw, 16)
            sp.dma_start(gw_sb[:, :, :], gate_wt.rearrange("(k p) e -> p k e", p=P)).then_inc(s_sw, 16)
            sp.dma_start(gb_sb[:, :], gate_b.rearrange("(a e) -> a e", a=1).to_broadcast([P, E])).then_inc(s_sw, 16)
            sp.dma_start(xs_dram.rearrange("(n p) d -> p n d", p=P),
                         zrow[:, :].rearrange("p (a d) -> p a d", a=1).to_broadcast([P, MAX_BLOCKS, D])).then_inc(s_zero, 16)

            def parts_out(b, par, r):
                for ready, parts, dram, s in ((s_ks, kparts, k_dram, s_kd), (s_qs, qparts, q_dram, s_qd)):
                    sp.wait_ge(ready, b + 2)
                    for part in range(3):
                        for c in range(KC):
                            for gg in range(2):
                                sp.dma_start(dram[b, 2 * c + gg, part].rearrange("d h s -> h d s"),
                                             parts[64 * gg:64 * gg + 64, part, c, :]).then_inc(s, 16)

            parts_out(0, 0, 0)
            for b in range(2, B):
                load(b, b % 2, 1)
                parts_out(b - 1, 0, 0)
            parts_out(B - 1, 0, 0)

            def stacks(b, g):
                for dst, dram, rows in ((q_st, q_dram, (0, 0, 0, 1, 1, 2)), (k_st, k_dram, (0, 1, 2, 0, 1, 0))):
                    for n, part in enumerate(rows):
                        sp.dma_start(dst[DK * n:DK * n + DK, g, :, :], dram[b, g, part]).then_inc(s_st[g], 16)

            sp.wait_ge(s_kd, 16 * 12 * (B + 1))
            sp.wait_ge(s_qd, 16 * 12 * (B + 1))
            for g in range(NG):
                stacks(0, g)

            def mrow(b, g, n):
                sp.wait_ge(s_mT, n + 1)
                for part in range(2):
                    sp.dma_start(q_st[96 + part:97 + part, g, :, :],
                                 mT[GH * TB * part:GH * TB * (part + 1), :]).then_inc(s_mrow[g], 16)

            mrow(0, 0, 0)

            def steps(b):
                _, _, _ = kinds(b, 0)
                last = isinstance(b, int) and b == B - 1
                for g in range(NG):
                    i = NG * b + g
                    if not (last and g == NG - 1):
                        mrow(b if g < NG - 1 else b + 1, (g + 1) % NG, i + 1)
                    if not last:
                        sp.wait_ge(s_s2, 2 * TB * (i + 1))
                        stacks(b + 1, g)

            steps(0)
            loop(sp, 1, B - 1, steps)
            steps(B - 1)

            sp.wait_ge(s_pv, 2 + TB * NG * B)
            sp.wait_ge(s_vg, NG * B)
            for e in range(E):
                sp.dma_start(w13_sb[:, e, :, 0:F], w1[e].rearrange("(k p) f -> p k f", p=P)).then_inc(s_ew, 16)
                sp.dma_start(w13_sb[:, e, :, F:2 * F], w3[e].rearrange("(k p) f -> p k f", p=P)).then_inc(s_ew, 16)
                sp.dma_start(w2_sb[:, e, 0:FC - 1, :], w2[e, 0:(FC - 1) * P, :].rearrange("(c p) d -> p c d", p=P)).then_inc(s_ew, 16)
            sp.dma_start(w2_sb[0:FL, :, FC - 1, :], w2[:, (FC - 1) * P:F, :].rearrange("e p d -> p e d")).then_inc(s_ew, 16)
            sp.dma_start(w2_sb[FL:FL + 1, :, FC - 1, :], b2.rearrange("(a e) d -> a e d", a=1)).then_inc(s_ew, 16)
            for n, bias in enumerate((b1, b3)):
                sp.dma_start(b13_sb[:, :, n * F:n * F + F],
                             bias.rearrange("(a e) f -> a e f", a=1).to_broadcast([P, E, F])).then_inc(s_ew, 16)

            sp.wait_ge(s_scat, 16 * TOP_K * NT)
            sp.wait_ge(s_up1, FC * B)

            def rows_in(n, par):
                sp.wait_ge(s_xbp, n + 1)
                sp.dma_start(xb[:, par, :], xs_dram.rearrange("(n p) d -> n p d", p=P)[n]).then_inc(s_xb[par], 16)

            def results_out(n, par):
                sp.wait_ge(s_oe, n + 3)
                sp.dma_start(os_dram.rearrange("(n p) d -> n p d", p=P)[n], e_o[:, par, :]).then_inc(s_os[par], 16)

            rows_in(0, 0)
            rows_in(1, 1)

            def blocks(n, par, r):
                rows_in(n + 2, par)
                results_out(n, par)

            NP = (MAX_BLOCKS - 3) // 2 * 2
            pairs(sp, NP, blocks)
            for n in range(NP, MAX_BLOCKS):
                if n + 2 < MAX_BLOCKS:
                    rows_in(n + 2, n % 2)
                results_out(n, n % 2)

            for j in range(NT):
                sp.wait_ge(s_fin, j + 1)
                sp.dma_start(out_v[j], xres[:, j, :]).then_inc(s_out, 16)
            sp.wait_ge(s_out, 16 * NT)

        @block.gpsimd
        def _(pool):
            chain = [0]

            def link(ins):
                chain[0] += 1
                ins.then_inc(s_pool, 1)
                pool.wait_ge(s_pool, chain[0])

            pool.memset(wo_sb[:, :, :], 0.0).then_inc(s_const, 1)
            pool.memset(sw2_sb[:, FC - 1, :], 1.0).then_inc(s_const, 1)
            pool.memset(zrow[:, :], 0.0).then_inc(s_const, 1)
            link(pool.memset(ident[:, :], 0.0))
            link(pool.memset(ident_b[:, :], 0.0))
            link(pool.memset(tri[:, :], 1.0))
            for m in (ident, ident_b):
                pool.affine_select(out=m[:, :], in_=m[:, :], compare_op=ALU.not_equal, fill=1.0, base=0,
                                   pattern=[[-1, P]], channel_multiplier=1).then_inc(s_const, 1)
            pool.affine_select(out=tri[:, :], in_=tri[:, :], compare_op=ALU.is_gt, fill=0.0, base=0,
                               pattern=[[1, P]], channel_multiplier=-1).then_inc(s_const, 1)
            pool.memset(ones_b[:, :], 1.0).then_inc(s_const, 1)
            pool.iota(iota_e[:, :], [[1, E]], base=-E, channel_multiplier=0,
                      allow_small_or_imprecise_dtypes=True).then_inc(s_const, 1)
            pool.iota(iota_n[:, :], [[1, MAX_BLOCKS]], base=0, channel_multiplier=0,
                      allow_small_or_imprecise_dtypes=True).then_inc(s_const, 1)
            pool.iota(iota_c[:, :], [[P, NT]], base=0, channel_multiplier=0,
                      allow_small_or_imprecise_dtypes=True).then_inc(s_const, 1)
            link(pool.memset(tB[:, :, :], 0.0))
            pool.memset(tB[:, :, DK:DK + 1], 1.0).then_inc(s_const, 1)
            pool.sem_inc(s_ks, 1)

            def split(b):
                pool.wait_ge(s_kf, 2 * b + 4)
                pool.wait_ge(s_kd, 16 * 12 * (b + 1))
                pool.wait_ge(s_pool, 4 + 3 * b)
                pool.tensor_copy(kparts[:, 0, :, :], kf[:, :, :]).then_inc(s_pool, 1)
                pool.wait_ge(s_pool, 5 + 3 * b)
                pool.wait_ge(s_vp, 2 * b + 4)
                pool.tensor_tensor(kf[:, :, :], kf[:, :, :], kparts[:, 0, :, :], ALU.subtract).then_inc(s_pool, 1)
                pool.wait_ge(s_pool, 6 + 3 * b)
                pool.tensor_copy(kparts[:, 1, :, :], kf[:, :, :]).then_inc(s_pool, 1)
                pool.wait_ge(s_pool, 7 + 3 * b)
                pool.tensor_tensor(kparts[:, 2, :, :], kf[:, :, :], kparts[:, 1, :, :], ALU.subtract).then_inc(s_ks, 1)

            for b in range(B):
                split(b)

            def v_group(b, g):
                i = NG * b + g
                if i >= 2:
                    pool.wait_ge(s_pv, TB * (i - 1) + 2)
                pool.tensor_copy(v_grp[:, g % 2, :, :, 0:DK],
                                 v_all[:, TB * b:TB * b + TB, GH * g:GH * g + GH, :]).then_inc(s_vg, 1)

            pool.wait_ge(s_v, 2 + 2 * B)
            for i in range(NG * B):
                v_group(i // NG, i % NG)

            pool.wait_ge(s_route, 1)
            pool.wait_ge(s_zero, 16)
            for j in range(NT):
                for k in range(TOP_K):
                    pool.indirect_dma_start(
                        out=xs_dram, out_offset=bass.IndirectOffsetOnAxis(ap=slot[:, k, j:j + 1], axis=0),
                        in_=xn[:, j, :], in_offset=None).then_inc(s_scat, 16)
            pool.wait_ge(s_os[0], 16 * ((MAX_BLOCKS + 1) // 2) + 16)
            pool.wait_ge(s_os[1], 16 * (MAX_BLOCKS // 2) + 16)
            for j in range(NT):
                if j >= 4:
                    pool.wait_ge(s_fin, j - 3)
                for k in range(TOP_K):
                    pool.indirect_dma_start(
                        out=gath[:, j % 4, k, :], out_offset=None, in_=os_dram,
                        in_offset=bass.IndirectOffsetOnAxis(ap=slot[:, k, j:j + 1], axis=0)).then_inc(s_g[j % 4], 16)

        @block.scalar
        def _(act):
            for s, n in ((s_cT, 2), (s_xT, 2), (s_kf, 2), (s_qf, 2), (s_exp, 2), (s_gT, 2), (s_ge, 1),
                         (s_xbe, 1), (s_h, 2), (s_hT, 1)):
                act.sem_inc(s, n)
            act.wait_ge(s_bq, 16)
            act.activation(bqs_sb[:, :], bq_sb[:, :], ACT.Copy, scale=SCALE).then_inc(s_act, 1)

            def rstd_guess(n):
                act.wait_ge(s_var, n + 1)
                act.activation(lnv[:, :], var[:, :], ACT.Ln).then_inc(s_act, 1)
                act.wait_ge(s_act, n + 2)
                act.activation(y0[:, :], lnv[:, :], ACT.Exp, scale=-0.5).then_inc(s_y0, 1)

            loop(act, 0, B, rstd_guess)

            def evac(b):
                act.wait_ge(s_kp, 2 * b + 2)
                for c in range(KC):
                    act.wait_ge(s_cTp, 2 * b + c + 1)
                    act.activation(cT[:, c, :], ps[:, 2 + c, :], ACT.Copy).then_inc(s_cT, 1)
                act.wait_ge(s_qp, 2 * b + 2)
                for c in range(KC):
                    act.wait_ge(s_xTp, 2 * b + c + 1)
                    act.activation(xT[:, c, :], ps[:, c, :], ACT.Copy).then_inc(s_xT, 1)
                act.wait_ge(s_vp, 2 * b + 2)
                act.wait_ge(s_ks, b + 1)
                for c in range(KC):
                    act.wait_ge(s_kp, 2 * b + c + 3)
                    act.activation(kf[:, c, :], ps[:, 6 + c, :], ACT.Identity, bias=bq_sb[:, c:c + 1]).then_inc(s_kf, 1)
                act.wait_ge(s_qs, b + 1)
                for c in range(KC):
                    act.wait_ge(s_qp, 2 * b + c + 3)
                    act.activation(qf[:, c, :], ps[:, 4 + c, :], ACT.Identity, bias=bqs_sb[:, c:c + 1],
                                   scale=SCALE).then_inc(s_qf, 1)

            act.wait_ge(s_act, 1)
            loop(act, 0, B, evac)

            def exps(i):
                for t in range(TB):
                    act.wait_ge(s_pv, TB * i + t + 1)
                    for q in range(2):
                        act.wait_ge(s_s2, 2 * TB * i + 2 * t + q + 1)
                        r = 4 * (t % 2) + 2 * q
                        act.activation(probs[:, r:r + 2, :], ps[:, BS2 + 2 * q:BS2 + 2 * q + 2, :],
                                       ACT.Exp).then_inc(s_exp, 1)

            act.wait_ge(s_v, 2 + 2 * B)
            loop(act, 0, NG * B, exps)

            loop(act, B, 2 * B, rstd_guess)

            def g_evac(b):
                for c in range(KC):
                    act.wait_ge(s_gTp, 2 * b + c + 1)
                    act.activation(x2T[:, c, bass.ds(S * b, S)], ps[:, c, :], ACT.Copy).then_inc(s_gT, 1)
                act.wait_ge(s_gp, b + 1)
                act.wait_ge(s_glp, b + 1)
                act.activation(lgT[0:E, :], ps[0:E, 2, :], ACT.Copy).then_inc(s_ge, 1)

            loop(act, 0, B, g_evac)
            act.wait_ge(s_lsh, 1)
            act.activation(lex[:, :, :], lsh[:, :, :], ACT.Exp).then_inc(s_lex, 1)

            def shared(b):
                def first(c):
                    n = FC * b + c
                    rows = P if c < FC - 1 else FL
                    act.wait_ge(s_up1, n + 1)
                    act.activation(sh_a[0:rows, c % 2, :], ps[0:rows, 2 * (c % 2), :], ACT.Identity,
                                   bias=sb13_sb[0:rows, c, 0:1]).then_inc(s_a1, 1)

                def silu(c):
                    n = FC * b + c
                    rows = P if c < FC - 1 else FL
                    act.wait_ge(s_z1, n + 1)
                    if c == 0:
                        act.wait_ge(s_dn1, 4 * b + 4)
                    act.activation(sh_hT[0:rows, c, :], sh_z[0:rows, c % 2, :], ACT.Silu).then_inc(s_h1, 1)

                first(0)
                first(1)
                silu(0)
                first(2)
                silu(1)
                silu(2)

            loop(act, 0, B, shared)

            def x_evac(n, par):
                act.wait_ge(s_xbp, n + 3)
                act.wait_ge(s_up, n + 1)
                act.activation(xbT[:, par, :, :], ps[:, 0, 0:D].rearrange("p (k s) -> p k s", k=KC),
                               ACT.Copy).then_inc(s_xbe, 1)

            def h_make(n, par):
                act.wait_ge(s_z, n + 1)
                act.wait_ge(s_hp, n + 1)
                act.activation(e_h[:, par, :], e_z[:, par, :], ACT.Silu).then_inc(s_h, 1)

            def h_evac(n, par):
                act.wait_ge(s_hp, n + 3)
                act.wait_ge(s_o, n + 1)
                act.activation(e_hT[:, par, 0:FC - 1, :],
                               ps[:, 5, 0:(FC - 1) * P].rearrange("p (c s) -> p c s", c=FC - 1), ACT.Copy)
                act.activation(e_hT[0:FL, par, FC - 1, :], ps[0:FL, 5, (FC - 1) * P:FC * P], ACT.Copy).then_inc(s_hT, 1)

            x_evac(0, 0)

            def blocks(n, par, r):
                h_make(n, par)
                x_evac(n + 1, 1 - par)
                h_evac(n, par)

            NP = (MAX_BLOCKS - 1) // 2 * 2
            pairs(act, NP, blocks)
            for n in range(NP, MAX_BLOCKS):
                h_make(n, n % 2)
                if n + 1 < MAX_BLOCKS:
                    x_evac(n + 1, 1 - n % 2)
                h_evac(n, n % 2)

        @block.vector
        def _(dve):
            for s, n in ((s_v, 2), (s_qs, 1), (s_rc, 3), (s_pvc, 1), (s_gl, 1), (s_y1, 1), (s_upc, 2), (s_oe, 2)):
                dve.sem_inc(s, n)
            dve.memset(k_st[96:98, :, :, :], 1.0).then_inc(s_ones, 1)
            for r in range(2):
                dve.memset(v_grp[:, r, :, :, DK:32], 1.0).then_inc(s_ones, 1)
            N_LN = 2 * TB + 4

            def layer_norm(n, b, base, arrived):
                c0 = base + N_LN * b
                k = [0]

                def link(ins):
                    k[0] += 1
                    ins.then_inc(s_dve, 1)

                def await_chain():
                    dve.wait_ge(s_dve, c0 + k[0])

                arrived()
                for j in range(TB):
                    link(dve.bn_stats(stats[:, j, :], xres[:, TB * b + j, :]))
                await_chain()
                for j in range(TB):
                    ins = dve.bn_aggr(mv[:, j, :], stats[:, j, :])
                    link(ins)
                await_chain()
                dve.tensor_scalar_add(var[:, :], mv[:, :, 1], EPS).then_inc(s_var, 1)
                dve.wait_ge(s_y0, n + 1)
                dve.wait_ge(s_var, n + 1)
                link(dve.tensor_tensor(newt[:, :], y0[:, :], y0[:, :], ALU.mult))
                await_chain()
                link(dve.tensor_tensor(newt[:, :], newt[:, :], var[:, :], ALU.mult))
                await_chain()
                link(dve.tensor_scalar(newt[:, :], newt[:, :], -0.5, 1.5, ALU.mult, ALU.add))
                await_chain()
                link(dve.tensor_tensor(rstd[:, :], newt[:, :], y0[:, :], ALU.mult))
                await_chain()
                for j in range(TB):
                    ins = dve.tensor_scalar(xn[:, TB * b + j, :], xres[:, TB * b + j, :], mv[:, j, 0:1],
                                            rstd[:, j:j + 1], ALU.subtract, ALU.mult)
                ins.then_inc(s_xn, 1)

            for b in range(B):
                layer_norm(b, b, 0, lambda: dve.wait_ge(s_x[b], 16))
            at = [N_LN * B]

            def project(b):
                for half in range(2):
                    dve.wait_ge(s_vp, 2 * b + half + 3)
                    dve.tensor_copy(v_all[:, bass.ds(TB * b + 2 * half, 2), :, :].rearrange("p j h d -> p (j h d)"),
                                    ps[:, 2 + half, :]).then_inc(s_v, 1)
                c0 = N_LN * B + 3 * b
                dve.wait_ge(s_qf, 2 * b + 4)
                dve.wait_ge(s_qd, 16 * 12 * (b + 1))
                dve.tensor_copy(qparts[:, 0, :, :], qf[:, :, :]).then_inc(s_dve, 1)
                dve.wait_ge(s_dve, c0 + 1)
                dve.tensor_tensor(qf[:, :, :], qf[:, :, :], qparts[:, 0, :, :], ALU.subtract).then_inc(s_dve, 1)
                dve.wait_ge(s_dve, c0 + 2)
                dve.tensor_copy(qparts[:, 1, :, :], qf[:, :, :]).then_inc(s_dve, 1)
                dve.wait_ge(s_dve, c0 + 3)
                dve.tensor_tensor(qparts[:, 2, :, :], qf[:, :, :], qparts[:, 1, :, :], ALU.subtract).then_inc(s_qs, 1)

            loop(dve, 0, B, project)
            at[0] += 3 * B

            STEP = GH * TB + 1 + 3
            A0 = at[0]

            def scores_tile(n, bank, u, par):
                dve.wait_ge(s_rp, n + 1)
                dve.tensor_reduce(nmax[:, par, u:u + 1], ps[:, BR + bank, :], AX_X, ALU.max, negate=True).then_inc(s_rc, 1)

            def max_parts(n, par, last_unit, c0):
                dve.wait_ge(s_rc, 3 + last_unit + 1)
                dve.wait_ge(s_rp, last_unit + 1)
                dve.tensor_copy(mparts[:, 0, :], nmax[:, par, :]).then_inc(s_dve, 1)
                dve.wait_ge(s_dve, c0 + 1)
                dve.tensor_tensor(mparts[:, 1, :], nmax[:, par, :], mparts[:, 0, :], ALU.subtract).then_inc(s_mp, 1)

            def max_rows(n, bank, after):
                dve.wait_ge(s_rp, n + 1)
                after()
                dve.tensor_copy(mT[:, :], ps[0:2 * GH * TB, BR + bank, 0:P // 2].bitcast(BF16)).then_inc(s_mT, 1)
                dve.wait_ge(s_mT, 1)

            def normalise(i, g, c0):
                dve.wait_ge(s_pv, 2 + TB * i + TB)
                dve.transpose(tA[:, :, :].rearrange("p a b -> p (a b)"), ps[:, BPV, :]).then_inc(s_pvc, 1)
                dve.wait_ge(s_pvc, i + 2)
                dve.reciprocal(rsum[:, :], tA[:, :, DK]).then_inc(s_dve, 1)
                dve.wait_ge(s_dve, c0 + 1)
                dve.tensor_tensor(tB[:, :, 0:DK], tA[:, :, 0:DK],
                                  rsum[:, :].rearrange("p (a b) -> p a b", b=1).to_broadcast([P, S // 32, DK]),
                                  ALU.mult).then_inc(s_dve, 1)
                dve.wait_ge(s_dve, c0 + 2)
                dve.transpose(aT[:, g, :], tB[:, :, :].rearrange("p a b -> p (a b)")).then_inc(s_norm, 1)

            def x_one(n, bank, tile, k):
                dve.wait_ge(s_rp, n + 1)
                dve.tensor_tensor(xres[:, tile, :], ps[:, BR + bank, 0:D], xres[:, tile, :], ALU.add).then_inc(s_rc, 1)

            dve.wait_ge(s_const, 11)
            for n in range(2):
                for u in range(GH * TB):
                    k = n * (GH * TB + 1) + u
                    scores_tile(k, k % 3, u, n)
                if n == 0:
                    max_parts(0, 0, GH * TB - 1, A0)
                    m_unit = GH * TB
                    max_rows(m_unit, m_unit % 3, lambda: None)
                    dve.wait_ge(s_mT, 1)
                    dve.sem_inc(s_rc, 1)
            max_parts(1, 1, PRE - 1, A0 + 1)
            A1 = A0 + 2

            def steps(b):
                offs, total = batch_units(b)
                rb = ring_base(b)
                for g in range(NG):
                    i = NG * b + g
                    with_wo, with_s1, with_m = kinds(b, g)
                    units = step_units(g, with_wo, with_s1, with_m)
                    c0 = A1 + 3 * i - 2 if with_m else A1 + 3 * i - 3
                    first_step = isinstance(i, int) and i == 0
                    normed = False
                    for k, (kind, u) in enumerate(units):
                        n = rb + offs[g] + k
                        bank = bank_of(b, offs[g] + k)
                        if not first_step and not normed and (k == TB or not with_s1):
                            normalise(i - 1, (g - 1) % NG, c0)
                            normed = True
                        if kind == "s1":
                            if u == 0:
                                dve.wait_ge(s_mp, i + 1)
                            scores_tile(n, bank, u, g % 2)
                        elif kind == "m":
                            max_rows(n, bank, lambda: dve.wait_ge(s_mrow[g], 32 * (b + 1)))
                            dve.wait_ge(s_mT, i + 2)
                            dve.sem_inc(s_rc, 1)
                        else:
                            x_one(n, bank, TB * (b - 1) + u, k)
                    if not first_step and not normed:
                        normalise(i - 1, (g - 1) % NG, c0)
                    if with_s1:
                        s1_last = max(k for k, (kind, u) in enumerate(units) if kind == "s1")
                        max_parts(i + 2, g % 2, rb + offs[g] + s1_last, c0 + 2)

            steps(0)
            loop(dve, 1, B - 1, steps)
            steps(B - 1)
            normalise(NG * B - 1, NG - 1, A1 + 3 * (NG * B) - 4)
            for j in range(TB):
                x_one(RING_END + j, (bank_of(1, 0) + (RING_END - ring_base(1)) + j) % 3, TB * (B - 1) + j, j)
            A2 = A1 + 3 * NG * B - 4 + 2

            dve.wait_ge(s_rc, 3 + RING_END + TB)
            dve.wait_ge(s_xTp, 2 * B)
            for b in range(B):
                layer_norm(B + b, b, A2, lambda: None)
            c = [A2 + N_LN * B]

            def logits(b):
                dve.wait_ge(s_glp, b + 2)
                dve.tensor_copy(lg[:, bass.ds(TB * b, TB), :],
                                ps[:, 3, 0:TB * E].rearrange("p (j e) -> p j e", j=TB)).then_inc(s_gl, 1)

            loop(dve, 0, B, logits)
            dve.wait_ge(s_gl, 1 + B)
            dve.wait_ge(s_sw, 16 * 11)

            def link(ins):
                c[0] += 1
                ins.then_inc(s_dve, 1)
                dve.wait_ge(s_dve, c[0])

            def over_e(v):
                return v.rearrange("p (j a) -> p j a", a=1).to_broadcast([P, NT, E])

            def over_j(v):
                return v.rearrange("p (a e) -> p a e", a=1).to_broadcast([P, NT, E])

            link(dve.reduce_max(rt1[:, :], lg[:, :, :], axis=AX_X))
            dve.tensor_tensor(lsh[:, :, :], lg[:, :, :], over_e(rt1[:, :]), ALU.subtract).then_inc(s_lsh, 1)
            dve.wait_ge(s_lex, 1)
            link(dve.reduce_sum(rt1[:, :], lex[:, :, :], axis=AX_X))
            link(dve.reciprocal(rt2[:, :], rt1[:, :]))
            link(dve.tensor_tensor(sco[:, :, :], lex[:, :, :], over_e(rt2[:, :]), ALU.mult))
            link(dve.tensor_tensor(bia[:, :, :], sco[:, :, :], over_j(gb_sb[:, :]), ALU.add))
            for k in range(TOP_K):
                link(dve.reduce_max(rt1[:, :], bia[:, :, :], axis=AX_X))
                link(dve.tensor_tensor(cand[:, :, :], bia[:, :, :], over_e(rt1[:, :]), ALU.is_equal))
                link(dve.tensor_tensor(cand[:, :, :], cand[:, :, :], over_j(iota_e[:, :]), ALU.mult))
                link(dve.tensor_reduce(rt2[:, :], cand[:, :, :], AX_X, ALU.min))
                link(dve.tensor_tensor(oneh[:, k, :, :], over_j(iota_e[:, :]), over_e(rt2[:, :]), ALU.is_equal))
                link(dve.tensor_tensor(cand[:, :, :], sco[:, :, :], oneh[:, k, :, :], ALU.mult))
                link(dve.reduce_sum(rw[:, k, :], cand[:, :, :], axis=AX_X))
                if k + 1 < TOP_K:
                    link(dve.scalar_tensor_tensor(bia[:, :, :], oneh[:, k, :, :], -3.0e38, bia[:, :, :],
                                                  ALU.mult, ALU.add))
            dve.tensor_tensor(selb[:, :, :], oneh[:, 0, :, :], oneh[:, 1, :, :], ALU.add).then_inc(s_sel, 1)
            dve.wait_ge(s_cnt, 1)
            before = ps[:, 4, 0:NT * E].rearrange("p (j e) -> p j e", j=NT)
            whole = ps[:, 4, NT * E:2 * NT * E].rearrange("p (j e) -> p j e", j=NT)
            link(dve.memset(cum[:, 0, :], 0.0))
            for j in range(NT):
                link(dve.tensor_tensor(cum[:, j + 1, :], whole[:, j, :], cum[:, j, :], ALU.add))
            link(dve.tensor_tensor(cmpc[:, :, :],
                                   cum[:, NT, :].rearrange("p (e a) -> p e a", a=1).to_broadcast([P, E, NT]),
                                   iota_c[:, :].rearrange("p (a n) -> p a n", a=1).to_broadcast([P, E, NT]), ALU.is_gt))
            link(dve.reduce_sum(nblk[:, :], cmpc[:, :, :], axis=AX_X))
            link(dve.memset(bend[:, 0:1], 0.0))
            for e in range(E):
                link(dve.tensor_tensor(bend[:, e + 1:e + 2], bend[:, e:e + 1], nblk[:, e:e + 1], ALU.add))
            link(dve.tensor_tensor(cmpn[:, :, :],
                                   iota_n[:, :].rearrange("p (n a) -> p n a", a=1).to_broadcast([P, MAX_BLOCKS, E]),
                                   bend[:, 1:E + 1].rearrange("p (a e) -> p a e", a=1).to_broadcast([P, MAX_BLOCKS, E]),
                                   ALU.is_ge))
            link(dve.reduce_sum(blkf[:, :], cmpn[:, :, :], axis=AX_X))
            link(dve.tensor_scalar_min(blkf[:, :], blkf[:, :], float(E - 1)))
            link(dve.tensor_copy(blk[:, :], blkf[:, :]))
            link(dve.tensor_scalar_mul(off[:, :], bend[:, 0:E], float(P)))
            link(dve.tensor_tensor(cand[:, :, :], before, cum[:, 0:NT, :], ALU.add))
            link(dve.tensor_tensor(cand[:, :, :], cand[:, :, :], over_j(off[:, :]), ALU.add))
            for k in range(TOP_K):
                link(dve.tensor_tensor(lsh[:, :, :], cand[:, :, :], oneh[:, k, :, :], ALU.mult))
                link(dve.reduce_sum(slotf[:, k, :], lsh[:, :, :], axis=AX_X))
            dve.tensor_copy(slot[:, :, :], slotf[:, :, :]).then_inc(s_route, 1)
            link(dve.memset(sh_hT[96:128, FC - 1, :], 1.0))

            def shared(b):
                for c in range(FC):
                    n = FC * b + c
                    rows = P if c < FC - 1 else FL
                    dve.wait_ge(s_a1, n + 1)
                    if not isinstance(n, int):
                        dve.wait_ge(s_h1, n - 1) if c >= 2 else None
                    dve.scalar_tensor_tensor(sh_z[0:rows, c % 2, :], ps[0:rows, 2 * (c % 2) + 1, :],
                                             sb13_sb[0:rows, c, 1:2], sh_a[0:rows, c % 2, :],
                                             ALU.add, ALU.mult).then_inc(s_z1, 1)
                for j in range(TB):
                    dve.wait_ge(s_dn1, 4 * b + j + 5)
                    if j % 2 == 1:
                        tile = TB * b + j - 1
                        dve.tensor_tensor(xres[:, bass.ds(tile, 2), :],
                                          ps[:, 6 + j // 2, :].rearrange("p (j d) -> p j d", j=2),
                                          xres[:, bass.ds(tile, 2), :], ALU.add).then_inc(s_y1, 1)

            loop(dve, 0, B, shared)
            dve.wait_ge(s_up1, FC * B)
            link(dve.memset(e_hT[96:128, :, FC - 1, :], 1.0))
            A3 = c[0]

            dve.wait_ge(s_ew, 16 * (3 * E + 4))

            def blocks(n, par):
                ex = dve.value_load(blk[0:1, bass.ds(n, 1)], min_val=0, max_val=E - 1)
                dve.wait_ge(s_up, n + 3)
                dve.tensor_tensor(e_a[:, :], ps[:, 1 + 2 * par, 0:F], b13_sb[:, ex, 0:F], ALU.add).then_inc(s_dve, 1)
                dve.tensor_tensor(e_c[:, :], ps[:, 2 + 2 * par, 0:F], b13_sb[:, ex, F:2 * F], ALU.add).then_inc(s_upc, 1)
                dve.wait_ge(s_dve, A3 + 1 + n)
                dve.wait_ge(s_upc, n + 3)
                dve.wait_ge(s_h, n + 1)
                dve.tensor_tensor(e_z[:, par, :], e_a[:, :], e_c[:, :], ALU.mult).then_inc(s_z, 1)

            def results(n, par, r):
                dve.wait_ge(s_o, n + 3)
                dve.wait_ge(s_os[par], 16 * r + 16)
                dve.tensor_copy(e_o[:, par, :], ps[:, 6 + par, 0:D]).then_inc(s_oe, 1)

            blocks(0, 0)

            def pair(n, par, r):
                blocks(n + 1, 1 - par)
                results(n, par, r)

            NP = (MAX_BLOCKS - 1) // 2 * 2
            pairs(dve, NP, pair)
            for n in range(NP, MAX_BLOCKS):
                if n + 1 < MAX_BLOCKS:
                    blocks(n + 1, 1 - n % 2)
                results(n, n % 2, n // 2)

            A4 = A3 + MAX_BLOCKS
            for j in range(NT):
                dve.wait_ge(s_g[j % 4], 32 * (j // 4) + 32)
                dve.scalar_tensor_tensor(xres[:, j, :], gath[:, j % 4, 0, :], rw[:, 0, j:j + 1], xres[:, j, :],
                                         ALU.mult, ALU.add).then_inc(s_dve, 1)
                dve.wait_ge(s_dve, A4 + j + 1)
                dve.scalar_tensor_tensor(xres[:, j, :], gath[:, j % 4, 1, :], rw[:, 1, j:j + 1], xres[:, j, :],
                                         ALU.mult, ALU.add).then_inc(s_fin, 1)

        @block.tensor
        def _(pe):
            for s, n in ((s_kp, 2), (s_qp, 2), (s_vp, 2), (s_pv, 2), (s_glp, 1), (s_dn1, 4), (s_xbp, 2),
                         (s_up, 2), (s_hp, 2), (s_o, 2)):
                pe.sem_inc(s, n)
            pe.wait_ge(s_const, 11)
            pe.wait_ge(s_wq, 16)

            def project(b, par, r):
                pe.wait_ge(s_c[par], 16 * r + 16)
                pe.wait_ge(s_v, 2 * b + 2)
                for c in range(KC):
                    for j in range(TB):
                        ins = pe.transpose(ps[:, 2 + c, P * j:P * j + P], cst[:, par, j, P * c:P * c + P], ident[:, :])
                    ins.then_inc(s_cTp, 1)
                pe.wait_ge(s_xn, b + 1)
                pe.wait_ge(s_xT, 2 * b + 2)
                for c in range(KC):
                    for j in range(TB):
                        ins = pe.transpose(ps[:, c, P * j:P * j + P], xn_tile(b, j, c), ident[:, :])
                    ins.then_inc(s_xTp, 1)
                pe.wait_ge(s_cT, 2 * b + 4)
                pe.wait_ge(s_kf, 2 * b + 2)
                for c in range(KC):
                    for k in range(KC):
                        ins = pe.matmul(ps[:, 6 + c, :], wq_sb[:, k, P * c:P * c + P], cT[:, k, :],
                                        start=(k == 0), stop=(k == KC - 1))
                    ins.then_inc(s_kp, 1)
                pe.wait_ge(s_xT, 2 * b + 4)
                pe.wait_ge(s_qf, 2 * b + 2)
                for c in range(KC):
                    for k in range(KC):
                        ins = pe.matmul(ps[:, 4 + c, :], wq_sb[:, k, P * c:P * c + P], xT[:, k, :],
                                        start=(k == 0), stop=(k == KC - 1))
                    ins.then_inc(s_qp, 1)
                pe.wait_ge(s_kf, 2 * b + 4)
                for j in range(TB):
                    for c in range(KC):
                        ins = pe.transpose(ps[:, 2 + j // 2, D * (j % 2) + P * c:D * (j % 2) + P * c + P],
                                           kf[:, c, P * j:P * j + P], ident[:, :])
                    if j % 2:
                        ins.then_inc(s_vp, 1)

            def xn_tile(b, j, c):
                return xn[:, TB * b + j, P * c:P * c + P]

            for b in range(B):
                project(b, b % 2, b // 2)

            pe.wait_ge(s_v, 2 + 2 * B)
            pe.wait_ge(s_qf, 2 + 2 * B)
            pe.wait_ge(s_ones, 3)

            def scores_for_max(n, bank, slot_, u):
                j, c = u // TB, u % TB
                pe.wait_ge(s_rc, n + 1)
                pe.matmul(ps[:, BR + bank, :], q_st[0:96, slot_, j, P * c:P * c + P], k_st[0:96, slot_, j, :],
                          start=True, stop=True).then_inc(s_rp, 1)

            def maxima(n, bank, i):
                pe.wait_ge(s_rc, n + 1)
                pe.wait_ge(s_mp, i + 1)
                pe.transpose(ps[0:2 * GH * TB, BR + bank, 0:P // 2].bitcast(BF16),
                             mparts[:, :, :].rearrange("p a b -> p (a b)"), ident_b[:, :]).then_inc(s_rp, 1)

            def out_projection(n, bank, j):
                pe.wait_ge(s_rc, n + 1)
                for g in range(NG):
                    ins = pe.matmul(ps[:, BR + bank, 0:D], aT[:, g, P * j:P * j + P], wo_sb[:, g, :],
                                    start=(g == 0), stop=(g == NG - 1))
                ins.then_inc(s_rp, 1)

            def weighted_sum(i, g, t):
                pe.wait_ge(s_exp, 2 + 2 * TB * i + 2 * t + 2)
                if t == 0:
                    pe.wait_ge(s_pvc, i + 1)
                    pe.wait_ge(s_vg, i + 1)
                for j in range(GH):
                    ins = pe.matmul(ps[32 * j:32 * j + 32, BPV, :], v_grp[:, g % 2, t, j, :],
                                    probs[:, 4 * (t % 2) + j, :], start=(t == 0), stop=(t == TB - 1))
                ins.then_inc(s_pv, 1)

            for n in range(2):
                pe.wait_ge(s_st[n], 16 * 12)
                for u in range(GH * TB):
                    k = n * (GH * TB + 1) + u
                    scores_for_max(k, k % 3, n, u)
                if n == 0:
                    maxima(GH * TB, (GH * TB) % 3, 0)

            def steps(b):
                offs, total = batch_units(b)
                rb = ring_base(b)
                for g in range(NG):
                    i = NG * b + g
                    with_wo, with_s1, with_m = kinds(b, g)
                    k = offs[g]
                    pe.wait_ge(s_mrow[g], 32 * (b + 1))
                    if with_s1:
                        b2_ = b if g + 2 < NG else b + 1
                        pe.wait_ge(s_st[(g + 2) % NG], 16 * 12 * (b2_ + 1))
                    for t in range(TB):
                        for q in range(2):
                            pe.wait_ge(s_exp, 2 * TB * i + 2 * t + q + 1)
                            for j in (2 * q, 2 * q + 1):
                                ins = pe.matmul(ps[:, BS2 + j, :], k_st[0:98, g, j, P * t:P * t + P],
                                                q_st[0:98, g, j, :], start=True, stop=True)
                            ins.then_inc(s_s2, 1)
                        if t == 1 and with_m:
                            maxima(rb + k, bank_of(b, k), i + 1)
                            k += 1
                        if with_s1:
                            for c in range(TB):
                                scores_for_max(rb + k, bank_of(b, k), (g + 2) % NG, t * TB + c)
                                k += 1
                        if t > 0:
                            weighted_sum(i, g, t - 1)
                        elif not (isinstance(i, int) and i == 0):
                            weighted_sum(i - 1, (g - 1) % NG, TB - 1)
                    if g == 0 and with_wo:
                        pe.wait_ge(s_norm, NG * b)
                        for j in range(TB):
                            out_projection(rb + k, bank_of(b, k), j)
                            k += 1

            pe.wait_ge(s_wo, 16 * (H + 1))
            steps(0)
            loop(pe, 1, B - 1, steps)
            steps(B - 1)
            weighted_sum(NG * B - 1, NG - 1, TB - 1)
            pe.wait_ge(s_norm, NG * B)
            for j in range(TB):
                out_projection(RING_END + j, (bank_of(1, 0) + (RING_END - ring_base(1)) + j) % 3, j)

            pe.wait_ge(s_rc, 3 + RING_END + TB)
            pe.wait_ge(s_sw, 16 * 11)

            def router(b):
                pe.wait_ge(s_xn, B + b + 1)
                pe.wait_ge(s_gT, 2 * b + 2)
                for c in range(KC):
                    for j in range(TB):
                        ins = pe.transpose(ps[:, c, P * j:P * j + P], xn_tile(b, j, c), ident[:, :])
                    ins.then_inc(s_gTp, 1)
                pe.wait_ge(s_gT, 2 * b + 4)
                pe.wait_ge(s_ge, b + 1)
                for k in range(KC):
                    ins = pe.matmul(ps[0:E, 2, :], gw_sb[:, k, :], x2T[:, k, S * b:S * b + S],
                                    start=(k == 0), stop=(k == KC - 1))
                ins.then_inc(s_gp, 1)
                pe.wait_ge(s_ge, b + 2)
                pe.wait_ge(s_gl, b + 1)
                for j in range(TB):
                    ins = pe.transpose(ps[:, 3, E * j:E * j + E], lgT[0:E, P * j:P * j + P], ident[0:E, 0:E])
                ins.then_inc(s_glp, 1)

            for b in range(B):
                router(b)

            def counts():
                pe.wait_ge(s_sel, 1)
                sel = selb[:, :, :].rearrange("p j e -> p (j e)")
                pe.matmul(ps[:, 4, 0:NT * E], tri[:, :], sel, start=True, stop=True)
                pe.matmul(ps[:, 4, NT * E:2 * NT * E], ones_b[:, :], sel, start=True, stop=True).then_inc(s_cnt, 1)

            def shared(b):
                def up(c):
                    n = FC * b + c
                    rows = P if c < FC - 1 else FL
                    if not (isinstance(b, int) and b == 0 and c < 2):
                        pe.wait_ge(s_z1, n - 1)
                    for half in range(2):
                        for k in range(KC):
                            ins = pe.matmul(ps[0:rows, 2 * (c % 2) + half, :],
                                            sw13_sb[:, k, F * half + P * c:F * half + P * c + rows],
                                            x2T[:, k, S * b:S * b + S], start=(k == 0), stop=(k == KC - 1))
                    ins.then_inc(s_up1, 1)

                for c in range(FC):
                    up(c)
                pe.wait_ge(s_h1, FC * b + FC)
                pe.wait_ge(s_y1, 2 * b + 1)
                for j in range(TB):
                    for c in range(FC):
                        rows = P if c < FC - 1 else FL + 1
                        ins = pe.matmul(ps[:, 6 + j // 2, D * (j % 2):D * (j % 2) + D], sh_hT[0:rows, c, P * j:P * j + P],
                                        sw2_sb[0:rows, c, :], start=(c == 0), stop=(c == FC - 1))
                    ins.then_inc(s_dn1, 1)

            counts()
            for b in range(B):
                shared(b)

            pe.wait_ge(s_ew, 16 * (3 * E + 4))
            pe.wait_ge(s_y1, 1 + 2 * B)

            def up(n, par, r):
                ex = pe.value_load(blk[0:1, bass.ds(n, 1)], min_val=0, max_val=E - 1)
                pe.wait_ge(s_xb[par], 16 * r + 16)
                pe.wait_ge(s_xbe, n + 1)
                for k in range(KC):
                    ins = pe.transpose(ps[:, 0, P * k:P * k + P], xb[:, par, P * k:P * k + P], ident[:, :])
                ins.then_inc(s_xbp, 1)
                pe.wait_ge(s_xbe, n + 2)
                pe.wait_ge(s_upc, n + 1)
                for half in range(2):
                    for k in range(KC):
                        ins = pe.matmul(ps[:, 1 + 2 * par + half, 0:F], xbT[:, par, k, :],
                                        w13_sb[:, ex, k, F * half:F * half + F], start=(k == 0), stop=(k == KC - 1))
                ins.then_inc(s_up, 1)

            def down(n, par):
                ex = pe.value_load(blk[0:1, bass.ds(n, 1)], min_val=0, max_val=E - 1)
                pe.wait_ge(s_h, n + 3)
                pe.wait_ge(s_hT, n + 1)
                for c in range(FC):
                    rows = P if c < FC - 1 else FL
                    ins = pe.transpose(ps[0:rows, 5, P * c:P * c + P], e_h[:, par, P * c:P * c + rows], ident[:, :])
                ins.then_inc(s_hp, 1)
                pe.wait_ge(s_hT, n + 2)
                pe.wait_ge(s_oe, n + 1)
                for c in range(FC):
                    rows = P if c < FC - 1 else FL + 1
                    ins = pe.matmul(ps[:, 6 + par, 0:D], e_hT[0:rows, par, c, :], w2_sb[0:rows, ex, c, :],
                                    start=(c == 0), stop=(c == FC - 1))
                ins.then_inc(s_o, 1)

            up(0, 0, 0)

            def pair(n, par, r):
                up(n + 1, 1 - par, r if par == 0 else r + 1)
                down(n, par)

            NP = (MAX_BLOCKS - 1) // 2 * 2
            pairs(pe, NP, pair)
            for n in range(NP, MAX_BLOCKS):
                if n + 1 < MAX_BLOCKS:
                    up(n + 1, 1 - n % 2, (n + 1) // 2)
                down(n, n % 2)


_NAMES = ["x", "ctx_1024", "L0_xattn_Wq", "L0_xattn_bq", "L0_xattn_Wo", "L0_xattn_bo", "L0_ffn_gate_w",
          "L0_ffn_gate_b", "L0_ffn_w1", "L0_ffn_b1", "L0_ffn_w3", "L0_ffn_b3", "L0_ffn_w2", "L0_ffn_b2",
          "L0_ffn_sw1", "L0_ffn_sb1", "L0_ffn_sw3", "L0_ffn_sb3", "L0_ffn_sw2", "L0_ffn_sb2"]


def kernel(**inputs):
    import numpy as _np
    import concourse.bacc as _bacc
    from concourse import mybir as _mybir
    from concourse.bass_utils import run_bass_kernel_spmd as _run

    nc = _bacc.Bacc("TRN2", target_bir_lowering=False, num_devices=1)
    arrays, args = {}, []
    for name in _NAMES:
        a = _np.asarray(inputs[name])
        if name == "L0_ffn_gate_w":
            a = a.T
        a = _np.ascontiguousarray(a)
        arrays[f"in_{name}"] = a
        args.append(nc.dram_tensor(f"in_{name}", a.shape, _mybir.dt.from_np(a.dtype), kind="ExternalInput").ap())
    shape = inputs["x"].shape
    out = nc.dram_tensor("out_x", shape, _mybir.dt.float32, kind="ExternalOutput").ap()
    xattn_moe_kernel(nc, *args, out)
    r = _run(nc, [arrays], core_ids=[0])
    return r.results[0]["out_x"]
```

```python
from contextlib import ExitStack

import concourse.bass as bass
from concourse import mybir

ALU = mybir.AluOpType
ACT = mybir.ActivationFunctionType
AX_X = mybir.AxisListType.X
F32 = mybir.dt.float32
BF16 = mybir.dt.bfloat16
I32 = mybir.dt.int32

P = 128
EPS = 1e-5
TOP_K = 2


def xattn_moe_kernel(nc, x, ctx_in, wq, bq, wo, bo, gate_wt, gate_b, w1, b1, w3, b3, w2, b2,
                     sw1, sb1, sw3, sb3, sw2, sb2, out):
    B, S, D = x.shape
    T = B * S
    NT = T // P
    TB = S // P
    DK = 16
    H = D // DK
    GH = 4
    NG = H // GH
    KC = D // P
    E, _, F = w1.shape
    FC = -(-F // P)
    FL = F - (FC - 1) * P
    MAX_BLOCKS = (T * TOP_K + E * (P - 1)) // P
    assert S == 512 and D == 256 and H == 16 and FL % 32 == 0 and FL < P
    SCALE = float(DK) ** -0.5

    x_v = x.rearrange("b (j p) d -> b p j d", p=P)
    ctx_v = ctx_in.rearrange("b (j p) d -> b p j d", p=P)
    out_v = out.rearrange("b (j p) d -> (b j) p d", p=P)

    q_dram = nc.dram_tensor("q_parts", (B, 3 * NG, DK, GH * S), BF16).ap()
    k_dram = nc.dram_tensor("k_parts", (B, 3 * NG, DK, GH * S), BF16).ap()
    xs_dram = nc.dram_tensor("slot_rows", (MAX_BLOCKS * P, D), F32).ap()
    os_dram = nc.dram_tensor("slot_results", (MAX_BLOCKS * P, D), F32).ap()

    with ExitStack() as stack:
        def sb(name, shape, dt=F32):
            return stack.enter_context(nc.sbuf_tensor(name, shape, dt))

        def sem(name):
            return stack.enter_context(nc.semaphore(name))

        xres = sb("xres", [P, NT, D])
        xn = sb("xn", [P, NT, D])
        wq_sb = sb("wq_sb", [P, KC, D])
        bq_sb = sb("bq_sb", [P, KC])
        bqs_sb = sb("bqs_sb", [P, KC])
        wo_sb = sb("wo_sb", [P, NG, D])
        ident = sb("ident", [P, P])
        ident_b = sb("ident_b", [P, P], BF16)
        stats = sb("stats", [P, TB, 6])
        mv = sb("mv", [P, TB, 2])
        var = sb("var", [P, TB])
        lnv = sb("lnv", [P, TB])
        y0 = sb("y0", [P, TB])
        newt = sb("newt", [P, TB])
        rstd = sb("rstd", [P, TB])
        aT = sb("aT", [P, NG, S])
        tA = sb("tA", [P, S // 32, 32])
        tB = sb("tB", [P, S // 32, 32])
        rsum = sb("rsum", [P, S // 32])
        nmax = sb("nmax", [P, 2, GH * TB])
        mparts = sb("mparts", [P, 2, GH * TB], BF16)
        mT = sb("mT", [2 * GH * TB, P], BF16)
        sw13_sb = sb("sw13_sb", [P, KC, 2 * F])
        sw2_sb = sb("sw2_sb", [P, FC, D])
        sb13_sb = sb("sb13_sb", [P, FC, 2])
        gw_sb = sb("gw_sb", [P, KC, E])
        gb_sb = sb("gb_sb", [P, E])

        W13_N, W2_N, B13_N = E * KC * 2 * F, E * FC * D, E * 2 * F
        QK_N, V_N, PR_N, VG_N = NG * GH * S // 2, NT * D, 8 * S, 2 * TB * GH * 32
        arena = sb("arena", [P, max(W13_N + W2_N + B13_N, 2 * QK_N + V_N + PR_N + VG_N)])
        q_st = arena[:, 0:QK_N].bitcast(BF16).rearrange("p (g h s) -> p g h s", g=NG, h=GH)
        k_st = arena[:, QK_N:2 * QK_N].bitcast(BF16).rearrange("p (g h s) -> p g h s", g=NG, h=GH)
        o = 2 * QK_N
        v_all = arena[:, o:o + V_N].rearrange("p (j g d h) -> p j g d h", j=NT, g=NG, h=GH)
        o += V_N
        probs = arena[:, o:o + PR_N].rearrange("p (r s) -> p r s", r=8)
        o += PR_N
        v_grp = arena[:, o:o + VG_N].rearrange("p (r j h d) -> p r j h d", r=2, j=TB, h=GH)
        w13_sb = arena[:, 0:W13_N].rearrange("p (e k f) -> p e k f", e=E, k=KC)
        w2_sb = arena[:, W13_N:W13_N + W2_N].rearrange("p (e c d) -> p e c d", e=E, c=FC)
        b13_sb = arena[:, W13_N + W2_N:W13_N + W2_N + B13_N].rearrange("p (e f) -> p e f", e=E)

        PB = [("cst", 2 * TB * D), ("xT", KC * S), ("cT", KC * S), ("kf", KC * S), ("qf", KC * S),
              ("qparts", 3 * KC * S // 2), ("kparts", 3 * KC * S // 2)]
        FB = [("x2T", KC * T), ("lgT", S), ("sa", 2 * S), ("sz", 2 * S), ("shT", FC * S)]
        EB = [("xb", 2 * D), ("xbT", 2 * D), ("ez", 2 * F), ("eh", 2 * F),
              ("ehT", 2 * FC * P), ("eo", 2 * D)]
        assert sum(n for _, n in EB) <= KC * T
        work = sb("work", [P, max(sum(n for _, n in PB), sum(n for _, n in FB))])

        def carve(parts):
            at, got = 0, {}
            for name, n in parts:
                got[name] = work[:, at:at + n]
                at += n
            return got

        pb, fb, eb = carve(PB), carve(FB), carve(EB)
        cst = pb["cst"].rearrange("p (r j d) -> p r j d", r=2, j=TB)
        xT = pb["xT"].rearrange("p (k s) -> p k s", k=KC)
        cT = pb["cT"].rearrange("p (k s) -> p k s", k=KC)
        kf = pb["kf"].rearrange("p (k s) -> p k s", k=KC)
        qf = pb["qf"].rearrange("p (k s) -> p k s", k=KC)
        qparts = pb["qparts"].bitcast(BF16).rearrange("p (t k s) -> p t k s", t=3, k=KC)
        kparts = pb["kparts"].bitcast(BF16).rearrange("p (t k s) -> p t k s", t=3, k=KC)
        x2T = fb["x2T"].rearrange("p (k t) -> p k t", k=KC)
        lgT = fb["lgT"]
        sh_a = fb["sa"].rearrange("p (r s) -> p r s", r=2)
        sh_z = fb["sz"].rearrange("p (r s) -> p r s", r=2)
        sh_hT = fb["shT"].rearrange("p (c s) -> p c s", c=FC)
        xb = eb["xb"].rearrange("p (r d) -> p r d", r=2)
        xbT = eb["xbT"].rearrange("p (r k s) -> p r k s", r=2, k=KC)
        e_a, e_c = fb["sa"][:, 0:F], fb["sa"][:, F:2 * F]
        e_z = eb["ez"].rearrange("p (r f) -> p r f", r=2)
        e_h = eb["eh"].rearrange("p (r f) -> p r f", r=2)
        e_hT = eb["ehT"].rearrange("p (r c s) -> p r c s", r=2, c=FC)
        e_o = eb["eo"].rearrange("p (r d) -> p r d", r=2)
        gath = fb["x2T"][:, 0:4 * TOP_K * D].rearrange("p (r k d) -> p r k d", r=4, k=TOP_K)

        lg = sb("lg", [P, NT, E])
        lsh = sb("lsh", [P, NT, E])
        lex = sb("lex", [P, NT, E])
        sco = sb("sco", [P, NT, E])
        bia = sb("bia", [P, NT, E])
        cand = sb("cand", [P, NT, E])
        oneh = sb("oneh", [P, TOP_K, NT, E])
        rt1 = sb("rt1", [P, NT])
        rt2 = sb("rt2", [P, NT])
        rw = sb("rw", [P, TOP_K, NT])
        selb = sb("selb", [P, NT, E], BF16)
        tri = sb("tri", [P, P], BF16)
        ones_b = sb("ones_b", [P, P], BF16)
        cum = sb("cum", [P, NT + 1, E])
        iota_e = sb("iota_e", [P, E])
        iota_n = sb("iota_n", [P, MAX_BLOCKS])
        iota_c = sb("iota_c", [P, NT])
        cmpc = sb("cmpc", [P, E, NT])
        nblk = sb("nblk", [P, E])
        bend = sb("bend", [P, E + 1])
        off = sb("off", [P, E])
        cmpn = sb("cmpn", [P, MAX_BLOCKS, E])
        blkf = sb("blkf", [P, MAX_BLOCKS])
        blk = sb("blk", [P, MAX_BLOCKS], I32)
        slotf = sb("slotf", [P, TOP_K, NT])
        slot = sb("slot", [P, TOP_K, NT], I32)
        zrow = sb("zrow", [P, D])

        ps = stack.enter_context(nc.psum_tensor("ps", [P, 8, 512], F32))
        stack.enter_context(nc.allow_non_contiguous_dma(reason="a few bias vectors, one value per partition"))

        s_const = sem("s_const")
        s_wq = sem("s_wq")
        s_bq = sem("s_bq")
        s_wo = sem("s_wo")
        s_sw = sem("s_sw")
        s_zero = sem("s_zero")
        s_ew = sem("s_ew")
        s_x = [sem(f"s_x{b}") for b in range(B)]
        s_c = [sem(f"s_c{r}") for r in range(2)]
        s_dve = sem("s_dve")
        s_act = sem("s_act")
        s_pool = sem("s_pool")
        s_ln = sem("s_ln")
        s_var = sem("s_var")
        s_y0 = sem("s_y0")
        s_xn = sem("s_xn")
        s_cTp = sem("s_cTp")
        s_xTp = sem("s_xTp")
        s_cT = sem("s_cT")
        s_xT = sem("s_xT")
        s_kp = sem("s_kp")
        s_qp = sem("s_qp")
        s_kf = sem("s_kf")
        s_qf = sem("s_qf")
        s_vp = sem("s_vp")
        s_v = sem("s_v")
        s_ks = sem("s_ks")
        s_qs = sem("s_qs")
        s_kd = sem("s_kd")
        s_qd = sem("s_qd")
        s_st = [sem(f"s_st{g}") for g in range(NG)]
        s_mrow = [sem(f"s_mrow{g}") for g in range(NG)]
        s_ones = sem("s_ones")
        s_rp = sem("s_rp")
        s_rc = sem("s_rc")
        s_mp = sem("s_mp")
        s_mT = sem("s_mT")
        s_s2 = sem("s_s2")
        s_exp = sem("s_exp")
        s_pv = sem("s_pv")
        s_pvc = sem("s_pvc")
        s_vg = sem("s_vg")
        s_norm = sem("s_norm")
        s_gTp = sem("s_gTp")
        s_gT = sem("s_gT")
        s_gp = sem("s_gp")
        s_ge = sem("s_ge")
        s_glp = sem("s_glp")
        s_gl = sem("s_gl")
        s_lsh = sem("s_lsh")
        s_lex = sem("s_lex")
        s_sel = sem("s_sel")
        s_cnt = sem("s_cnt")
        s_route = sem("s_route")
        s_scat = sem("s_scat")
        s_up1 = sem("s_up1")
        s_a1 = sem("s_a1")
        s_z1 = sem("s_z1")
        s_h1 = sem("s_h1")
        s_dn1 = sem("s_dn1")
        s_y1 = sem("s_y1")
        s_xb = [sem(f"s_xb{r}") for r in range(2)]
        s_xbp = sem("s_xbp")
        s_xbe = sem("s_xbe")
        s_upa = sem("s_upa")
        s_up = sem("s_up")
        s_upc = sem("s_upc")
        s_z = sem("s_z")
        s_h = sem("s_h")
        s_hp = sem("s_hp")
        s_hT = sem("s_hT")
        s_o = sem("s_o")
        s_oe = sem("s_oe")
        s_os = [sem(f"s_os{r}") for r in range(2)]
        s_g = [sem(f"s_g{r}") for r in range(4)]
        s_fin = sem("s_fin")
        s_out = sem("s_out")

        def loop(eng, lo, hi, body):
            with eng.Fori(lo, hi) as i:
                body(i)

        def pairs(eng, n, body):
            with eng.Fori(0, n // 2) as r:
                for par in range(2):
                    body(2 * r + par, par, r)

        SR = 7 * DK
        PRE = 2 * GH * TB + 1
        PER = NG * (GH * TB + 1)
        BR, BS2, BPV = 0, 3, 7

        def ring_base(b):
            return PRE + PER + (PER + TB) * (b - 1) if not isinstance(b, int) or b else PRE

        def step_units(g, with_wo, with_s1, with_m):
            units = []
            for t in range(TB):
                if t == 1 and with_m:
                    units.append(("m", 0))
                if with_s1:
                    units += [("s1", t * TB + c) for c in range(TB)]
            if g == 0 and with_wo:
                units += [("wo", j) for j in range(TB)]
            return units

        def kinds(b, g):
            first, last = isinstance(b, int) and b == 0, isinstance(b, int) and b == B - 1
            return not first, not (last and g >= NG - 2), not (last and g == NG - 1)

        def batch_units(b):
            at, offs = 0, []
            for g in range(NG):
                offs.append(at)
                at += len(step_units(g, *kinds(b, g)))
            return offs, at

        def bank_of(b, k):
            return (ring_base(b if isinstance(b, int) and b == 0 else 1) + k) % 3

        RING_END = ring_base(B - 1) + batch_units(B - 1)[1]

        block = stack.enter_context(nc.Block())

        @block.sync
        def _(sp):
            sp.dma_start(wq_sb[:, :, :], wq.rearrange("(k p) e -> p k e", p=P)).then_inc(s_wq, 16)
            sp.dma_start(bq_sb[:, :], bq.rearrange("(k p) -> p k", p=P)).then_inc(s_bq, 16)
            sp.wait_ge(s_const, 3)

            def load(b, r, n):
                if n:
                    sp.wait_ge(s_cTp, 2 * (b - 1))
                sp.dma_start(cst[:, r, :, :], ctx_v[b]).then_inc(s_c[r], 16)

            sp.sem_inc(s_kd, 16)
            sp.sem_inc(s_qd, 16)
            for r in range(2):
                sp.sem_inc(s_os[r], 16)
            for b in range(B):
                if b < 2:
                    load(b, b, 0)
                sp.dma_start(xres[:, TB * b:TB * b + TB, :], x_v[b]).then_inc(s_x[b], 16)
            for g in range(NG):
                for j in range(GH):
                    h = GH * g + j
                    sp.dma_start(wo_sb[32 * j:32 * j + DK, g, :], wo[DK * h:DK * h + DK, :]).then_inc(s_wo, 16)
            sp.dma_start(wo_sb[DK:DK + 1, 0, :], bo.rearrange("(a d) -> a d", a=1)).then_inc(s_wo, 16)
            sp.dma_start(sw13_sb[:, :, 0:F], sw1.rearrange("(k p) f -> p k f", p=P)).then_inc(s_sw, 16)
            sp.dma_start(sw13_sb[:, :, F:2 * F], sw3.rearrange("(k p) f -> p k f", p=P)).then_inc(s_sw, 16)
            sp.dma_start(sw2_sb[:, 0:FC - 1, :], sw2[0:(FC - 1) * P, :].rearrange("(c p) d -> p c d", p=P)).then_inc(s_sw, 16)
            sp.dma_start(sw2_sb[0:FL, FC - 1, :], sw2[(FC - 1) * P:F, :]).then_inc(s_sw, 16)
            sp.dma_start(sw2_sb[FL:FL + 1, FC - 1, :], sb2.rearrange("(a d) -> a d", a=1)).then_inc(s_sw, 16)
            for n, bias in enumerate((sb1, sb3)):
                sp.dma_start(sb13_sb[:, 0:FC - 1, n], bias[0:(FC - 1) * P].rearrange("(c p) -> p c", p=P)).then_inc(s_sw, 16)
                sp.dma_start(sb13_sb[0:FL, FC - 1, n:n + 1], bias[(FC - 1) * P:F].rearrange("(p a) -> p a", a=1)).then_inc(s_sw, 16)
            sp.dma_start(gw_sb[:, :, :], gate_wt.rearrange("(k p) e -> p k e", p=P)).then_inc(s_sw, 16)
            sp.dma_start(gb_sb[:, :], gate_b.rearrange("(a e) -> a e", a=1).to_broadcast([P, E])).then_inc(s_sw, 16)
            sp.dma_start(xs_dram.rearrange("(n p) d -> p n d", p=P),
                         zrow[:, :].rearrange("p (a d) -> p a d", a=1).to_broadcast([P, MAX_BLOCKS, D])).then_inc(s_zero, 16)

            def parts_out(b, par, r):
                for ready, parts, dram, s in ((s_ks, kparts, k_dram, s_kd), (s_qs, qparts, q_dram, s_qd)):
                    sp.wait_ge(ready, b + 2)
                    sp.dma_start(dram[b].rearrange("(n g) d (h s) -> (g d h) n s", g=NG // KC, s=S),
                                 parts.rearrange("p t k s -> p (t k) s")).then_inc(s, 16)

            def stacks(b, g):
                qd, kd = (dram[b].rearrange("(t g) d s -> g t d s", g=NG)[g] for dram in (q_dram, k_dram))
                for part in range(2):
                    rows = slice(3 * DK * part, 3 * DK * (part + 1))
                    sp.dma_start(q_st[rows, g, :, :].rearrange("p h s -> p (h s)"),
                                 qd[part:part + 1].to_broadcast([3, DK, GH * S])).then_inc(s_st[g], 16)
                    sp.dma_start(k_st[rows, g, :, :].rearrange("p h s -> p (h s)"), kd).then_inc(s_st[g], 16)
                rows = slice(6 * DK, 7 * DK)
                sp.dma_start(q_st[rows, g, :, :].rearrange("p h s -> p (h s)"), qd[2]).then_inc(s_st[g], 16)
                sp.dma_start(k_st[rows, g, :, :].rearrange("p h s -> p (h s)"), kd[0]).then_inc(s_st[g], 16)

            parts_out(0, 0, 0)
            load(2, 0, 1)
            sp.wait_ge(s_ones, 3)
            sp.wait_ge(s_kd, 32)
            sp.wait_ge(s_qd, 32)
            for g in range(NG):
                stacks(0, g)
            for b in range(1, B):
                parts_out(b, 0, 0)
                if b + 2 < B:
                    load(b + 2, b % 2, 1)
            sp.wait_ge(s_kd, 16 * (B + 1))
            sp.wait_ge(s_qd, 16 * (B + 1))

            def mrow(b, g, n):
                sp.wait_ge(s_mT, n + 1)
                for part in range(2):
                    sp.dma_start(q_st[SR + part:SR + part + 1, g, :, :],
                                 mT[GH * TB * part:GH * TB * (part + 1), :]).then_inc(s_mrow[g], 16)

            mrow(0, 0, 0)

            def steps(b):
                _, _, _ = kinds(b, 0)
                last = isinstance(b, int) and b == B - 1
                for g in range(NG):
                    i = NG * b + g
                    if not (last and g == NG - 1):
                        mrow(b if g < NG - 1 else b + 1, (g + 1) % NG, i + 1)
                    if not last:
                        sp.wait_ge(s_s2, 2 * TB * (i + 1))
                        stacks(b + 1, g)

            steps(0)
            loop(sp, 1, B - 1, steps)
            steps(B - 1)

            sp.wait_ge(s_pv, 2 + TB * NG * B)
            sp.wait_ge(s_vg, NG * B)
            for e in range(E):
                sp.dma_start(w13_sb[:, e, :, 0:F], w1[e].rearrange("(k p) f -> p k f", p=P)).then_inc(s_ew, 16)
                sp.dma_start(w13_sb[:, e, :, F:2 * F], w3[e].rearrange("(k p) f -> p k f", p=P)).then_inc(s_ew, 16)
                sp.dma_start(w2_sb[:, e, 0:FC - 1, :], w2[e, 0:(FC - 1) * P, :].rearrange("(c p) d -> p c d", p=P)).then_inc(s_ew, 16)
            sp.dma_start(w2_sb[0:FL, :, FC - 1, :], w2[:, (FC - 1) * P:F, :].rearrange("e p d -> p e d")).then_inc(s_ew, 16)
            sp.dma_start(w2_sb[FL:FL + 1, :, FC - 1, :], b2.rearrange("(a e) d -> a e d", a=1)).then_inc(s_ew, 16)
            for n, bias in enumerate((b1, b3)):
                sp.dma_start(b13_sb[:, :, n * F:n * F + F],
                             bias.rearrange("(a e) f -> a e f", a=1).to_broadcast([P, E, F])).then_inc(s_ew, 16)

            sp.wait_ge(s_scat, 16 * TOP_K * NT)
            sp.wait_ge(s_up1, FC * B)

            def rows_in(n, par):
                sp.wait_ge(s_xbp, n + 1)
                sp.dma_start(xb[:, par, :], xs_dram.rearrange("(n p) d -> n p d", p=P)[n]).then_inc(s_xb[par], 16)

            def results_out(n, par):
                sp.wait_ge(s_oe, n + 3)
                sp.dma_start(os_dram.rearrange("(n p) d -> n p d", p=P)[n], e_o[:, par, :]).then_inc(s_os[par], 16)

            AHEAD = 4
            for n in range(AHEAD):
                rows_in(n, n % 2)

            def blocks(n, par, r):
                rows_in(n + AHEAD, par)
                results_out(n, par)

            NP = (MAX_BLOCKS - AHEAD) // 2 * 2
            pairs(sp, NP, blocks)
            for n in range(NP, MAX_BLOCKS):
                if n + AHEAD < MAX_BLOCKS:
                    rows_in(n + AHEAD, n % 2)
                results_out(n, n % 2)

            for j in range(NT):
                sp.wait_ge(s_fin, j + 1)
                sp.dma_start(out_v[j], xres[:, j, :]).then_inc(s_out, 16)
            sp.wait_ge(s_out, 16 * NT)

        @block.gpsimd
        def _(pool):
            chain = [0]

            def link(ins):
                chain[0] += 1
                ins.then_inc(s_pool, 1)
                pool.wait_ge(s_pool, chain[0])

            pool.memset(wo_sb[:, :, :], 0.0).then_inc(s_const, 1)
            pool.memset(sw2_sb[:, FC - 1, :], 1.0).then_inc(s_const, 1)
            pool.memset(zrow[:, :], 0.0).then_inc(s_const, 1)
            link(pool.memset(ident[:, :], 0.0))
            link(pool.memset(ident_b[:, :], 0.0))
            link(pool.memset(tri[:, :], 1.0))
            for m in (ident, ident_b):
                pool.affine_select(out=m[:, :], in_=m[:, :], compare_op=ALU.not_equal, fill=1.0, base=0,
                                   pattern=[[-1, P]], channel_multiplier=1).then_inc(s_const, 1)
            pool.affine_select(out=tri[:, :], in_=tri[:, :], compare_op=ALU.is_gt, fill=0.0, base=0,
                               pattern=[[1, P]], channel_multiplier=-1).then_inc(s_const, 1)
            pool.memset(ones_b[:, :], 1.0).then_inc(s_const, 1)
            pool.iota(iota_e[:, :], [[1, E]], base=-E, channel_multiplier=0,
                      allow_small_or_imprecise_dtypes=True).then_inc(s_const, 1)
            pool.iota(iota_n[:, :], [[1, MAX_BLOCKS]], base=0, channel_multiplier=0,
                      allow_small_or_imprecise_dtypes=True).then_inc(s_const, 1)
            pool.iota(iota_c[:, :], [[P, NT]], base=0, channel_multiplier=0,
                      allow_small_or_imprecise_dtypes=True).then_inc(s_const, 1)
            link(pool.memset(tB[:, :, :], 0.0))
            pool.memset(tB[:, :, DK:DK + 1], 1.0).then_inc(s_const, 1)
            pool.sem_inc(s_ks, 1)

            def split(b):
                pool.wait_ge(s_kf, 2 * b + 4)
                pool.wait_ge(s_kd, 16 * (b + 1))
                pool.wait_ge(s_pool, 4 + 3 * b)
                pool.tensor_copy(kparts[:, 0, :, :], kf[:, :, :]).then_inc(s_pool, 1)
                pool.wait_ge(s_pool, 5 + 3 * b)
                pool.wait_ge(s_vp, 2 * b + 4)
                pool.tensor_tensor(kf[:, :, :], kf[:, :, :], kparts[:, 0, :, :], ALU.subtract).then_inc(s_pool, 1)
                pool.wait_ge(s_pool, 6 + 3 * b)
                pool.tensor_copy(kparts[:, 1, :, :], kf[:, :, :]).then_inc(s_pool, 1)
                pool.wait_ge(s_pool, 7 + 3 * b)
                pool.tensor_tensor(kparts[:, 2, :, :], kf[:, :, :], kparts[:, 1, :, :], ALU.subtract).then_inc(s_ks, 1)

            for b in range(B):
                split(b)

            def v_group(b, g):
                i = NG * b + g
                if i >= 2:
                    pool.wait_ge(s_pv, TB * (i - 1) + 2)
                pool.tensor_copy(v_grp[:, g % 2, :, :, 0:DK],
                                 v_all[:, TB * b:TB * b + TB, g, :, :].rearrange("p j d h -> p j h d")).then_inc(s_vg, 1)

            pool.wait_ge(s_v, 2 + 2 * B)
            for i in range(NG * B):
                v_group(i // NG, i % NG)

            pool.wait_ge(s_route, 1)
            pool.wait_ge(s_zero, 16)
            for j in range(NT):
                for k in range(TOP_K):
                    pool.indirect_dma_start(
                        out=xs_dram, out_offset=bass.IndirectOffsetOnAxis(ap=slot[:, k, j:j + 1], axis=0),
                        in_=xn[:, j, :], in_offset=None).then_inc(s_scat, 16)
            pool.wait_ge(s_os[0], 16 * ((MAX_BLOCKS + 1) // 2) + 16)
            pool.wait_ge(s_os[1], 16 * (MAX_BLOCKS // 2) + 16)
            for j in range(NT):
                if j >= 4:
                    pool.wait_ge(s_fin, j - 3)
                for k in range(TOP_K):
                    pool.indirect_dma_start(
                        out=gath[:, j % 4, k, :], out_offset=None, in_=os_dram,
                        in_offset=bass.IndirectOffsetOnAxis(ap=slot[:, k, j:j + 1], axis=0)).then_inc(s_g[j % 4], 16)

        @block.scalar
        def _(act):
            for s, n in ((s_cT, 2), (s_xT, 2), (s_kf, 2), (s_qf, 2), (s_exp, 2), (s_gT, 2), (s_ge, 1),
                         (s_xbe, 1), (s_h, 2), (s_hT, 1)):
                act.sem_inc(s, n)
            act.wait_ge(s_bq, 16)
            act.activation(bqs_sb[:, :], bq_sb[:, :], ACT.Copy, scale=SCALE).then_inc(s_act, 1)

            def rstd_guess(n):
                act.wait_ge(s_var, n + 1)
                act.activation(lnv[:, :], var[:, :], ACT.Ln).then_inc(s_act, 1)
                act.wait_ge(s_act, n + 2)
                act.activation(y0[:, :], lnv[:, :], ACT.Exp, scale=-0.5).then_inc(s_y0, 1)

            for n in range(B):
                rstd_guess(n)

            def evac(b):
                act.wait_ge(s_kp, 2 * b + 2)
                for c in range(KC):
                    act.wait_ge(s_cTp, 2 * b + c + 1)
                    act.activation(cT[:, c, :], ps[:, 2 + c, :], ACT.Copy).then_inc(s_cT, 1)
                act.wait_ge(s_qp, 2 * b + 2)
                for c in range(KC):
                    act.wait_ge(s_xTp, 2 * b + c + 1)
                    act.activation(xT[:, c, :], ps[:, c, :], ACT.Copy).then_inc(s_xT, 1)
                act.wait_ge(s_vp, 2 * b + 2)
                act.wait_ge(s_ks, b + 1)
                for c in range(KC):
                    act.wait_ge(s_kp, 2 * b + c + 3)
                    act.activation(kf[:, c, :], ps[:, 6 + c, :], ACT.Identity, bias=bq_sb[:, c:c + 1]).then_inc(s_kf, 1)
                act.wait_ge(s_qs, b + 1)
                for c in range(KC):
                    act.wait_ge(s_qp, 2 * b + c + 3)
                    act.activation(qf[:, c, :], ps[:, 4 + c, :], ACT.Identity, bias=bqs_sb[:, c:c + 1],
                                   scale=SCALE).then_inc(s_qf, 1)

            act.wait_ge(s_act, 1)
            loop(act, 0, B, evac)

            def exps(i):
                for t in range(TB):
                    act.wait_ge(s_pv, TB * i + t + 1)
                    for q in range(2):
                        act.wait_ge(s_s2, 2 * TB * i + 2 * t + q + 1)
                        r = 4 * (t % 2) + 2 * q
                        act.activation(probs[:, r:r + 2, :], ps[:, BS2 + 2 * q:BS2 + 2 * q + 2, :],
                                       ACT.Exp).then_inc(s_exp, 1)

            act.wait_ge(s_v, 2 + 2 * B)
            for i in range(NG):
                exps(i)

            def exps_and_guess(b):
                for g in range(NG):
                    exps(NG * b + g)
                    if g == 1:
                        rstd_guess(B - 1 + b)

            loop(act, 1, B, exps_and_guess)

            def g_evac(b):
                for c in range(KC):
                    act.wait_ge(s_gTp, 2 * b + c + 1)
                    act.activation(x2T[:, c, bass.ds(S * b, S)], ps[:, 3 + c, :], ACT.Copy).then_inc(s_gT, 1)
                act.wait_ge(s_gp, b + 1)
                act.wait_ge(s_glp, b + 1)
                act.activation(lgT[0:E, :], ps[0:E, 5, :], ACT.Copy).then_inc(s_ge, 1)

            g_evac(0)
            rstd_guess(2 * B - 1)
            loop(act, 1, B, g_evac)
            act.wait_ge(s_lsh, 1)
            act.activation(lex[:, :, :], lsh[:, :, :], ACT.Exp).then_inc(s_lex, 1)

            def shared(b):
                def first(c):
                    n = FC * b + c
                    rows = P if c < FC - 1 else FL
                    act.wait_ge(s_up1, n + 1)
                    act.activation(sh_a[0:rows, c % 2, :], ps[0:rows, 2 * (c % 2), :], ACT.Identity,
                                   bias=sb13_sb[0:rows, c, 0:1]).then_inc(s_a1, 1)

                def silu(c):
                    n = FC * b + c
                    rows = P if c < FC - 1 else FL
                    act.wait_ge(s_z1, n + 1)
                    if c == 0:
                        act.wait_ge(s_dn1, 4 * b + 4)
                    act.activation(sh_hT[0:rows, c, :], sh_z[0:rows, c % 2, :], ACT.Silu).then_inc(s_h1, 1)

                first(0)
                first(1)
                silu(0)
                first(2)
                silu(1)
                silu(2)

            loop(act, 0, B, shared)

            def x_evac(n, par):
                act.wait_ge(s_xbp, n + 3)
                act.wait_ge(s_up, n + 1)
                act.activation(xbT[:, par, :, :], ps[:, 0, 0:D].rearrange("p (k s) -> p k s", k=KC),
                               ACT.Copy).then_inc(s_xbe, 1)

            def h_make(n, par):
                act.wait_ge(s_z, n + 1)
                act.wait_ge(s_hp, n + 1)
                act.activation(e_h[:, par, :], e_z[:, par, :], ACT.Silu).then_inc(s_h, 1)

            def h_evac(n, par):
                act.wait_ge(s_hp, n + 3)
                act.wait_ge(s_o, n + 1)
                act.activation(e_hT[:, par, 0:FC - 1, :],
                               ps[:, 5, 0:(FC - 1) * P].rearrange("p (c s) -> p c s", c=FC - 1), ACT.Copy)
                act.activation(e_hT[0:FL, par, FC - 1, :], ps[0:FL, 5, (FC - 1) * P:FC * P], ACT.Copy).then_inc(s_hT, 1)

            x_evac(0, 0)
            x_evac(1, 1)
            h_make(0, 0)

            def blocks(n, par, r):
                h_evac(n, par)
                x_evac(n + 2, par)
                h_make(n + 1, 1 - par)

            NP = (MAX_BLOCKS - 2) // 2 * 2
            pairs(act, NP, blocks)
            for n in range(NP, MAX_BLOCKS):
                h_evac(n, n % 2)
                if n + 2 < MAX_BLOCKS:
                    x_evac(n + 2, n % 2)
                if n + 1 < MAX_BLOCKS:
                    h_make(n + 1, 1 - n % 2)

        @block.vector
        def _(dve):
            for s, n in ((s_v, 2), (s_qs, 1), (s_rc, 3), (s_pvc, 1), (s_gl, 1), (s_y1, 1), (s_upc, 2), (s_oe, 2)):
                dve.sem_inc(s, n)
            dve.memset(k_st[96:128, :, :, :], 1.0).then_inc(s_ones, 1)
            for r in range(2):
                dve.memset(v_grp[:, r, :, :, DK:32], 1.0).then_inc(s_ones, 1)
            N_LN = 2 * TB + 4

            def norm_stats(n, b):
                for j in range(TB):
                    dve.bn_stats(stats[:, j, :], xres[:, TB * b + j, :]).then_inc(s_ln, 1)

            def norm_means(n):
                for j in range(TB):
                    dve.bn_aggr(mv[:, j, :], stats[:, j, :]).then_inc(s_ln, 1)

            def norm_var(n):
                dve.wait_ge(s_ln, N_LN * n + 2 * TB)
                dve.tensor_scalar_add(var[:, :], mv[:, :, 1], EPS).then_inc(s_var, 1)

            def norm_rstd(n):
                c0 = N_LN * n + 2 * TB
                dve.wait_ge(s_y0, n + 1)
                dve.wait_ge(s_var, n + 1)
                dve.tensor_tensor(newt[:, :], y0[:, :], y0[:, :], ALU.mult).then_inc(s_ln, 1)
                dve.wait_ge(s_ln, c0 + 1)
                dve.tensor_tensor(newt[:, :], newt[:, :], var[:, :], ALU.mult).then_inc(s_ln, 1)
                dve.wait_ge(s_ln, c0 + 2)
                dve.tensor_scalar(newt[:, :], newt[:, :], -0.5, 1.5, ALU.mult, ALU.add).then_inc(s_ln, 1)
                dve.wait_ge(s_ln, c0 + 3)
                dve.tensor_tensor(rstd[:, :], newt[:, :], y0[:, :], ALU.mult).then_inc(s_ln, 1)

            def norm_apply(n, b):
                dve.wait_ge(s_ln, N_LN * (n + 1))
                for j in range(TB):
                    ins = dve.tensor_scalar(xn[:, TB * b + j, :], xres[:, TB * b + j, :], mv[:, j, 0:1],
                                            rstd[:, j:j + 1], ALU.subtract, ALU.mult)
                ins.then_inc(s_xn, 1)

            def layer_norm(n, b):
                norm_stats(n, b)
                dve.wait_ge(s_ln, N_LN * n + TB)
                norm_means(n)
                norm_var(n)
                norm_rstd(n)
                norm_apply(n, b)

            for b in range(B):
                dve.wait_ge(s_x[b], 16)
                if b:
                    dve.wait_ge(s_xn, b)
                layer_norm(b, b)
            at = [0]

            def project(b):
                for half in range(2):
                    dve.wait_ge(s_vp, 2 * b + half + 3)
                    dve.tensor_copy(v_all[:, bass.ds(TB * b + 2 * half, 2), :, :, :].rearrange("p j g d h -> p (j g d h)"),
                                    ps[:, 2 + half, :]).then_inc(s_v, 1)
                c0 = 3 * b
                dve.wait_ge(s_qf, 2 * b + 4)
                dve.wait_ge(s_qd, 16 * (b + 1))
                dve.tensor_copy(qparts[:, 0, :, :], qf[:, :, :]).then_inc(s_dve, 1)
                dve.wait_ge(s_dve, c0 + 1)
                dve.tensor_tensor(qf[:, :, :], qf[:, :, :], qparts[:, 0, :, :], ALU.subtract).then_inc(s_dve, 1)
                dve.wait_ge(s_dve, c0 + 2)
                dve.tensor_copy(qparts[:, 1, :, :], qf[:, :, :]).then_inc(s_dve, 1)
                dve.wait_ge(s_dve, c0 + 3)
                dve.tensor_tensor(qparts[:, 2, :, :], qf[:, :, :], qparts[:, 1, :, :], ALU.subtract).then_inc(s_qs, 1)

            loop(dve, 0, B, project)
            at[0] += 3 * B

            STEP = GH * TB + 1 + 3
            A0 = at[0]

            def scores_tile(n, bank, u, par):
                dve.wait_ge(s_rp, n + 1)
                dve.tensor_reduce(nmax[:, par, u:u + 1], ps[:, BR + bank, :], AX_X, ALU.max, negate=True).then_inc(s_rc, 1)

            def max_parts(n, par, last_unit, c0):
                dve.wait_ge(s_rc, 3 + last_unit + 1)
                dve.wait_ge(s_rp, last_unit + 1)
                dve.tensor_copy(mparts[:, 0, :], nmax[:, par, :]).then_inc(s_dve, 1)
                dve.wait_ge(s_dve, c0 + 1)
                dve.tensor_tensor(mparts[:, 1, :], nmax[:, par, :], mparts[:, 0, :], ALU.subtract).then_inc(s_mp, 1)

            def max_rows(n, bank, after):
                dve.wait_ge(s_rp, n + 1)
                after()
                dve.tensor_copy(mT[:, :], ps[0:2 * GH * TB, BR + bank, 0:P // 2].bitcast(BF16)).then_inc(s_mT, 1)
                dve.wait_ge(s_mT, 1)

            def outputs_copy(i):
                dve.wait_ge(s_pv, 2 + TB * i + TB)
                dve.transpose(tA[:, :, :].rearrange("p a b -> p (a b)"), ps[:, BPV, :]).then_inc(s_pvc, 1)

            def outputs_rsum(i, c0):
                dve.wait_ge(s_pvc, i + 2)
                dve.reciprocal(rsum[:, :], tA[:, :, DK]).then_inc(s_dve, 1)

            def outputs_scale(i, c0):
                dve.wait_ge(s_dve, c0 + 1)
                dve.tensor_tensor(tB[:, :, 0:DK], tA[:, :, 0:DK],
                                  rsum[:, :].rearrange("p (a b) -> p a b", b=1).to_broadcast([P, S // 32, DK]),
                                  ALU.mult).then_inc(s_dve, 1)

            def outputs_back(i, g, c0):
                dve.wait_ge(s_dve, c0 + 2)
                dve.transpose(aT[:, g, :], tB[:, :, :].rearrange("p a b -> p (a b)")).then_inc(s_norm, 1)

            def normalise(i, g, c0):
                outputs_copy(i)
                outputs_rsum(i, c0)
                outputs_scale(i, c0)
                outputs_back(i, g, c0)

            def x_one(n, bank, tile, k):
                dve.wait_ge(s_rp, n + 1)
                dve.tensor_tensor(xres[:, tile, :], ps[:, BR + bank, 0:D], xres[:, tile, :], ALU.add).then_inc(s_rc, 1)

            dve.wait_ge(s_const, 11)
            for n in range(2):
                for u in range(GH * TB):
                    k = n * (GH * TB + 1) + u
                    scores_tile(k, k % 3, u, n)
                if n == 0:
                    max_parts(0, 0, GH * TB - 1, A0)
                    m_unit = GH * TB
                    max_rows(m_unit, m_unit % 3, lambda: None)
                    dve.wait_ge(s_mT, 1)
                    dve.sem_inc(s_rc, 1)
            max_parts(1, 1, PRE - 1, A0 + 1)
            A1 = A0 + 2

            def steps(b):
                offs, total = batch_units(b)
                rb = ring_base(b)
                for g in range(NG):
                    i = NG * b + g
                    with_wo, with_s1, with_m = kinds(b, g)
                    units = step_units(g, with_wo, with_s1, with_m)
                    c0 = A1 + 3 * i - 2 if with_m else A1 + 3 * i - 3
                    first_step = isinstance(i, int) and i == 0
                    if not first_step and not with_s1:
                        normalise(i - 1, (g - 1) % NG, c0)
                    for k, (kind, u) in enumerate(units):
                        n = rb + offs[g] + k
                        bank = bank_of(b, offs[g] + k)
                        if kind == "s1":
                            if u == 0:
                                dve.wait_ge(s_mp, i + 1)
                                if g == 1 and with_wo:
                                    dve.wait_ge(s_rc, rb + offs[1] + 3)
                            if g == 1 and with_wo and u == 10:
                                dve.wait_ge(s_ln, N_LN * (B - 1 + b) + TB)
                            scores_tile(n, bank, u, g % 2)
                            if u == 4 and not first_step:
                                outputs_copy(i - 1)
                            if u == 5 and not first_step:
                                outputs_rsum(i - 1, c0)
                            if u == 6 and not first_step:
                                outputs_scale(i - 1, c0)
                            if u == 7 and not first_step:
                                outputs_back(i - 1, (g - 1) % NG, c0)
                            if g == 1 and with_wo:
                                if u == 0:
                                    norm_stats(B - 1 + b, b - 1)
                                if u == 10:
                                    norm_means(B - 1 + b)
                                if u == 11:
                                    norm_var(B - 1 + b)
                            if g == 2 and u == 8 and with_wo:
                                norm_rstd(B - 1 + b)
                            if g == 2 and u == 9 and with_wo:
                                norm_apply(B - 1 + b, b - 1)
                        elif kind == "m":
                            max_rows(n, bank, lambda: dve.wait_ge(s_mrow[g], 32 * (b + 1)))
                            dve.wait_ge(s_mT, i + 2)
                            dve.sem_inc(s_rc, 1)
                        else:
                            x_one(n, bank, TB * (b - 1) + u, k)
                    if g == 2 and with_wo and not with_s1:
                        norm_rstd(B - 1 + b)
                        norm_apply(B - 1 + b, b - 1)
                    if with_s1:
                        s1_last = max(k for k, (kind, u) in enumerate(units) if kind == "s1")
                        max_parts(i + 2, g % 2, rb + offs[g] + s1_last, c0 + 2)

            steps(0)
            loop(dve, 1, B - 1, steps)
            steps(B - 1)
            normalise(NG * B - 1, NG - 1, A1 + 3 * (NG * B) - 4)
            for j in range(TB):
                x_one(RING_END + j, (bank_of(1, 0) + (RING_END - ring_base(1)) + j) % 3, TB * (B - 1) + j, j)
            A2 = A1 + 3 * NG * B - 4 + 2

            dve.wait_ge(s_rc, 3 + RING_END + TB)
            layer_norm(2 * B - 1, B - 1)
            c = [A2]

            def logits(b):
                dve.wait_ge(s_glp, b + 2)
                dve.tensor_copy(lg[:, bass.ds(TB * b, TB), :],
                                ps[:, 6, 0:TB * E].rearrange("p (j e) -> p j e", j=TB)).then_inc(s_gl, 1)

            loop(dve, 0, B, logits)
            dve.wait_ge(s_gl, 1 + B)
            dve.wait_ge(s_sw, 16 * 11)

            def shared(b):
                for c in range(FC):
                    n = FC * b + c
                    rows = P if c < FC - 1 else FL
                    dve.wait_ge(s_a1, n + 1)
                    if not isinstance(b, int) or n >= 2:
                        dve.wait_ge(s_h1, n - 1)
                    dve.scalar_tensor_tensor(sh_z[0:rows, c % 2, :], ps[0:rows, 2 * (c % 2) + 1, :],
                                             sb13_sb[0:rows, c, 1:2], sh_a[0:rows, c % 2, :],
                                             ALU.add, ALU.mult).then_inc(s_z1, 1)
                for j in range(TB):
                    dve.wait_ge(s_dn1, 4 * b + j + 5)
                    if j % 2 == 1:
                        tile = TB * b + j - 1
                        dve.tensor_tensor(xres[:, bass.ds(tile, 2), :],
                                          ps[:, 6 + j // 2, :].rearrange("p (j d) -> p j d", j=2),
                                          xres[:, bass.ds(tile, 2), :], ALU.add).then_inc(s_y1, 1)

            def link(ins):
                c[0] += 1
                ins.then_inc(s_dve, 1)
                dve.wait_ge(s_dve, c[0])

            def over_e(v):
                return v.rearrange("p (j a) -> p j a", a=1).to_broadcast([P, NT, E])

            def over_j(v):
                return v.rearrange("p (a e) -> p a e", a=1).to_broadcast([P, NT, E])

            link(dve.reduce_max(rt1[:, :], lg[:, :, :], axis=AX_X))
            dve.tensor_tensor(lsh[:, :, :], lg[:, :, :], over_e(rt1[:, :]), ALU.subtract).then_inc(s_lsh, 1)
            dve.wait_ge(s_lex, 1)
            link(dve.reduce_sum(rt1[:, :], lex[:, :, :], axis=AX_X))
            link(dve.reciprocal(rt2[:, :], rt1[:, :]))
            link(dve.tensor_tensor(sco[:, :, :], lex[:, :, :], over_e(rt2[:, :]), ALU.mult))
            link(dve.tensor_tensor(bia[:, :, :], sco[:, :, :], over_j(gb_sb[:, :]), ALU.add))
            for k in range(TOP_K):
                link(dve.reduce_max(rt1[:, :], bia[:, :, :], axis=AX_X))
                link(dve.tensor_tensor(cand[:, :, :], bia[:, :, :], over_e(rt1[:, :]), ALU.is_equal))
                link(dve.tensor_tensor(cand[:, :, :], cand[:, :, :], over_j(iota_e[:, :]), ALU.mult))
                link(dve.tensor_reduce(rt2[:, :], cand[:, :, :], AX_X, ALU.min))
                link(dve.tensor_tensor(oneh[:, k, :, :], over_j(iota_e[:, :]), over_e(rt2[:, :]), ALU.is_equal))
                link(dve.tensor_tensor(cand[:, :, :], sco[:, :, :], oneh[:, k, :, :], ALU.mult))
                link(dve.reduce_sum(rw[:, k, :], cand[:, :, :], axis=AX_X))
                if k + 1 < TOP_K:
                    link(dve.scalar_tensor_tensor(bia[:, :, :], oneh[:, k, :, :], -3.0e38, bia[:, :, :],
                                                  ALU.mult, ALU.add))
            dve.tensor_tensor(selb[:, :, :], oneh[:, 0, :, :], oneh[:, 1, :, :], ALU.add).then_inc(s_sel, 1)
            link(dve.memset(sh_hT[96:128, FC - 1, :], 1.0))
            shared(0)

            dve.wait_ge(s_cnt, 1)
            before = ps[:, 4, 0:NT * E].rearrange("p (j e) -> p j e", j=NT)
            whole = ps[:, 4, NT * E:2 * NT * E].rearrange("p (j e) -> p j e", j=NT)
            link(dve.memset(cum[:, 0, :], 0.0))
            for j in range(NT):
                link(dve.tensor_tensor(cum[:, j + 1, :], whole[:, j, :], cum[:, j, :], ALU.add))
            link(dve.tensor_tensor(cmpc[:, :, :],
                                   cum[:, NT, :].rearrange("p (e a) -> p e a", a=1).to_broadcast([P, E, NT]),
                                   iota_c[:, :].rearrange("p (a n) -> p a n", a=1).to_broadcast([P, E, NT]), ALU.is_gt))
            link(dve.reduce_sum(nblk[:, :], cmpc[:, :, :], axis=AX_X))
            link(dve.memset(bend[:, 0:1], 0.0))
            for e in range(E):
                link(dve.tensor_tensor(bend[:, e + 1:e + 2], bend[:, e:e + 1], nblk[:, e:e + 1], ALU.add))
            link(dve.tensor_tensor(cmpn[:, :, :],
                                   iota_n[:, :].rearrange("p (n a) -> p n a", a=1).to_broadcast([P, MAX_BLOCKS, E]),
                                   bend[:, 1:E + 1].rearrange("p (a e) -> p a e", a=1).to_broadcast([P, MAX_BLOCKS, E]),
                                   ALU.is_ge))
            link(dve.reduce_sum(blkf[:, :], cmpn[:, :, :], axis=AX_X))
            link(dve.tensor_scalar_min(blkf[:, :], blkf[:, :], float(E - 1)))
            link(dve.tensor_copy(blk[:, :], blkf[:, :]))
            link(dve.tensor_scalar_mul(off[:, :], bend[:, 0:E], float(P)))
            link(dve.tensor_tensor(cand[:, :, :], before, cum[:, 0:NT, :], ALU.add))
            link(dve.tensor_tensor(cand[:, :, :], cand[:, :, :], over_j(off[:, :]), ALU.add))
            for k in range(TOP_K):
                link(dve.tensor_tensor(lsh[:, :, :], cand[:, :, :], oneh[:, k, :, :], ALU.mult))
                link(dve.reduce_sum(slotf[:, k, :], lsh[:, :, :], axis=AX_X))
            dve.tensor_copy(slot[:, :, :], slotf[:, :, :]).then_inc(s_route, 1)
            loop(dve, 1, B, shared)
            dve.wait_ge(s_up1, FC * B)
            link(dve.memset(e_hT[96:128, :, FC - 1, :], 1.0))
            A3 = c[0]

            dve.wait_ge(s_ew, 16 * (3 * E + 4))

            def blocks(n, par):
                ex = dve.value_load(blk[0:1, bass.ds(n, 1)], min_val=0, max_val=E - 1)
                dve.wait_ge(s_upa, n + 1)
                if not isinstance(n, int) or n:
                    dve.wait_ge(s_z, n)
                dve.tensor_tensor(e_a[:, :], ps[:, 1 + 2 * par, 0:F], b13_sb[:, ex, 0:F], ALU.add).then_inc(s_dve, 1)
                dve.wait_ge(s_up, n + 3)
                dve.tensor_tensor(e_c[:, :], ps[:, 2 + 2 * par, 0:F], b13_sb[:, ex, F:2 * F], ALU.add).then_inc(s_upc, 1)
                dve.wait_ge(s_dve, A3 + 1 + n)
                dve.wait_ge(s_upc, n + 3)
                dve.wait_ge(s_h, n + 1)
                dve.tensor_tensor(e_z[:, par, :], e_a[:, :], e_c[:, :], ALU.mult).then_inc(s_z, 1)

            def results(n, par, r):
                dve.wait_ge(s_o, n + 3)
                dve.wait_ge(s_os[par], 16 * r + 16)
                dve.tensor_copy(e_o[:, par, :], ps[:, 6 + par, 0:D]).then_inc(s_oe, 1)

            blocks(0, 0)

            def pair(n, par, r):
                blocks(n + 1, 1 - par)
                results(n, par, r)

            NP = (MAX_BLOCKS - 1) // 2 * 2
            pairs(dve, NP, pair)
            for n in range(NP, MAX_BLOCKS):
                if n + 1 < MAX_BLOCKS:
                    blocks(n + 1, 1 - n % 2)
                results(n, n % 2, n // 2)

            A4 = A3 + MAX_BLOCKS
            for j in range(NT):
                dve.wait_ge(s_g[j % 4], 32 * (j // 4) + 32)
                dve.scalar_tensor_tensor(xres[:, j, :], gath[:, j % 4, 0, :], rw[:, 0, j:j + 1], xres[:, j, :],
                                         ALU.mult, ALU.add).then_inc(s_dve, 1)
                dve.wait_ge(s_dve, A4 + j + 1)
                dve.scalar_tensor_tensor(xres[:, j, :], gath[:, j % 4, 1, :], rw[:, 1, j:j + 1], xres[:, j, :],
                                         ALU.mult, ALU.add).then_inc(s_fin, 1)

        @block.tensor
        def _(pe):
            for s, n in ((s_kp, 2), (s_qp, 2), (s_vp, 2), (s_pv, 2), (s_glp, 1), (s_dn1, 4), (s_xbp, 2),
                         (s_up, 2), (s_hp, 2), (s_o, 2)):
                pe.sem_inc(s, n)
            pe.wait_ge(s_const, 11)
            pe.wait_ge(s_wq, 16)

            def project(b, par, r):
                pe.wait_ge(s_c[par], 16 * r + 16)
                pe.wait_ge(s_v, 2 * b + 2)
                for c in range(KC):
                    for j in range(TB):
                        ins = pe.transpose(ps[:, 2 + c, P * j:P * j + P], cst[:, par, j, P * c:P * c + P], ident[:, :])
                    ins.then_inc(s_cTp, 1)
                pe.wait_ge(s_xn, b + 1)
                pe.wait_ge(s_xT, 2 * b + 2)
                for c in range(KC):
                    for j in range(TB):
                        ins = pe.transpose(ps[:, c, P * j:P * j + P], xn_tile(b, j, c), ident[:, :])
                    ins.then_inc(s_xTp, 1)
                pe.wait_ge(s_cT, 2 * b + 4)
                pe.wait_ge(s_kf, 2 * b + 2)
                for c in range(KC):
                    for k in range(KC):
                        ins = pe.matmul(ps[:, 6 + c, :], wq_sb[:, k, P * c:P * c + P], cT[:, k, :],
                                        start=(k == 0), stop=(k == KC - 1))
                    ins.then_inc(s_kp, 1)
                pe.wait_ge(s_xT, 2 * b + 4)
                pe.wait_ge(s_qf, 2 * b + 2)
                for c in range(KC):
                    for k in range(KC):
                        ins = pe.matmul(ps[:, 4 + c, :], wq_sb[:, k, P * c:P * c + P], xT[:, k, :],
                                        start=(k == 0), stop=(k == KC - 1))
                    ins.then_inc(s_qp, 1)
                pe.wait_ge(s_kf, 2 * b + 4)
                for j in range(TB):
                    for c in range(KC):
                        ins = pe.transpose(ps[:, 2 + j // 2, D * (j % 2) + P * c:D * (j % 2) + P * c + P],
                                           kf[:, c, P * j:P * j + P], ident[:, :])
                    if j % 2:
                        ins.then_inc(s_vp, 1)

            def xn_tile(b, j, c):
                return xn[:, TB * b + j, P * c:P * c + P]

            for b in range(B):
                project(b, b % 2, b // 2)

            pe.wait_ge(s_v, 2 + 2 * B)
            pe.wait_ge(s_qf, 2 + 2 * B)
            pe.wait_ge(s_ones, 3)

            def scores_for_max(n, bank, slot_, u):
                j, c = u // TB, u % TB
                pe.wait_ge(s_rc, n + 1)
                pe.matmul(ps[:, BR + bank, :], q_st[0:SR, slot_, j, P * c:P * c + P], k_st[0:SR, slot_, j, :],
                          start=True, stop=True).then_inc(s_rp, 1)

            def maxima(n, bank, i):
                pe.wait_ge(s_rc, n + 1)
                pe.wait_ge(s_mp, i + 1)
                pe.transpose(ps[0:2 * GH * TB, BR + bank, 0:P // 2].bitcast(BF16),
                             mparts[:, :, :].rearrange("p a b -> p (a b)"), ident_b[:, :]).then_inc(s_rp, 1)

            def out_projection(n, bank, j):
                pe.wait_ge(s_rc, n + 1)
                for g in range(NG):
                    ins = pe.matmul(ps[:, BR + bank, 0:D], aT[:, g, P * j:P * j + P], wo_sb[:, g, :],
                                    start=(g == 0), stop=(g == NG - 1))
                ins.then_inc(s_rp, 1)

            def weighted_sum(i, g, t):
                pe.wait_ge(s_exp, 2 + 2 * TB * i + 2 * t + 2)
                if t == 0:
                    pe.wait_ge(s_pvc, i + 1)
                    pe.wait_ge(s_vg, i + 1)
                for j in range(GH):
                    ins = pe.matmul(ps[32 * j:32 * j + 32, BPV, :], v_grp[:, g % 2, t, j, :],
                                    probs[:, 4 * (t % 2) + j, :], start=(t == 0), stop=(t == TB - 1))
                ins.then_inc(s_pv, 1)

            for n in range(2):
                pe.wait_ge(s_st[n], 16 * 6)
                for u in range(GH * TB):
                    k = n * (GH * TB + 1) + u
                    scores_for_max(k, k % 3, n, u)
                if n == 0:
                    maxima(GH * TB, (GH * TB) % 3, 0)

            def steps(b):
                offs, total = batch_units(b)
                rb = ring_base(b)
                for g in range(NG):
                    i = NG * b + g
                    with_wo, with_s1, with_m = kinds(b, g)
                    k = offs[g]
                    pe.wait_ge(s_mrow[g], 32 * (b + 1))
                    if with_s1:
                        b2_ = b if g + 2 < NG else b + 1
                        pe.wait_ge(s_st[(g + 2) % NG], 16 * 6 * (b2_ + 1))
                    for t in range(TB):
                        for q in range(2):
                            pe.wait_ge(s_exp, 2 * TB * i + 2 * t + q + 1)
                            for j in (2 * q, 2 * q + 1):
                                ins = pe.matmul(ps[:, BS2 + j, :], k_st[0:SR + 2, g, j, P * t:P * t + P],
                                                q_st[0:SR + 2, g, j, :], start=True, stop=True)
                            ins.then_inc(s_s2, 1)
                        if t == 1 and with_m:
                            maxima(rb + k, bank_of(b, k), i + 1)
                            k += 1
                        if with_s1:
                            for c in range(TB):
                                scores_for_max(rb + k, bank_of(b, k), (g + 2) % NG, t * TB + c)
                                k += 1
                        if t > 0:
                            weighted_sum(i, g, t - 1)
                        elif not (isinstance(i, int) and i == 0):
                            weighted_sum(i - 1, (g - 1) % NG, TB - 1)
                    if g == 0 and with_wo:
                        pe.wait_ge(s_norm, NG * b)
                        for j in range(TB):
                            out_projection(rb + k, bank_of(b, k), j)
                            k += 1

            pe.wait_ge(s_wo, 16 * (H + 1))
            steps(0)
            loop(pe, 1, B - 1, steps)
            steps(B - 1)
            weighted_sum(NG * B - 1, NG - 1, TB - 1)
            pe.wait_ge(s_exp, 2 + 2 * TB * NG * B)
            pe.wait_ge(s_sw, 16 * 11)

            def router(b):
                pe.wait_ge(s_xn, B + b + 1)
                pe.wait_ge(s_gT, 2 * b + 2)
                for c in range(KC):
                    for j in range(TB):
                        ins = pe.transpose(ps[:, 3 + c, P * j:P * j + P], xn_tile(b, j, c), ident[:, :])
                    ins.then_inc(s_gTp, 1)
                pe.wait_ge(s_gT, 2 * b + 4)
                pe.wait_ge(s_ge, b + 1)
                for k in range(KC):
                    ins = pe.matmul(ps[0:E, 5, :], gw_sb[:, k, :], x2T[:, k, bass.ds(S * b, S)],
                                    start=(k == 0), stop=(k == KC - 1))
                ins.then_inc(s_gp, 1)
                pe.wait_ge(s_ge, b + 2)
                pe.wait_ge(s_gl, b + 1)
                for j in range(TB):
                    ins = pe.transpose(ps[:, 6, E * j:E * j + E], lgT[0:E, P * j:P * j + P], ident[0:E, 0:E])
                ins.then_inc(s_glp, 1)

            router(0)
            pe.wait_ge(s_norm, NG * B)
            for j in range(TB):
                out_projection(RING_END + j, (bank_of(1, 0) + (RING_END - ring_base(1)) + j) % 3, j)
            for b in range(1, B):
                router(b)

            def counts():
                pe.wait_ge(s_sel, 1)
                sel = selb[:, :, :].rearrange("p j e -> p (j e)")
                pe.matmul(ps[:, 4, 0:NT * E], tri[:, :], sel, start=True, stop=True)
                pe.matmul(ps[:, 4, NT * E:2 * NT * E], ones_b[:, :], sel, start=True, stop=True).then_inc(s_cnt, 1)

            def shared(b):
                def up(c):
                    n = FC * b + c
                    rows = P if c < FC - 1 else FL
                    if not (isinstance(b, int) and b == 0 and c < 2):
                        pe.wait_ge(s_z1, n - 1)
                    for half in range(2):
                        for k in range(KC):
                            ins = pe.matmul(ps[0:rows, 2 * (c % 2) + half, :],
                                            sw13_sb[:, k, F * half + P * c:F * half + P * c + rows],
                                            x2T[:, k, bass.ds(S * b, S)], start=(k == 0), stop=(k == KC - 1))
                    ins.then_inc(s_up1, 1)

                for c in range(FC):
                    up(c)
                pe.wait_ge(s_h1, FC * b + FC)
                pe.wait_ge(s_y1, 2 * b + 1)
                for j in range(TB):
                    for c in range(FC):
                        rows = P if c < FC - 1 else FL + 1
                        ins = pe.matmul(ps[:, 6 + j // 2, D * (j % 2):D * (j % 2) + D], sh_hT[0:rows, c, P * j:P * j + P],
                                        sw2_sb[0:rows, c, :], start=(c == 0), stop=(c == FC - 1))
                    ins.then_inc(s_dn1, 1)

            pe.wait_ge(s_rc, 3 + RING_END + TB)
            pe.wait_ge(s_gl, 1 + B)
            shared(0)
            counts()
            loop(pe, 1, B, shared)

            pe.wait_ge(s_ew, 16 * (3 * E + 4))
            pe.wait_ge(s_y1, 1 + 2 * B)
            pe.wait_ge(s_z1, FC * B)

            def expert_of(n):
                return pe.value_load(blk[0:1, bass.ds(n, 1)], min_val=0, max_val=E - 1)

            def x_transpose(n, par, r):
                pe.wait_ge(s_xb[par], 16 * r + 16)
                pe.wait_ge(s_xbe, n + 1)
                for k in range(KC):
                    ins = pe.transpose(ps[:, 0, P * k:P * k + P], xb[:, par, P * k:P * k + P], ident[:, :])
                ins.then_inc(s_xbp, 1)

            def up(n, par, half, ex):
                if half == 0:
                    pe.wait_ge(s_xbe, n + 2)
                    pe.wait_ge(s_upc, n + 1)
                for k in range(KC):
                    ins = pe.matmul(ps[:, 1 + 2 * par + half, 0:F], xbT[:, par, k, :],
                                    w13_sb[:, ex, k, F * half:F * half + F], start=(k == 0), stop=(k == KC - 1))
                ins.then_inc((s_upa, s_up)[half], 1)

            def h_transpose(n, par):
                pe.wait_ge(s_h, n + 3)
                pe.wait_ge(s_hT, n + 1)
                for c in range(FC):
                    rows = P if c < FC - 1 else FL
                    ins = pe.transpose(ps[0:rows, 5, P * c:P * c + P], e_h[:, par, P * c:P * c + rows], ident[:, :])
                ins.then_inc(s_hp, 1)

            def down(n, par, ex):
                pe.wait_ge(s_hT, n + 2)
                pe.wait_ge(s_oe, n + 1)
                for c in range(FC):
                    rows = P if c < FC - 1 else FL + 1
                    ins = pe.matmul(ps[:, 6 + par, 0:D], e_hT[0:rows, par, c, :], w2_sb[0:rows, ex, c, :],
                                    start=(c == 0), stop=(c == FC - 1))
                ins.then_inc(s_o, 1)

            def step(n, par, r):
                if not isinstance(n, int) or n + 1 < MAX_BLOCKS:
                    ex_next = expert_of(n + 1)
                    up(n + 1, 1 - par, 0, ex_next)
                h_transpose(n, par)
                if not isinstance(n, int) or n + 2 < MAX_BLOCKS:
                    x_transpose(n + 2, par, r + 1)
                if not isinstance(n, int) or n + 1 < MAX_BLOCKS:
                    up(n + 1, 1 - par, 1, ex_next)
                down(n, par, expert_of(n))

            x_transpose(0, 0, 0)
            x_transpose(1, 1, 0)
            ex_first = expert_of(0)
            up(0, 0, 0, ex_first)
            up(0, 0, 1, ex_first)
            NP = (MAX_BLOCKS - 2) // 2 * 2
            pairs(pe, NP, step)
            for n in range(NP, MAX_BLOCKS):
                step(n, n % 2, n // 2)


_NAMES = ["x", "ctx_1024", "L0_xattn_Wq", "L0_xattn_bq", "L0_xattn_Wo", "L0_xattn_bo", "L0_ffn_gate_w",
          "L0_ffn_gate_b", "L0_ffn_w1", "L0_ffn_b1", "L0_ffn_w3", "L0_ffn_b3", "L0_ffn_w2", "L0_ffn_b2",
          "L0_ffn_sw1", "L0_ffn_sb1", "L0_ffn_sw3", "L0_ffn_sb3", "L0_ffn_sw2", "L0_ffn_sb2"]


def kernel(**inputs):
    import numpy as _np
    import concourse.bacc as _bacc
    from concourse import mybir as _mybir
    from concourse.bass_utils import run_bass_kernel_spmd as _run

    nc = _bacc.Bacc("TRN2", target_bir_lowering=False, num_devices=1)
    arrays, args = {}, []
    for name in _NAMES:
        a = _np.asarray(inputs[name])
        if name == "L0_ffn_gate_w":
            a = a.T
        if name in ("L0_xattn_Wq", "L0_xattn_bq"):
            a = _np.swapaxes(a.reshape(a.shape[:-1] + (4, 4, 16)), -1, -2).reshape(a.shape)
        a = _np.ascontiguousarray(a)
        arrays[f"in_{name}"] = a
        args.append(nc.dram_tensor(f"in_{name}", a.shape, _mybir.dt.from_np(a.dtype), kind="ExternalInput").ap())
    shape = inputs["x"].shape
    out = nc.dram_tensor("out_x", shape, _mybir.dt.float32, kind="ExternalOutput").ap()
    xattn_moe_kernel(nc, *args, out)
    r = _run(nc, [arrays], core_ids=[0])
    return r.results[0]["out_x"]
```

```python
from contextlib import ExitStack

import concourse.bass as bass
from concourse import mybir

ALU = mybir.AluOpType
ACT = mybir.ActivationFunctionType
AX_X = mybir.AxisListType.X
F32 = mybir.dt.float32
BF16 = mybir.dt.bfloat16
I32 = mybir.dt.int32

P = 128
EPS = 1e-5
TOP_K = 2
BF16_PAIR_OF_ONES = (1.0 + 127 / 2 ** 16)


def xattn_moe_kernel(nc, x, ctx_in, wq, bq, wo, bo, gate_wt, gate_b, w1, b1, w3, b3, w2, b2,
                     sw1, sb1, sw3, sb3, sw2, sb2, out):
    B, S, D = x.shape
    T = B * S
    NT = T // P
    TB = S // P
    DK = 16
    H = D // DK
    GH = 4
    NG = H // GH
    KC = D // P
    E, _, F = w1.shape
    FC = -(-F // P)
    FL = F - (FC - 1) * P
    MAX_BLOCKS = (T * TOP_K + E * (P - 1)) // P
    REG = T + P
    SPARE = E * REG
    SB = B - 2
    EARLY = 1
    SPARE_BLOCKS = MAX_BLOCKS - T * TOP_K // P
    assert B % 2 == 0 and S == 512 and D == 256 and H == 16 and FL % 32 == 0 and FL < P
    SCALE = float(DK) ** -0.5

    x_v = x.rearrange("b (j p) d -> b p j d", p=P)
    ctx_v = ctx_in.rearrange("b (j p) d -> b p j d", p=P)
    out_v = out.rearrange("b (j p) d -> (b j) p d", p=P)

    q_dram = nc.dram_tensor("q_parts", (B, 3 * NG, DK, GH * S), BF16).ap()
    k_dram = nc.dram_tensor("k_parts", (B, 3 * NG, DK, GH * S), BF16).ap()
    xs_dram = nc.dram_tensor("slot_rows", (SPARE + SPARE_BLOCKS * P, D), F32).ap()
    os_dram = nc.dram_tensor("block_results", (MAX_BLOCKS * P, D), F32).ap()

    with ExitStack() as stack:
        def sb(name, shape, dt=F32):
            return stack.enter_context(nc.sbuf_tensor(name, shape, dt))

        def sem(name):
            return stack.enter_context(nc.semaphore(name))

        xres = sb("xres", [P, NT, D])
        xn = sb("xn", [P, NT, D])
        wq_sb = sb("wq_sb", [P, KC, D])
        bq_sb = sb("bq_sb", [P, KC])
        bqs_sb = sb("bqs_sb", [P, KC])
        wo_sb = sb("wo_sb", [P, NG // 2, D])
        bo_sb = sb("bo_sb", [P, D])
        ident = sb("ident", [P, P])
        ident_b = sb("ident_b", [P, P], BF16)
        stats = sb("stats", [P, NT, 6])
        mv = sb("mv", [P, NT, 2])
        var = sb("var", [P, NT])
        newt = sb("newt", [P, NT])
        rstd = sb("rstd", [P, NT])
        aT = sb("aT", [P, NG // 2, S])
        tA = sb("tA", [P, S // 32, 32])
        tB = sb("tB", [P, S // 32, 32])
        rsum = sb("rsum", [P, S // 32])
        nmax = sb("nmax", [P, 2, GH * TB])
        mparts = sb("mparts", [P, 2, GH * TB], BF16)
        mT = sb("mT", [2 * GH * TB, P], BF16)
        sw13_sb = sb("sw13_sb", [P, KC, 2 * F])
        sw2_sb = sb("sw2_sb", [P, FC, D])
        sb13_sb = sb("sb13_sb", [P, FC, 2])
        gw_sb = sb("gw_sb", [P, KC, E])
        gb_sb = sb("gb_sb", [P, E])

        W13_N, W2_N, B13_N = E * KC * 2 * F, E * FC * D, E * 2 * F
        QK_N, V_N, PR_N, VG_N = NG * GH * S // 2, NT * D, 8 * S, 2 * TB * GH * 32
        PARTS_N = 3 * KC * S // 2
        arena = sb("arena", [P, max(W13_N + W2_N + B13_N, 2 * QK_N + V_N + PR_N + VG_N + 2 * PARTS_N)])
        q_st = arena[:, 0:QK_N].bitcast(BF16).rearrange("p (g h s) -> p g h s", g=NG, h=GH)
        k_st = arena[:, QK_N:2 * QK_N].bitcast(BF16).rearrange("p (g h s) -> p g h s", g=NG, h=GH)
        o = 2 * QK_N
        k_ones = arena[96:128, QK_N:2 * QK_N]
        v_all = arena[:, o:o + V_N].rearrange("p (j g d h) -> p j g d h", j=NT, g=NG, h=GH)
        o += V_N
        probs = arena[:, o:o + PR_N].rearrange("p (r s) -> p r s", r=8)
        o += PR_N
        v_grp = arena[:, o:o + VG_N].rearrange("p (r j h d) -> p r j h d", r=2, j=TB, h=GH)
        o += VG_N
        odd_parts = [arena[:, o + n * PARTS_N:o + (n + 1) * PARTS_N] for n in range(2)]
        w13_sb = arena[:, 0:W13_N].rearrange("p (e k f) -> p e k f", e=E, k=KC)
        w2_sb = arena[:, W13_N:W13_N + W2_N].rearrange("p (e c d) -> p e c d", e=E, c=FC)
        b13_sb = arena[:, W13_N + W2_N:W13_N + W2_N + B13_N].rearrange("p (e f) -> p e f", e=E)

        PB = [("cst", 2 * TB * D), ("xT", KC * S), ("cT", KC * S), ("kf", KC * S), ("qf", KC * S),
              ("qparts", PARTS_N), ("kparts", PARTS_N)]
        FB = [("x2T", KC * T), ("sa", 2 * S), ("sz", 2 * S), ("shT", FC * S),
              ("xb", 2 * D), ("eo", 2 * D), ("xbT", 2 * D)]
        EB = [("eh", 2 * F), ("ehT", 2 * FC * P)]
        assert sum(n for _, n in EB) <= KC * SB * S
        work = sb("work", [P, max(sum(n for _, n in PB), sum(n for _, n in FB))])

        def carve(parts):
            at, got = 0, {}
            for name, n in parts:
                got[name] = work[:, at:at + n]
                at += n
            return got

        pb, fb, eb = carve(PB), carve(FB), carve(EB)
        cst = pb["cst"].rearrange("p (r j d) -> p r j d", r=2, j=TB)
        xT = pb["xT"].rearrange("p (k s) -> p k s", k=KC)
        cT = pb["cT"].rearrange("p (k s) -> p k s", k=KC)
        kf = pb["kf"].rearrange("p (k s) -> p k s", k=KC)
        qf = pb["qf"].rearrange("p (k s) -> p k s", k=KC)
        qparts = [m.bitcast(BF16).rearrange("p (t k s) -> p t k s", t=3, k=KC) for m in (pb["qparts"], odd_parts[0])]
        kparts = [m.bitcast(BF16).rearrange("p (t k s) -> p t k s", t=3, k=KC) for m in (pb["kparts"], odd_parts[1])]
        x2T = fb["x2T"].rearrange("p (b k s) -> p b k s", b=B, k=KC)
        sh_a = fb["sa"].rearrange("p (r s) -> p r s", r=2)
        sh_z = fb["sz"].rearrange("p (r s) -> p r s", r=2)
        sh_hT = fb["shT"].rearrange("p (c s) -> p c s", c=FC)
        xb = fb["xb"].rearrange("p (r d) -> p r d", r=2)
        xbT = fb["xbT"].rearrange("p (r k s) -> p r k s", r=2, k=KC)
        e_a, e_c = fb["sa"][:, 0:F], fb["sa"][:, F:2 * F]
        e_z = fb["sz"][:, 0:2 * F].rearrange("p (r f) -> p r f", r=2)
        e_h = eb["eh"].rearrange("p (r f) -> p r f", r=2)
        e_hT = eb["ehT"].rearrange("p (r c s) -> p r c s", r=2, c=FC)
        e_o = fb["eo"].rearrange("p (r d) -> p r d", r=2)
        gath = fb["x2T"][:, 0:4 * TOP_K * D].rearrange("p (r k d) -> p r k d", r=4, k=TOP_K)

        lg = sb("lg", [P, NT, E])
        lsh = sb("lsh", [P, NT, E])
        lex = sb("lex", [P, NT, E])
        sco = sb("sco", [P, NT, E])
        bia = sb("bia", [P, NT, E])
        cand = sb("cand", [P, NT, E])
        oneh = sb("oneh", [P, TOP_K, NT, E])
        rt1 = sb("rt1", [P, NT])
        rt2 = sb("rt2", [P, NT])
        rw = sb("rw", [P, TOP_K, NT])
        selb = sb("selb", [P, NT, E], BF16)
        tri = sb("tri", [P, P], BF16)
        ones_b = sb("ones_b", [P, P], BF16)
        cum = sb("cum", [P, NT + 1, E])
        iota_e = sb("iota_e", [P, E])
        iota_n = sb("iota_n", [P, MAX_BLOCKS])
        iota_c = sb("iota_c", [P, NT])
        iota_r = sb("iota_r", [P, E])
        cnt = sb("cnt", [P, 2, NT, E])
        total = sb("total", [P, E])
        skip = sb("skip", [P, E])
        rowf = sb("rowf", [P, MAX_BLOCKS])
        blkrow = sb("blkrow", [P, MAX_BLOCKS], I32)
        fill = sb("fill", [P, E], I32)
        cmpc = sb("cmpc", [P, E, NT])
        nblk = sb("nblk", [P, E])
        bend = sb("bend", [P, E + 1])
        cmpn = sb("cmpn", [P, MAX_BLOCKS, E])
        blkf = sb("blkf", [P, MAX_BLOCKS])
        blk = sb("blk", [P, MAX_BLOCKS], I32)
        slotf = sb("slotf", [P, TOP_K, NT])
        slot = sb("slot", [P, TOP_K, NT], I32)
        shift = sb("shift", [P, E])
        place = sb("place", [P, TOP_K, NT], I32)
        zrow = sb("zrow", [P, D])

        ps = stack.enter_context(nc.psum_tensor("ps", [P, 8, 512], F32))
        stack.enter_context(nc.allow_non_contiguous_dma(reason="a few bias vectors, one value per partition"))

        s_const = sem("s_const")
        s_wq = sem("s_wq")
        s_bq = sem("s_bq")
        s_wo = sem("s_wo")
        s_bo = sem("s_bo")
        s_xbo = sem("s_xbo")
        s_sw = sem("s_sw")
        s_zero = sem("s_zero")
        s_ew = sem("s_ew")
        s_x = [sem(f"s_x{b}") for b in range(B)]
        s_c = [sem(f"s_c{r}") for r in range(2)]
        s_dve = sem("s_dve")
        s_act = sem("s_act")
        s_pool = sem("s_pool")
        s_ln = sem("s_ln")
        s_var = sem("s_var")
        s_xn = sem("s_xn")
        s_cTp = sem("s_cTp")
        s_xTp = sem("s_xTp")
        s_cT = sem("s_cT")
        s_xT = sem("s_xT")
        s_kp = sem("s_kp")
        s_qp = sem("s_qp")
        s_kf = sem("s_kf")
        s_qf = sem("s_qf")
        s_vp = sem("s_vp")
        s_v = sem("s_v")
        s_kc = sem("s_kc")
        s_kr = sem("s_kr")
        s_ks = sem("s_ks")
        s_qs = sem("s_qs")
        s_kd = [sem(f"s_kd{r}") for r in range(2)]
        s_qd = [sem(f"s_qd{r}") for r in range(2)]
        s_st = [sem(f"s_st{g}") for g in range(NG)]
        s_mrow = [sem(f"s_mrow{g}") for g in range(NG)]
        s_ones = sem("s_ones")
        s_rp = sem("s_rp")
        s_rc = sem("s_rc")
        s_mp = sem("s_mp")
        s_rsum = sem("s_rsum")
        s_scale = sem("s_scale")
        s_s2 = sem("s_s2")
        s_exp = sem("s_exp")
        s_pv = sem("s_pv")
        s_pvc = sem("s_pvc")
        s_vg = sem("s_vg")
        s_norm = sem("s_norm")
        s_lastp = sem("s_lastp")
        s_lastx = sem("s_lastx")
        s_gTp = sem("s_gTp")
        s_gT = sem("s_gT")
        s_gp = sem("s_gp")
        s_gl = sem("s_gl")
        s_lsh = sem("s_lsh")
        s_lex = sem("s_lex")
        s_sel = sem("s_sel")
        s_cnt = sem("s_cnt")
        s_cntc = sem("s_cntc")
        s_slots = sem("s_slots")
        s_fill = sem("s_fill")
        s_blk = sem("s_blk")
        s_place = sem("s_place")
        s_scat = sem("s_scat")
        s_up1 = sem("s_up1")
        s_a1 = sem("s_a1")
        s_z1 = sem("s_z1")
        s_h1 = sem("s_h1")
        s_dn1 = sem("s_dn1")
        s_y1 = sem("s_y1")
        s_xb = [sem(f"s_xb{r}") for r in range(2)]
        s_xbp = sem("s_xbp")
        s_xbe = sem("s_xbe")
        s_upa = sem("s_upa")
        s_up = sem("s_up")
        s_upc = sem("s_upc")
        s_z = sem("s_z")
        s_h = sem("s_h")
        s_hp = sem("s_hp")
        s_hT = sem("s_hT")
        s_o = sem("s_o")
        s_oe = sem("s_oe")
        s_os = [sem(f"s_os{r}") for r in range(2)]
        s_g = [sem(f"s_g{r}") for r in range(4)]
        s_fin = sem("s_fin")
        s_out = sem("s_out")

        def loop(eng, lo, hi, body):
            with eng.Fori(lo, hi) as i:
                body(i)

        def pairs(eng, n, body):
            with eng.Fori(0, n // 2) as r:
                for par in range(2):
                    body(2 * r + par, par, r)

        SR = 7 * DK
        PRE = 2 * GH * TB + 1
        PER = NG * (GH * TB + 1)
        RING, BR, BS2, BPV = 4, 0, 4, 7
        S2_BANK = [n % 3 for n in range(GH * TB - 1)] + [1]

        def s2_before(n):
            m = n - 1
            while S2_BANK[m % (GH * TB)] != S2_BANK[n]:
                m -= 1
            return m

        def ring_base(b):
            return PRE + PER + (PER + TB) * (b - 1) if not isinstance(b, int) or b else PRE

        def step_units(g, with_wo, with_s1, with_m):
            units = []
            for t in range(TB):
                s1 = [("s1", t * TB + c) for c in range(TB)] if with_s1 else []
                m = [("m", 0)] if t == 1 and with_m else []
                units += s1[:1] + m + s1[1:]
                if g == 1 and with_wo:
                    units.append(("wo", t))
            return units

        def kinds(b, g):
            first, last = isinstance(b, int) and b == 0, isinstance(b, int) and b == B - 1
            return not first, not (last and g >= NG - 2), not (last and g == NG - 1)

        def batch_units(b):
            at, offs = 0, []
            for g in range(NG):
                offs.append(at)
                at += len(step_units(g, *kinds(b, g)))
            return offs, at

        def bank_of(b, k):
            return (ring_base(b if isinstance(b, int) and b == 0 else 1) + k) % RING

        RING_END = ring_base(B - 1) + batch_units(B - 1)[1]

        block = stack.enter_context(nc.Block())

        @block.sync
        def _(sp):
            sp.dma_start(bq_sb[:, :], bq.rearrange("(k p) -> p k", p=P)).then_inc(s_bq, 16)

            def load(b, r, n):
                if n:
                    sp.wait_ge(s_cTp, 2 * (b - 1))
                sp.dma_start(cst[:, r, :, :], ctx_v[b]).then_inc(s_c[r], 16)

            for r in range(2):
                sp.sem_inc(s_os[r], 16)
            for b in range(B):
                sp.dma_start(xres[:, TB * b:TB * b + TB, :], x_v[b]).then_inc(s_x[b], 16)
                if b < 2:
                    load(b, b, 0)
                if b == 0:
                    sp.dma_start(wq_sb[:, :, :], wq.rearrange("(k p) e -> p k e", p=P)).then_inc(s_wq, 16)
            sp.wait_ge(s_const, 2)
            for g in range(NG):
                for j in range(GH):
                    h = GH * g + j
                    row = 32 * j + DK * (g % 2)
                    sp.dma_start(wo_sb[row:row + DK, g // 2, :], wo[DK * h:DK * h + DK, :]).then_inc(s_wo, 16)
            sp.dma_start(bo_sb[:, :], bo.rearrange("(a d) -> a d", a=1).to_broadcast([P, D])).then_inc(s_bo, 16)
            sp.dma_start(sw13_sb[:, :, 0:F], sw1.rearrange("(k p) f -> p k f", p=P)).then_inc(s_sw, 16)
            sp.dma_start(sw13_sb[:, :, F:2 * F], sw3.rearrange("(k p) f -> p k f", p=P)).then_inc(s_sw, 16)
            sp.dma_start(sw2_sb[:, 0:FC - 1, :], sw2[0:(FC - 1) * P, :].rearrange("(c p) d -> p c d", p=P)).then_inc(s_sw, 16)
            sp.dma_start(sw2_sb[0:FL, FC - 1, :], sw2[(FC - 1) * P:F, :]).then_inc(s_sw, 16)
            sp.dma_start(sw2_sb[FL:FL + 1, FC - 1, :], sb2.rearrange("(a d) -> a d", a=1)).then_inc(s_sw, 16)
            for n, bias in enumerate((sb1, sb3)):
                sp.dma_start(sb13_sb[:, 0:FC - 1, n], bias[0:(FC - 1) * P].rearrange("(c p) -> p c", p=P)).then_inc(s_sw, 16)
                sp.dma_start(sb13_sb[0:FL, FC - 1, n:n + 1], bias[(FC - 1) * P:F].rearrange("(p a) -> p a", a=1)).then_inc(s_sw, 16)
            sp.dma_start(gw_sb[:, :, :], gate_wt.rearrange("(k p) e -> p k e", p=P)).then_inc(s_sw, 16)
            sp.dma_start(gb_sb[:, :], gate_b.rearrange("(a e) -> a e", a=1).to_broadcast([P, E])).then_inc(s_sw, 16)
            sp.dma_start(xs_dram[SPARE:SPARE + SPARE_BLOCKS * P, :].rearrange("(n p) d -> p n d", p=P),
                         zrow[:, :].rearrange("p (a d) -> p a d", a=1).to_broadcast([P, SPARE_BLOCKS, D])).then_inc(s_zero, 16)

            def parts_out(b):
                r = b % 2
                for ready, parts, dram, s in ((s_ks, kparts[r], k_dram, s_kd[r]), (s_qs, qparts[r], q_dram, s_qd[r])):
                    sp.wait_ge(ready, b + 2)
                    sp.dma_start(dram[b].rearrange("(n g) d (h s) -> (g d h) n s", g=NG // KC, s=S),
                                 parts.rearrange("p t k s -> p (t k) s")).then_inc(s, 16)

            def stacks(b, g):
                qd, kd = (dram[b].rearrange("(t g) d s -> g t d s", g=NG)[g] for dram in (q_dram, k_dram))
                for part in range(2):
                    rows = slice(3 * DK * part, 3 * DK * (part + 1))
                    sp.dma_start(q_st[rows, g, :, :].rearrange("p h s -> p (h s)"),
                                 qd[part:part + 1].to_broadcast([3, DK, GH * S])).then_inc(s_st[g], 16)
                    sp.dma_start(k_st[rows, g, :, :].rearrange("p h s -> p (h s)"), kd).then_inc(s_st[g], 16)
                rows = slice(6 * DK, 7 * DK)
                sp.dma_start(q_st[rows, g, :, :].rearrange("p h s -> p (h s)"), qd[2]).then_inc(s_st[g], 16)
                sp.dma_start(k_st[rows, g, :, :].rearrange("p h s -> p (h s)"), kd[0]).then_inc(s_st[g], 16)

            parts_out(0)
            load(2, 0, 1)
            load(3, 1, 1)
            sp.wait_ge(s_ones, 3)
            sp.wait_ge(s_kd[0], 16)
            sp.wait_ge(s_qd[0], 16)
            for g in range(NG):
                stacks(0, g)
                if g == 1:
                    parts_out(1)
            for b in range(2, B):
                parts_out(b)
            for r in range(2):
                sp.wait_ge(s_kd[r], 16 * (B // 2))
                sp.wait_ge(s_qd[r], 16 * (B // 2))

            def mrow(b, g, unit):
                sp.wait_ge(s_rc, RING + unit + 1)
                for part in range(2):
                    sp.dma_start(q_st[SR + part:SR + part + 1, g, :, :],
                                 mT[GH * TB * part:GH * TB * (part + 1), :]).then_inc(s_mrow[g], 16)

            mrow(0, 0, GH * TB)

            def steps(b):
                last = isinstance(b, int) and b == B - 1
                offs, _ = batch_units(b)
                for g in range(NG):
                    i = NG * b + g
                    if not (last and g == NG - 1):
                        mrow(b if g < NG - 1 else b + 1, (g + 1) % NG,
                             ring_base(b) + offs[g] + step_units(g, *kinds(b, g)).index(("m", 0)))
                    if not last:
                        sp.wait_ge(s_s2, GH * TB * (i + 1))
                        stacks(b + 1, g)

            steps(0)
            loop(sp, 1, B - 1, steps)
            steps(B - 1)

            sp.wait_ge(s_pv, 2 + TB * NG * B)
            sp.wait_ge(s_vg, NG * B)
            for e in range(E):
                sp.dma_start(w13_sb[:, e, :, 0:F], w1[e].rearrange("(k p) f -> p k f", p=P)).then_inc(s_ew, 16)
                sp.dma_start(w13_sb[:, e, :, F:2 * F], w3[e].rearrange("(k p) f -> p k f", p=P)).then_inc(s_ew, 16)
                sp.dma_start(w2_sb[:, e, 0:FC - 1, :],
                             w2[e, 0:(FC - 1) * P, :].rearrange("(c p) d -> p c d", p=P)).then_inc(s_ew, 16)
            sp.dma_start(w2_sb[0:FL, :, FC - 1, :], w2[:, (FC - 1) * P:F, :].rearrange("e p d -> p e d")).then_inc(s_ew, 16)
            sp.dma_start(w2_sb[FL:FL + 1, :, FC - 1, :], b2.rearrange("(a e) d -> a e d", a=1)).then_inc(s_ew, 16)
            for n, bias in enumerate((b1, b3)):
                sp.dma_start(b13_sb[:, :, n * F:n * F + F],
                             bias.rearrange("(a e) f -> a e f", a=1).to_broadcast([P, E, F])).then_inc(s_ew, 16)

            sp.wait_ge(s_fill, 1)
            for e in range(E):
                behind = sp.value_load(fill[0:1, e:e + 1], min_val=0, max_val=SPARE - P)
                sp.dma_start(xs_dram[bass.ds(behind, P), :], zrow[:, :]).then_inc(s_zero, 16)

            def first_slot(n):
                return sp.value_load(blkrow[0:1, bass.ds(n, 1)], min_val=0, max_val=SPARE + (SPARE_BLOCKS - 1) * P)

            def rows_in(n, par, at):
                sp.wait_ge(s_xbp, n + 1)
                sp.dma_start(xb[:, par, :], xs_dram[bass.ds(at, P), :]).then_inc(s_xb[par], 16)

            def results_out(n, par):
                sp.wait_ge(s_oe, n + 3)
                sp.dma_start(os_dram.rearrange("(n p) d -> n p d", p=P)[n], e_o[:, par, :]).then_inc(s_os[par], 16)

            AHEAD = 4
            sp.wait_ge(s_blk, 1)
            first = [first_slot(n) for n in range(2)]
            sp.wait_ge(s_zero, 16 + 16 * E)
            sp.wait_ge(s_scat, 16 * TOP_K * NT)
            for n in range(AHEAD):
                rows_in(n, n % 2, first[n] if n < 2 else first_slot(n))

            def blocks(n, par, r):
                rows_in(n + AHEAD, par, first_slot(n + AHEAD))
                results_out(n, par)

            NP = (MAX_BLOCKS - AHEAD) // 2 * 2
            pairs(sp, NP, blocks)
            for n in range(NP, MAX_BLOCKS):
                if n + AHEAD < MAX_BLOCKS:
                    rows_in(n + AHEAD, n % 2, first_slot(n + AHEAD))
                results_out(n, n % 2)

            for j in range(NT):
                sp.wait_ge(s_fin, j + 1)
                sp.dma_start(out_v[j], xres[:, j, :]).then_inc(s_out, 16)
            sp.wait_ge(s_out, 16 * NT)

        @block.gpsimd
        def _(pool):
            chain = [0]

            def link(ins):
                chain[0] += 1
                ins.then_inc(s_pool, 1)
                pool.wait_ge(s_pool, chain[0])

            pool.memset(sw2_sb[:, FC - 1, :], 1.0).then_inc(s_const, 1)
            pool.memset(zrow[:, :], 0.0).then_inc(s_const, 1)
            link(pool.memset(ident[:, :], 0.0))
            link(pool.memset(ident_b[:, :], 0.0))
            link(pool.memset(tri[:, :], 1.0))
            for m in (ident, ident_b):
                pool.affine_select(out=m[:, :], in_=m[:, :], compare_op=ALU.not_equal, fill=1.0, base=0,
                                   pattern=[[-1, P]], channel_multiplier=1).then_inc(s_const, 1)
            pool.affine_select(out=tri[:, :], in_=tri[:, :], compare_op=ALU.is_gt, fill=0.0, base=0,
                               pattern=[[1, P]], channel_multiplier=-1).then_inc(s_const, 1)
            pool.memset(ones_b[:, :], 1.0).then_inc(s_const, 1)
            pool.iota(iota_e[:, :], [[1, E]], base=-E, channel_multiplier=0,
                      allow_small_or_imprecise_dtypes=True).then_inc(s_const, 1)
            pool.iota(iota_n[:, :], [[1, MAX_BLOCKS]], base=0, channel_multiplier=0,
                      allow_small_or_imprecise_dtypes=True).then_inc(s_const, 1)
            pool.iota(iota_c[:, :], [[P, NT]], base=0, channel_multiplier=0,
                      allow_small_or_imprecise_dtypes=True).then_inc(s_const, 1)
            pool.iota(iota_r[:, :], [[REG, E]], base=0, channel_multiplier=0,
                      allow_small_or_imprecise_dtypes=True).then_inc(s_const, 1)
            pool.sem_inc(s_ks, 1)

            def split(b):
                pool.wait_ge(s_kc, 2 * b + 1)
                pool.wait_ge(s_vp, 2 * b + 4)
                pool.tensor_tensor(kf[:, :, :], kf[:, :, :], kparts[b % 2][:, 0, :, :], ALU.subtract).then_inc(s_kr, 1)
                pool.wait_ge(s_kc, 2 * b + 2)
                pool.tensor_tensor(kparts[b % 2][:, 2, :, :], kf[:, :, :], kparts[b % 2][:, 1, :, :],
                                   ALU.subtract).then_inc(s_ks, 1)

            for b in range(B):
                split(b)

            def v_group(b, g):
                i = NG * b + g
                if i >= 2:
                    pool.wait_ge(s_pv, TB * (i - 1) + 2)
                pool.tensor_copy(v_grp[:, g % 2, :, :, 0:DK],
                                 v_all[:, TB * b:TB * b + TB, g, :, :].rearrange("p j d h -> p j h d")).then_inc(s_vg, 1)

            pool.wait_ge(s_v, 2 + 2 * B)
            for i in range(2):
                v_group(i // NG, i % NG)
            pool.wait_ge(s_bo, 16)
            pool.wait_ge(s_xn, B)
            for b in range(B):
                pool.tensor_tensor(xres[:, TB * b:TB * b + TB, :], xres[:, TB * b:TB * b + TB, :],
                                   bo_sb[:, :].rearrange("p (a d) -> p a d", a=1).to_broadcast([P, TB, D]),
                                   ALU.add).then_inc(s_xbo, 1)

            def scale(i):
                g = i % NG
                pool.wait_ge(s_rsum, i + 1)
                if g % 2 == 0 and i >= 2:
                    pool.wait_ge(s_norm, i // 2)
                pool.tensor_tensor(tB[:, :, DK * (g % 2):DK * (g % 2) + DK], tA[:, :, 0:DK],
                                   rsum[:, :].rearrange("p (a b) -> p a b", b=1).to_broadcast([P, S // 32, DK]),
                                   ALU.mult).then_inc(s_scale, 1)

            for i in range(2, NG * B):
                v_group(i // NG, i % NG)
                scale(i - 2)
            for i in range(NG * B - 2, NG * B):
                scale(i)

            for part, tiles in enumerate(((0, NT - TB), (NT - TB, NT))):
                pool.wait_ge(s_slots, part + 1)
                for j in range(*tiles):
                    for k in range(TOP_K):
                        pool.indirect_dma_start(
                            out=xs_dram, out_offset=bass.IndirectOffsetOnAxis(ap=slot[:, k, j:j + 1], axis=0),
                            in_=xn[:, j, :], in_offset=None).then_inc(s_scat, 16)
            pool.wait_ge(s_place, 1)
            pool.wait_ge(s_os[0], 16 * ((MAX_BLOCKS + 1) // 2) + 16)
            pool.wait_ge(s_os[1], 16 * (MAX_BLOCKS // 2) + 16)
            for j in range(NT):
                if j >= 4:
                    pool.wait_ge(s_fin, j - 3)
                for k in range(TOP_K):
                    pool.indirect_dma_start(
                        out=gath[:, j % 4, k, :], out_offset=None, in_=os_dram,
                        in_offset=bass.IndirectOffsetOnAxis(ap=place[:, k, j:j + 1], axis=0)).then_inc(s_g[j % 4], 16)

        @block.scalar
        def _(act):
            for s, n in ((s_cT, 2), (s_xT, 2), (s_kf, 2), (s_qf, 2), (s_exp, 4), (s_gT, 2),
                         (s_xbe, 1), (s_h, 2), (s_hT, 1)):
                act.sem_inc(s, n)
            act.wait_ge(s_bq, 16)
            act.activation(bqs_sb[:, :], bq_sb[:, :], ACT.Copy, scale=SCALE).then_inc(s_act, 1)

            def ctx_evac(b):
                act.wait_ge(s_kp, 2 * b + 2)
                for c in range(KC):
                    act.wait_ge(s_cTp, 2 * b + c + 1)
                    act.activation(cT[:, c, :], ps[:, 2 + c, :], ACT.Copy).then_inc(s_cT, 1)

            def tokens_evac(b):
                act.wait_ge(s_qp, 2 * b + 2)
                for c in range(KC):
                    act.wait_ge(s_xTp, 2 * b + c + 1)
                    act.activation(xT[:, c, :], ps[:, c, :], ACT.Copy).then_inc(s_xT, 1)

            def k_evac(b):
                act.wait_ge(s_vp, 2 * b + 2)
                act.wait_ge(s_ks, b + 1)
                for c in range(KC):
                    act.wait_ge(s_kp, 2 * b + c + 3)
                    act.activation(kf[:, c, :], ps[:, 6 + c, :], ACT.Identity, bias=bq_sb[:, c:c + 1]).then_inc(s_kf, 1)

            def q_evac(b):
                act.wait_ge(s_qs, b + 1)
                for c in range(KC):
                    act.wait_ge(s_qp, 2 * b + c + 3)
                    act.activation(qf[:, c, :], ps[:, 4 + c, :], ACT.Identity, bias=bqs_sb[:, c:c + 1],
                                   scale=SCALE).then_inc(s_qf, 1)

            def evac(b):
                tokens_evac(b)
                ctx_evac(b)
                k_evac(b)
                q_evac(b)

            act.wait_ge(s_act, 1)
            ctx_evac(0)
            k_evac(0)
            tokens_evac(0)
            q_evac(0)
            loop(act, 1, B, evac)

            def exps(i):
                for t in range(TB):
                    act.wait_ge(s_pv, TB * i + t + 1)
                    for j in range(GH):
                        n = GH * t + j
                        act.wait_ge(s_s2, GH * TB * i + n + 1)
                        act.activation(probs[:, GH * (t % 2) + j, :], ps[:, BS2 + S2_BANK[n], :],
                                       ACT.Exp).then_inc(s_exp, 1)

            act.wait_ge(s_v, 2 + 2 * B)
            for i in range(NG):
                exps(i)

            def batch_exps(b):
                for g in range(NG):
                    exps(NG * b + g)

            loop(act, 1, B, batch_exps)

            def x2T_evac(b, bank):
                for c in range(KC):
                    act.wait_ge(s_gTp, 2 * b + c + 1)
                    act.activation(x2T[:, b, c, :], ps[:, bank + c, :], ACT.Copy).then_inc(s_gT, 1)

            def exp_logits(part, lo, hi):
                act.wait_ge(s_lsh, part + 1)
                act.activation(lex[:, lo:hi, :], lsh[:, lo:hi, :], ACT.Exp).then_inc(s_lex, 1)

            def sh_first(b, c):
                rows = P if c < FC - 1 else FL
                act.wait_ge(s_up1, FC * b + c + 1)
                act.activation(sh_a[0:rows, (FC * b + c) % 2, :], ps[0:rows, 2 * ((FC * b + c) % 2), :], ACT.Identity,
                               bias=sb13_sb[0:rows, c, 0:1]).then_inc(s_a1, 1)

            def sh_silu(b, c):
                rows = P if c < FC - 1 else FL
                act.wait_ge(s_z1, FC * b + c + 1)
                if c == 0:
                    act.wait_ge(s_dn1, 4 * b + 4)
                act.activation(sh_hT[0:rows, c, :], sh_z[0:rows, (FC * b + c) % 2, :], ACT.Silu).then_inc(s_h1, 1)

            def shared(b):
                sh_first(b, 0)
                sh_first(b, 1)
                sh_silu(b, 0)
                sh_first(b, 2)
                sh_silu(b, 1)
                sh_silu(b, 2)

            exp_logits(0, 0, NT - TB)
            sh_first(0, 0)
            sh_first(0, 1)
            sh_silu(0, 0)
            sh_first(0, 2)
            sh_silu(0, 1)
            x2T_evac(B - 1, 4)
            sh_silu(0, 2)
            exp_logits(1, NT - TB, NT)
            for b in range(1, SB):
                shared(b)
            for c in range(EARLY):
                sh_first(SB, c)
            for c in range(EARLY):
                sh_silu(SB, c)

            def x_evac(n, par):
                act.wait_ge(s_xbp, n + 3)
                act.wait_ge(s_up, n + 1)
                act.activation(xbT[:, par, :, :], ps[:, 0, 0:D].rearrange("p (k s) -> p k s", k=KC),
                               ACT.Copy).then_inc(s_xbe, 1)

            def h_make(n, par):
                act.wait_ge(s_z, n + 1)
                act.wait_ge(s_hp, n + 1)
                act.activation(e_h[:, par, :], e_z[:, par, :], ACT.Silu).then_inc(s_h, 1)

            def h_evac(n, par):
                act.wait_ge(s_hp, n + 3)
                act.wait_ge(s_o, n + 1)
                act.activation(e_hT[:, par, 0:FC - 1, :],
                               ps[:, 5, 0:(FC - 1) * P].rearrange("p (c s) -> p c s", c=FC - 1), ACT.Copy)
                act.activation(e_hT[0:FL, par, FC - 1, :], ps[0:FL, 5, (FC - 1) * P:FC * P], ACT.Copy).then_inc(s_hT, 1)

            x_evac(0, 0)
            x_evac(1, 1)
            h_make(0, 0)

            def blocks(n, par, r):
                h_evac(n, par)
                x_evac(n + 2, par)
                h_make(n + 1, 1 - par)

            NP = (MAX_BLOCKS - 2) // 2 * 2
            pairs(act, NP, blocks)
            for n in range(NP, MAX_BLOCKS):
                h_evac(n, n % 2)
                if n + 2 < MAX_BLOCKS:
                    x_evac(n + 2, n % 2)
                if n + 1 < MAX_BLOCKS:
                    h_make(n + 1, 1 - n % 2)
            for c in range(EARLY, FC):
                sh_first(SB, c)
                sh_silu(SB, c)
            for b in range(SB + 1, B):
                shared(b)

        @block.vector
        def _(dve):
            for s, n in ((s_v, 2), (s_qs, 1), (s_rc, RING), (s_pvc, 1), (s_y1, 1), (s_upc, 2), (s_oe, 2)):
                dve.sem_inc(s, n)
            N_RS = 11
            N_LN = 2 * TB + N_RS
            LN_X1 = 2 * NT + 2 * N_RS

            def norm_stats(at, tile, n=TB, first=0):
                for j in range(first, n):
                    dve.bn_stats(stats[:, at + j, :], xres[:, tile + j, :]).then_inc(s_ln, 1)

            def norm_means(at=0, n=TB):
                for j in range(at, at + n):
                    dve.bn_aggr(mv[:, j, :], stats[:, j, :]).then_inc(s_ln, 1)

            def norm_var(done, at=0, n=TB):
                dve.wait_ge(s_ln, done)
                dve.tensor_scalar_add(var[:, at:at + n], mv[:, at:at + n, 1], EPS).then_inc(s_var, 1)

            def rstd_step(r, done, variances, at=0, n=TB):
                js = slice(at, at + n)
                if r == 0:
                    dve.wait_ge(s_var, variances)
                    ins = dve.tensor_single_scalar(newt[:, js].bitcast(I32), var[:, js].bitcast(I32), 1,
                                                   op=ALU.logical_shift_right)
                else:
                    dve.wait_ge(s_ln, done + r)
                    if r == 1:
                        ins = dve.tensor_scalar(rstd[:, js].bitcast(I32), newt[:, js].bitcast(I32), -1.0,
                                                float(0x5f3759df), ALU.mult, ALU.add)
                    elif r % 3 == 2:
                        ins = dve.scalar_tensor_tensor(newt[:, js], rstd[:, js], -0.5, rstd[:, js], ALU.mult, ALU.mult)
                    elif r % 3 == 0:
                        ins = dve.tensor_tensor(newt[:, js], newt[:, js], var[:, js], ALU.mult)
                    else:
                        ins = dve.scalar_tensor_tensor(rstd[:, js], newt[:, js], 1.5, rstd[:, js], ALU.add, ALU.mult)
                ins.then_inc(s_ln, 1)

            def norm_rstd(done, variances, at=0, n=TB):
                for r in range(N_RS):
                    rstd_step(r, done, variances, at, n)

            def norm_apply(done, at, tile):
                dve.wait_ge(s_ln, done)
                for j in range(TB):
                    ins = dve.tensor_scalar(xn[:, tile + j, :], xres[:, tile + j, :], mv[:, at + j, 0:1],
                                            rstd[:, at + j:at + j + 1], ALU.subtract, ALU.mult)
                ins.then_inc(s_xn, 1)

            dve.wait_ge(s_x[0], 16)
            norm_stats(0, 0)
            dve.wait_ge(s_ln, TB)
            norm_means()
            norm_var(2 * TB)
            norm_rstd(2 * TB, 1)
            norm_apply(N_LN, 0, 0)
            for b in range(1, B):
                dve.wait_ge(s_x[b], 16)
                norm_stats(TB * b, TB * b)
            dve.wait_ge(s_ln, N_LN + NT - TB)
            norm_means(TB, NT - TB)
            norm_var(N_LN + 2 * (NT - TB), TB, NT - TB)
            dve.memset(k_ones, BF16_PAIR_OF_ONES).then_inc(s_ones, 1)
            for r in range(2):
                dve.memset(v_grp[:, r, :, :, DK:32], 1.0).then_inc(s_ones, 1)
            norm_rstd(N_LN + 2 * (NT - TB), 2, TB, NT - TB)
            norm_apply(LN_X1, TB, TB)
            at = [0]

            def project(b):
                qp, kp = qparts[b % 2], kparts[b % 2]
                dve.wait_ge(s_kf, 2 * b + 4)
                if b >= 2:
                    dve.wait_ge(s_kd[b % 2], 16 * (b // 2))
                dve.tensor_copy(kp[:, 0, :, :], kf[:, :, :]).then_inc(s_kc, 1)
                for half in range(2):
                    dve.wait_ge(s_vp, 2 * b + half + 3)
                    dve.tensor_copy(v_all[:, bass.ds(TB * b + 2 * half, 2), :, :, :].rearrange("p j g d h -> p (j g d h)"),
                                    ps[:, 2 + half, :]).then_inc(s_v, 1)
                c0 = 3 * b
                dve.wait_ge(s_qf, 2 * b + 4)
                if b >= 2:
                    dve.wait_ge(s_qd[b % 2], 16 * (b // 2))
                dve.tensor_copy(qp[:, 0, :, :], qf[:, :, :]).then_inc(s_dve, 1)
                dve.wait_ge(s_dve, c0 + 1)
                dve.tensor_tensor(qf[:, :, :], qf[:, :, :], qp[:, 0, :, :], ALU.subtract).then_inc(s_dve, 1)
                dve.wait_ge(s_kr, b + 1)
                dve.tensor_copy(kp[:, 1, :, :], kf[:, :, :]).then_inc(s_kc, 1)
                dve.wait_ge(s_dve, c0 + 2)
                dve.tensor_copy(qp[:, 1, :, :], qf[:, :, :]).then_inc(s_dve, 1)
                dve.wait_ge(s_dve, c0 + 3)
                dve.tensor_tensor(qp[:, 2, :, :], qf[:, :, :], qp[:, 1, :, :], ALU.subtract).then_inc(s_qs, 1)

            project(0)
            for b in range(2, B):
                norm_apply(LN_X1, TB * b, TB * b)
            for b in range(1, B):
                project(b)
            at[0] += 3 * B

            A0 = at[0]

            def scores_tile(n, bank, u, par):
                dve.wait_ge(s_rp, n + 1)
                dve.tensor_reduce(nmax[:, par, u:u + 1], ps[:, BR + bank, :], AX_X, ALU.max, negate=True).then_inc(s_rc, 1)

            def max_first(par, units_done):
                dve.wait_ge(s_rc, RING + units_done)
                dve.tensor_copy(mparts[:, 0, :], nmax[:, par, :]).then_inc(s_dve, 1)

            def max_second(par, c0):
                dve.wait_ge(s_dve, c0 + 1)
                dve.tensor_tensor(mparts[:, 1, :], nmax[:, par, :], mparts[:, 0, :], ALU.subtract).then_inc(s_mp, 1)

            def max_rows(n, bank):
                dve.wait_ge(s_rp, n + 1)
                dve.tensor_copy(mT[:, :], ps[0:2 * GH * TB, BR + bank, 0:P // 2].bitcast(BF16)).then_inc(s_rc, 1)

            def outputs_copy(i):
                dve.wait_ge(s_pv, 2 + TB * i + TB)
                if not (isinstance(i, int) and i == 0):
                    dve.wait_ge(s_scale, i)
                dve.transpose(tA[:, :, :].rearrange("p a b -> p (a b)"), ps[:, BPV, :]).then_inc(s_pvc, 1)

            def outputs_rsum(i):
                dve.wait_ge(s_pvc, i + 2)
                dve.reciprocal(rsum[:, :], tA[:, :, DK]).then_inc(s_rsum, 1)

            def outputs_back(i, g):
                if g % 2:
                    dve.wait_ge(s_scale, i + 1)
                    dve.transpose(aT[:, g // 2, :], tB[:, :, :].rearrange("p a b -> p (a b)")).then_inc(s_norm, 1)

            def normalise(i, g):
                outputs_copy(i)
                outputs_rsum(i)
                outputs_back(i, g)

            def x_one(n, bank, tile, k):
                dve.wait_ge(s_rp, n + 1)
                dve.tensor_tensor(xres[:, tile, :], ps[:, BR + bank, 0:D], xres[:, tile, :], ALU.add).then_inc(s_rc, 1)

            for n in range(2):
                for u in range(GH * TB):
                    k = n * (GH * TB + 1) + u
                    scores_tile(k, k % RING, u, n)
                if n == 0:
                    max_first(0, GH * TB)
                    max_second(0, A0)
                    max_rows(GH * TB, (GH * TB) % RING)
            A1 = A0 + 1

            STATS_AT = [0, 3, 6, 7]
            RSTD_AT = [(2, u) for u in range(12, 16)] + [(3, u) for u in range(N_RS - 4)]

            def steps(b):
                offs, total = batch_units(b)
                rb = ring_base(b)
                for g in range(NG):
                    i = NG * b + g
                    with_wo, with_s1, with_m = kinds(b, g)
                    units = step_units(g, with_wo, with_s1, with_m)
                    first_step = isinstance(i, int) and i == 0
                    c0 = A1 + i
                    if not with_s1:
                        if with_m:
                            max_first(1 - g % 2, rb + offs[g])
                            max_second(1 - g % 2, c0)
                        normalise(i - 1, (g - 1) % NG)
                    for k, (kind, u) in enumerate(units):
                        n = rb + offs[g] + k
                        bank = bank_of(b, offs[g] + k)
                        if kind == "s1":
                            if u == 0:
                                dve.wait_ge(s_mp, i + 1)
                                if g == 2 and with_wo:
                                    dve.wait_ge(s_rc, rb + offs[2] + RING)
                            if g == 2 and with_wo and u == 10:
                                dve.wait_ge(s_ln, LN_X1 + N_LN * (b - 1) + TB)
                            scores_tile(n, bank, u, g % 2)
                            if u == 1:
                                max_first(1 - g % 2, rb + offs[g])
                            if u == 2:
                                max_second(1 - g % 2, c0)
                            if u == 4 and not first_step:
                                outputs_copy(i - 1)
                            if u == 5 and not first_step:
                                outputs_rsum(i - 1)
                            if u == 8 and not first_step:
                                outputs_back(i - 1, (g - 1) % NG)
                            if g == 2 and with_wo:
                                if u in STATS_AT:
                                    j = STATS_AT.index(u)
                                    norm_stats(0, TB * (b - 1), j + 1, j)
                                if u == 10:
                                    norm_means()
                                if u == 11:
                                    norm_var(LN_X1 + N_LN * (b - 1) + 2 * TB)
                            if with_wo and (g, u) in RSTD_AT:
                                rstd_step(RSTD_AT.index((g, u)), LN_X1 + N_LN * (b - 1) + 2 * TB, 2 + b)
                            if g == 3 and u == 9 and with_wo:
                                norm_apply(LN_X1 + N_LN * b, 0, TB * (b - 1))
                        elif kind == "m":
                            dve.wait_ge(s_mrow[g], 32 * (b + 1))
                            max_rows(n, bank)
                        else:
                            x_one(n, bank, TB * (b - 1) + u, k)
                    if g == 2 and with_wo and not with_s1:
                        dve.wait_ge(s_rc, rb + offs[2] + RING)
                        norm_stats(0, TB * (b - 1))
                        dve.wait_ge(s_ln, LN_X1 + N_LN * (b - 1) + TB)
                        norm_means()
                        norm_var(LN_X1 + N_LN * (b - 1) + 2 * TB)
                        x2T_copy(0)
                        x2T_copy(1)
                    if g == 3 and with_wo and not with_s1:
                        norm_rstd(LN_X1 + N_LN * (b - 1) + 2 * TB, 2 + b)
                        norm_apply(LN_X1 + N_LN * b, 0, TB * (b - 1))

            def x2T_copy(b):
                for k in range(KC):
                    dve.wait_ge(s_gTp, KC * b + k + 1)
                    dve.tensor_copy(x2T[:, b, k, :], ps[:, k, :]).then_inc(s_gT, 1)

            def logits(lo, hi, bank):
                dve.wait_ge(s_gp, hi)
                dve.tensor_copy(lg[:, TB * lo:TB * hi, :],
                                ps[:, bank, 0:TB * E * (hi - lo)].rearrange("p (j e) -> p j e", e=E)).then_inc(s_gl, 1)

            def sh_product(b, c):
                n = FC * b + c
                rows = P if c < FC - 1 else FL
                dve.wait_ge(s_a1, n + 1)
                if n >= 2:
                    dve.wait_ge(s_h1, n - 1)
                dve.scalar_tensor_tensor(sh_z[0:rows, (FC * b + c) % 2, :], ps[0:rows, 2 * (n % 2) + 1, :],
                                         sb13_sb[0:rows, c, 1:2], sh_a[0:rows, (FC * b + c) % 2, :],
                                         ALU.add, ALU.mult).then_inc(s_z1, 1)

            def sh_add(b, half):
                tile = TB * b + 2 * half
                dve.wait_ge(s_dn1, 4 * b + 2 * half + 6)
                dve.tensor_tensor(xres[:, tile:tile + 2, :],
                                  ps[:, 6 + half, :].rearrange("p (j d) -> p j d", j=2),
                                  xres[:, tile:tile + 2, :], ALU.add).then_inc(s_y1, 1)

            def link(ins):
                c[0] += 1
                ins.then_inc(s_dve, 1)
                dve.wait_ge(s_dve, c[0])

            def over_e(v, n):
                return v.rearrange("p (j a) -> p j a", a=1).to_broadcast([P, n, E])

            def over_j(v, n):
                return v.rearrange("p (a e) -> p a e", a=1).to_broadcast([P, n, E])

            def shift_logits(lo, hi):
                n, js = hi - lo, slice(lo, hi)
                link(dve.reduce_max(rt1[:, js], lg[:, js, :], axis=AX_X))
                dve.tensor_tensor(lsh[:, js, :], lg[:, js, :], over_e(rt1[:, js], n), ALU.subtract).then_inc(s_lsh, 1)

            def choose(part, lo, hi):
                n, js = hi - lo, slice(lo, hi)
                dve.wait_ge(s_lex, part + 1)
                link(dve.reduce_sum(rt1[:, js], lex[:, js, :], axis=AX_X))
                link(dve.reciprocal(rt2[:, js], rt1[:, js]))
                link(dve.tensor_tensor(sco[:, js, :], lex[:, js, :], over_e(rt2[:, js], n), ALU.mult))
                link(dve.tensor_tensor(bia[:, js, :], sco[:, js, :], over_j(gb_sb[:, :], n), ALU.add))
                for k in range(TOP_K):
                    link(dve.reduce_max(rt1[:, js], bia[:, js, :], axis=AX_X))
                    link(dve.tensor_tensor(cand[:, js, :], bia[:, js, :], over_e(rt1[:, js], n), ALU.is_equal))
                    link(dve.tensor_tensor(cand[:, js, :], cand[:, js, :], over_j(iota_e[:, :], n), ALU.mult))
                    link(dve.tensor_reduce(rt2[:, js], cand[:, js, :], AX_X, ALU.min))
                    link(dve.tensor_tensor(oneh[:, k, js, :], over_j(iota_e[:, :], n), over_e(rt2[:, js], n), ALU.is_equal))
                    if k + 1 < TOP_K:
                        link(dve.scalar_tensor_tensor(bia[:, js, :], oneh[:, k, js, :], -3.0e38, bia[:, js, :],
                                                      ALU.mult, ALU.add))
                dve.tensor_tensor(selb[:, js, :], oneh[:, 0, js, :], oneh[:, 1, js, :], ALU.add).then_inc(s_sel, 1)

            def weights(lo, hi):
                js = slice(lo, hi)
                for k in range(TOP_K):
                    link(dve.tensor_tensor(cand[:, js, :], sco[:, js, :], oneh[:, k, js, :], ALU.mult))
                    link(dve.reduce_sum(rw[:, k, js], cand[:, js, :], axis=AX_X))

            def places():
                link(dve.scalar_tensor_tensor(shift[:, :], bend[:, 0:E], float(P), iota_r[:, :], ALU.mult, ALU.subtract))
                link(dve.tensor_tensor(cand[:, :, :], cnt[:, 0, :, :], cum[:, 0:NT, :], ALU.add))
                link(dve.tensor_tensor(cand[:, :, :], cand[:, :, :], over_j(shift[:, :], NT), ALU.add))
                for k in range(TOP_K):
                    link(dve.tensor_tensor(lsh[:, :, :], cand[:, :, :], oneh[:, k, :, :], ALU.mult))
                    link(dve.reduce_sum(slotf[:, k, :], lsh[:, :, :], axis=AX_X))
                dve.tensor_copy(place[:, :, :], slotf[:, :, :]).then_inc(s_place, 1)

            def take_counts(part, lo, hi):
                dve.wait_ge(s_cnt, part + 1)
                n = hi - lo
                dve.tensor_copy(cnt[:, :, lo:hi, :], ps[:, 7, 0:2 * n * E].rearrange(
                    "p (a j e) -> p a j e", a=2, j=n)).then_inc(s_cntc, 1)
                dve.wait_ge(s_cntc, part + 1)

            def slots(lo, hi):
                js = slice(lo, hi)
                for j in range(lo, hi):
                    link(dve.tensor_tensor(cum[:, j + 1, :], cnt[:, 1, j, :], cum[:, j, :], ALU.add))
                link(dve.tensor_tensor(cand[:, js, :], cnt[:, 0, js, :], cum[:, js, :], ALU.add))
                for k in range(TOP_K):
                    link(dve.tensor_tensor(lsh[:, js, :], cand[:, js, :], oneh[:, k, js, :], ALU.mult))
                    link(dve.reduce_sum(slotf[:, k, js], lsh[:, js, :], axis=AX_X))
                dve.tensor_copy(slot[:, :, js], slotf[:, :, js]).then_inc(s_slots, 1)

            def block_table():
                link(dve.tensor_tensor(total[:, :], cum[:, NT, :], cum[:, 0, :], ALU.subtract))
                link(dve.tensor_tensor(cmpc[:, :, :],
                                       total[:, :].rearrange("p (e a) -> p e a", a=1).to_broadcast([P, E, NT]),
                                       iota_c[:, :].rearrange("p (a n) -> p a n", a=1).to_broadcast([P, E, NT]), ALU.is_gt))
                link(dve.reduce_sum(nblk[:, :], cmpc[:, :, :], axis=AX_X))
                link(dve.tensor_scalar(skip[:, :], nblk[:, :], -float(P), float(REG), ALU.mult, ALU.add))
                for e in range(E):
                    link(dve.tensor_tensor(bend[:, e + 1:e + 2], bend[:, e:e + 1], nblk[:, e:e + 1], ALU.add))
                link(dve.tensor_tensor(cmpn[:, :, :],
                                       iota_n[:, :].rearrange("p (n a) -> p n a", a=1).to_broadcast([P, MAX_BLOCKS, E]),
                                       bend[:, 1:E + 1].rearrange("p (a e) -> p a e", a=1).to_broadcast([P, MAX_BLOCKS, E]),
                                       ALU.is_ge))
                link(dve.reduce_sum(blkf[:, :], cmpn[:, :, :], axis=AX_X))
                link(dve.tensor_scalar_min(blkf[:, :], blkf[:, :], float(E - 1)))
                link(dve.tensor_copy(blk[:, :], blkf[:, :]))
                link(dve.tensor_tensor(cmpn[:, :, :], cmpn[:, :, :],
                                       skip[:, :].rearrange("p (a e) -> p a e", a=1).to_broadcast([P, MAX_BLOCKS, E]),
                                       ALU.mult))
                link(dve.reduce_sum(rowf[:, :], cmpn[:, :, :], axis=AX_X))
                link(dve.scalar_tensor_tensor(rowf[:, :], iota_n[:, :], float(P), rowf[:, :], ALU.mult, ALU.add))
                dve.tensor_copy(blkrow[:, :], rowf[:, :]).then_inc(s_blk, 1)

            steps(0)
            dve.wait_ge(s_xbo, B)
            loop(dve, 1, B - 1, steps)
            steps(B - 1)
            c = [A1 + NG * B - 1]
            x2T_copy(2)
            logits(0, B - 1, 2)
            dve.wait_ge(s_gl, 1)
            shift_logits(0, NT - TB)
            normalise(NG * B - 1, NG - 1)
            link(dve.memset(sh_hT[96:128, FC - 1, :], 1.0))
            link(dve.memset(bend[:, 0:1], 0.0))
            link(dve.tensor_copy(cum[:, 0, :], iota_r[:, :]))
            dve.wait_ge(s_sw, 16 * 11)
            choose(0, 0, NT - TB)
            sh_product(0, 0)
            for half in range(2):
                tile = NT - TB + 2 * half
                dve.wait_ge(s_lastp, half + 1)
                dve.tensor_tensor(xres[:, tile:tile + 2, :], ps[:, 4 + half, :].rearrange("p (j d) -> p j d", j=2),
                                  xres[:, tile:tile + 2, :], ALU.add).then_inc(s_lastx, 1)
            dve.wait_ge(s_lastx, 2)
            last = LN_X1 + N_LN * (B - 1)
            norm_stats(0, NT - TB)
            dve.wait_ge(s_ln, last + TB)
            norm_means()
            norm_var(last + 2 * TB)
            take_counts(0, 0, NT - TB)
            slots(0, NT - TB)
            norm_rstd(last + 2 * TB, 2 + B)
            norm_apply(last + N_LN, 0, NT - TB)
            sh_product(0, 1)
            sh_product(0, 2)
            logits(B - 1, B, 4)
            dve.wait_ge(s_gl, 2)
            shift_logits(NT - TB, NT)
            choose(1, NT - TB, NT)
            sh_add(0, 0)
            sh_add(0, 1)
            sh_product(1, 0)
            take_counts(1, NT - TB, NT)
            slots(NT - TB, NT)
            dve.tensor_copy(fill[:, :], cum[:, NT, :]).then_inc(s_fill, 1)
            sh_product(1, 1)
            sh_product(1, 2)
            block_table()
            sh_add(1, 0)
            sh_add(1, 1)
            for ch in range(EARLY):
                sh_product(SB, ch)
            weights(0, NT)
            places()
            dve.wait_ge(s_up1, FC * SB)
            link(dve.memset(e_hT[96:128, :, FC - 1, :], 1.0))
            dve.wait_ge(s_h1, FC * SB + EARLY)
            A3 = c[0]

            dve.wait_ge(s_ew, 16 * (3 * E + 4))

            def blocks(n, par):
                ex = dve.value_load(blk[0:1, bass.ds(n, 1)], min_val=0, max_val=E - 1)
                dve.wait_ge(s_upa, n + 1)
                if not isinstance(n, int) or n:
                    dve.wait_ge(s_z, n)
                dve.tensor_tensor(e_a[:, :], ps[:, 1 + 2 * par, 0:F], b13_sb[:, ex, 0:F], ALU.add).then_inc(s_dve, 1)
                dve.wait_ge(s_up, n + 3)
                dve.tensor_tensor(e_c[:, :], ps[:, 2 + 2 * par, 0:F], b13_sb[:, ex, F:2 * F], ALU.add).then_inc(s_upc, 1)
                dve.wait_ge(s_dve, A3 + 1 + n)
                dve.wait_ge(s_upc, n + 3)
                dve.wait_ge(s_h, n + 1)
                dve.tensor_tensor(e_z[:, par, :], e_a[:, :], e_c[:, :], ALU.mult).then_inc(s_z, 1)

            def results(n, par, r):
                dve.wait_ge(s_o, n + 3)
                dve.wait_ge(s_os[par], 16 * r + 16)
                dve.tensor_copy(e_o[:, par, :], ps[:, 6 + par, 0:D]).then_inc(s_oe, 1)

            blocks(0, 0)

            def pair(n, par, r):
                blocks(n + 1, 1 - par)
                results(n, par, r)

            NP = (MAX_BLOCKS - 1) // 2 * 2
            pairs(dve, NP, pair)
            for n in range(NP, MAX_BLOCKS):
                if n + 1 < MAX_BLOCKS:
                    blocks(n + 1, 1 - n % 2)
                results(n, n % 2, n // 2)

            A4 = A3 + MAX_BLOCKS

            def combine(j):
                dve.wait_ge(s_g[j % 4], 32 * (j // 4) + 32)
                dve.scalar_tensor_tensor(xres[:, j, :], gath[:, j % 4, 0, :], rw[:, 0, j:j + 1], xres[:, j, :],
                                         ALU.mult, ALU.add).then_inc(s_dve, 1)
                dve.wait_ge(s_dve, A4 + j + 1)
                dve.scalar_tensor_tensor(xres[:, j, :], gath[:, j % 4, 1, :], rw[:, 1, j:j + 1], xres[:, j, :],
                                         ALU.mult, ALU.add).then_inc(s_fin, 1)

            product, add = sh_product, sh_add
            between = {0: [(product, SB, 1)], 1: [(product, SB, 2)], 3: [(product, SB + 1, 0)],
                       5: [(add, SB, 0), (add, SB, 1)], 7: [(product, SB + 1, 1)], 9: [(product, SB + 1, 2)],
                       11: [(add, SB + 1, 0)], 13: [(add, SB + 1, 1)]}
            for j in range(NT):
                for step, b, part in between.get(j, []):
                    step(b, part)
                if j >= TB * SB and j % 2 == 0:
                    dve.wait_ge(s_y1, 1 + j // 2 + 1)
                combine(j)

        @block.tensor
        def _(pe):
            for s, n in ((s_kp, 2), (s_qp, 2), (s_vp, 2), (s_pv, 2), (s_dn1, 4), (s_xbp, 2),
                         (s_up, 2), (s_hp, 2), (s_o, 2)):
                pe.sem_inc(s, n)
            pe.wait_ge(s_const, 10)

            def project(b, par, r):
                def ctx_transpose():
                    pe.wait_ge(s_c[par], 16 * r + 16)
                    pe.wait_ge(s_v, 2 * b + 2)
                    for c in range(KC):
                        for j in range(TB):
                            ins = pe.transpose(ps[:, 2 + c, P * j:P * j + P], cst[:, par, j, P * c:P * c + P], ident[:, :])
                        ins.then_inc(s_cTp, 1)

                def tokens_transpose():
                    pe.wait_ge(s_xn, b + 1)
                    pe.wait_ge(s_xT, 2 * b + 2)
                    for c in range(KC):
                        for j in range(TB):
                            ins = pe.transpose(ps[:, c, P * j:P * j + P], xn_tile(b, j, c), ident[:, :])
                        ins.then_inc(s_xTp, 1)

                def k_product():
                    pe.wait_ge(s_cT, 2 * b + 4)
                    pe.wait_ge(s_kf, 2 * b + 2)
                    for c in range(KC):
                        for k in range(KC):
                            ins = pe.matmul(ps[:, 6 + c, :], wq_sb[:, k, P * c:P * c + P], cT[:, k, :],
                                            start=(k == 0), stop=(k == KC - 1))
                        ins.then_inc(s_kp, 1)

                if b == 0:
                    ctx_transpose()
                    pe.wait_ge(s_wq, 16)
                    k_product()
                    tokens_transpose()
                else:
                    tokens_transpose()
                    ctx_transpose()
                    k_product()
                pe.wait_ge(s_xT, 2 * b + 4)
                pe.wait_ge(s_qf, 2 * b + 2)
                for c in range(KC):
                    for k in range(KC):
                        ins = pe.matmul(ps[:, 4 + c, :], wq_sb[:, k, P * c:P * c + P], xT[:, k, :],
                                        start=(k == 0), stop=(k == KC - 1))
                    ins.then_inc(s_qp, 1)
                pe.wait_ge(s_kf, 2 * b + 4)
                for j in range(TB):
                    for c in range(KC):
                        ins = pe.transpose(ps[:, 2 + j // 2, D * (j % 2) + P * c:D * (j % 2) + P * c + P],
                                           kf[:, c, P * j:P * j + P], ident[:, :])
                    if j % 2:
                        ins.then_inc(s_vp, 1)

            def xn_tile(b, j, c):
                return xn[:, TB * b + j, P * c:P * c + P]

            for b in range(B):
                project(b, b % 2, b // 2)

            pe.wait_ge(s_v, 2 + 2 * B)
            pe.wait_ge(s_qf, 2 + 2 * B)
            pe.wait_ge(s_ones, 3)

            def scores_for_max(n, bank, slot_, u):
                j, c = u // TB, u % TB
                pe.wait_ge(s_rc, n + 1)
                pe.matmul(ps[:, BR + bank, :], q_st[0:SR, slot_, j, P * c:P * c + P], k_st[0:SR, slot_, j, :],
                          start=True, stop=True).then_inc(s_rp, 1)

            def maxima(n, bank, i):
                pe.wait_ge(s_rc, n + 1)
                pe.wait_ge(s_mp, i + 1)
                pe.transpose(ps[0:2 * GH * TB, BR + bank, 0:P // 2].bitcast(BF16),
                             mparts[:, :, :].rearrange("p a b -> p (a b)"), ident_b[:, :]).then_inc(s_rp, 1)

            def out_projection(n, bank, j):
                pe.wait_ge(s_rc, n + 1)
                for g in range(NG // 2):
                    ins = pe.matmul(ps[:, BR + bank, 0:D], aT[:, g, P * j:P * j + P], wo_sb[:, g, :],
                                    start=(g == 0), stop=(g == NG // 2 - 1))
                ins.then_inc(s_rp, 1)

            def weighted_sum(i, g, t):
                pe.wait_ge(s_exp, 4 + GH * (TB * i + t + 1))
                if t == 0:
                    pe.wait_ge(s_pvc, i + 1)
                    pe.wait_ge(s_vg, i + 1)
                for j in range(GH):
                    ins = pe.matmul(ps[32 * j:32 * j + 32, BPV, :], v_grp[:, g % 2, t, j, :],
                                    probs[:, 4 * (t % 2) + j, :], start=(t == 0), stop=(t == TB - 1))
                ins.then_inc(s_pv, 1)

            for n in range(2):
                pe.wait_ge(s_st[n], 16 * 6)
                for u in range(GH * TB):
                    k = n * (GH * TB + 1) + u
                    scores_for_max(k, k % RING, n, u)
                if n == 0:
                    maxima(GH * TB, (GH * TB) % RING, 0)

            def router_transpose(b, bank):
                pe.wait_ge(s_xn, B + b + 1)
                pe.wait_ge(s_gT, 2 * b + 2)
                for c in range(KC):
                    for j in range(TB):
                        ins = pe.transpose(ps[:, bank + c, P * j:P * j + P], xn_tile(b, j, c), ident[:, :])
                    ins.then_inc(s_gTp, 1)

            def router_product(b, bank):
                pe.wait_ge(s_gT, 2 * b + 4)
                for j in range(TB):
                    at = E * (TB * b + j if b < B - 1 else j)
                    for k in range(KC):
                        ins = pe.matmul(ps[:, bank, at:at + E], x2T[:, b, k, P * j:P * j + P], gw_sb[:, k, :],
                                        start=(k == 0), stop=(k == KC - 1))
                ins.then_inc(s_gp, 1)

            ROUTER_AT = {(2, 2): [(router_transpose, 0, 0)],
                         (2, 3): [(router_product, 0, 2), (router_transpose, 1, 0)],
                         (3, 0): [(router_product, 1, 2)],
                         (3, 2): [(router_transpose, 2, 0)],
                         (3, 3): [(router_product, 2, 2)]}

            def steps(b):
                offs, total = batch_units(b)
                rb = ring_base(b)
                for g in range(NG):
                    i = NG * b + g
                    with_wo, with_s1, with_m = kinds(b, g)
                    k = offs[g]
                    pe.wait_ge(s_mrow[g], 32 * (b + 1))
                    if with_s1:
                        b2_ = b if g + 2 < NG else b + 1
                        pe.wait_ge(s_st[(g + 2) % NG], 16 * 6 * (b2_ + 1))
                    for t in range(TB):
                        for j in range(GH):
                            n = GH * t + j
                            pe.wait_ge(s_exp, 4 + GH * TB * i + s2_before(n) + 1)
                            pe.matmul(ps[:, BS2 + S2_BANK[n], :], k_st[0:SR + 2, g, j, P * t:P * t + P],
                                      q_st[0:SR + 2, g, j, :], start=True, stop=True).then_inc(s_s2, 1)
                            if with_s1:
                                scores_for_max(rb + k, bank_of(b, k), (g + 2) % NG, t * TB + j)
                                k += 1
                            if t == 1 and j == 0 and with_m:
                                maxima(rb + k, bank_of(b, k), i + 1)
                                k += 1
                        if g == 1 and with_wo:
                            pe.wait_ge(s_norm, NG // 2 * b)
                            out_projection(rb + k, bank_of(b, k), t)
                            k += 1
                        if t > 0:
                            weighted_sum(i, g, t - 1)
                        elif not (isinstance(i, int) and i == 0):
                            weighted_sum(i - 1, (g - 1) % NG, TB - 1)
                        if with_wo and not with_s1:
                            for route, of_batch, bank in ROUTER_AT.get((g, t), []):
                                if of_batch == 0:
                                    pe.wait_ge(s_rc, RING + RING_END)
                                route(of_batch, bank)

            pe.wait_ge(s_wo, 16 * H)
            steps(0)
            loop(pe, 1, B - 1, steps)
            pe.wait_ge(s_sw, 16 * 11)
            steps(B - 1)
            weighted_sum(NG * B - 1, NG - 1, TB - 1)
            pe.wait_ge(s_exp, 4 + GH * TB * NG * B)

            def counts(part, lo, hi):
                pe.wait_ge(s_sel, part + 1)
                pe.wait_ge(s_y1, 2 * part + 1)
                sel = selb[:, lo:hi, :].rearrange("p j e -> p (j e)")
                n = (hi - lo) * E
                pe.matmul(ps[:, 7, 0:n], tri[:, :], sel, start=True, stop=True)
                pe.matmul(ps[:, 7, n:2 * n], ones_b[:, :], sel, start=True, stop=True).then_inc(s_cnt, 1)

            def sh_up(b, c):
                n = FC * b + c
                rows = P if c < FC - 1 else FL
                if n >= 2:
                    pe.wait_ge(s_z1, n - 1)
                for half in range(2):
                    for k in range(KC):
                        ins = pe.matmul(ps[0:rows, 2 * (n % 2) + half, :],
                                        sw13_sb[:, k, F * half + P * c:F * half + P * c + rows],
                                        x2T[:, b, k, :], start=(k == 0), stop=(k == KC - 1))
                ins.then_inc(s_up1, 1)

            def sh_down(b):
                pe.wait_ge(s_h1, FC * b + FC)
                pe.wait_ge(s_y1, 2 * b + 1)
                for j in range(TB):
                    for c in range(FC):
                        rows = P if c < FC - 1 else FL + 1
                        ins = pe.matmul(ps[:, 6 + j // 2, D * (j % 2):D * (j % 2) + D], sh_hT[0:rows, c, P * j:P * j + P],
                                        sw2_sb[0:rows, c, :], start=(c == 0), stop=(c == FC - 1))
                    ins.then_inc(s_dn1, 1)

            sh_up(0, 0)
            pe.wait_ge(s_norm, NG // 2 * B)
            for j in range(TB):
                for g in range(NG // 2):
                    ins = pe.matmul(ps[:, 4 + j // 2, D * (j % 2):D * (j % 2) + D], aT[:, g, P * j:P * j + P],
                                    wo_sb[:, g, :], start=(g == 0), stop=(g == NG // 2 - 1))
                if j % 2:
                    ins.then_inc(s_lastp, 1)
            pe.wait_ge(s_gl, 1)
            pe.wait_ge(s_pvc, 1 + NG * B)
            counts(0, 0, NT - TB)
            sh_up(0, 1)
            sh_up(0, 2)
            pe.wait_ge(s_lastx, 2)
            router_transpose(B - 1, 4)
            router_product(B - 1, 4)
            pe.wait_ge(s_cntc, 1)
            sh_down(0)
            sh_up(1, 0)
            counts(1, NT - TB, NT)
            sh_up(1, 1)
            sh_up(1, 2)
            pe.wait_ge(s_cntc, 2)
            sh_down(1)
            for c in range(EARLY):
                sh_up(SB, c)
            pe.wait_ge(s_ew, 16 * (3 * E + 4))
            pe.wait_ge(s_blk, 1)
            pe.wait_ge(s_gl, 2)
            pe.wait_ge(s_y1, 1 + 2 * SB)
            pe.wait_ge(s_z1, FC * SB + EARLY)

            def expert_of(n):
                return pe.value_load(blk[0:1, bass.ds(n, 1)], min_val=0, max_val=E - 1)

            def x_transpose(n, par, r):
                pe.wait_ge(s_xb[par], 16 * r + 16)
                pe.wait_ge(s_xbe, n + 1)
                for k in range(KC):
                    ins = pe.transpose(ps[:, 0, P * k:P * k + P], xb[:, par, P * k:P * k + P], ident[:, :])
                ins.then_inc(s_xbp, 1)

            def up(n, par, half, ex):
                if half == 0:
                    pe.wait_ge(s_xbe, n + 2)
                    pe.wait_ge(s_upc, n + 1)
                for k in range(KC):
                    ins = pe.matmul(ps[:, 1 + 2 * par + half, 0:F], xbT[:, par, k, :],
                                    w13_sb[:, ex, k, F * half:F * half + F], start=(k == 0), stop=(k == KC - 1))
                ins.then_inc((s_upa, s_up)[half], 1)

            def h_transpose(n, par):
                pe.wait_ge(s_h, n + 3)
                pe.wait_ge(s_hT, n + 1)
                for c in range(FC):
                    rows = P if c < FC - 1 else FL
                    ins = pe.transpose(ps[0:rows, 5, P * c:P * c + P], e_h[:, par, P * c:P * c + rows], ident[:, :])
                ins.then_inc(s_hp, 1)

            def down(n, par, ex):
                pe.wait_ge(s_hT, n + 2)
                pe.wait_ge(s_oe, n + 1)
                for c in range(FC):
                    rows = P if c < FC - 1 else FL + 1
                    ins = pe.matmul(ps[:, 6 + par, 0:D], e_hT[0:rows, par, c, :], w2_sb[0:rows, ex, c, :],
                                    start=(c == 0), stop=(c == FC - 1))
                ins.then_inc(s_o, 1)

            def step(n, par, r):
                if not isinstance(n, int) or n + 1 < MAX_BLOCKS:
                    ex_next = expert_of(n + 1)
                    up(n + 1, 1 - par, 0, ex_next)
                h_transpose(n, par)
                if not isinstance(n, int) or n + 2 < MAX_BLOCKS:
                    x_transpose(n + 2, par, r + 1)
                if not isinstance(n, int) or n + 1 < MAX_BLOCKS:
                    up(n + 1, 1 - par, 1, ex_next)
                down(n, par, expert_of(n))

            x_transpose(0, 0, 0)
            x_transpose(1, 1, 0)
            ex_first = expert_of(0)
            up(0, 0, 0, ex_first)
            up(0, 0, 1, ex_first)
            NP = (MAX_BLOCKS - 2) // 2 * 2
            pairs(pe, NP, step)
            for n in range(NP, MAX_BLOCKS):
                step(n, n % 2, n // 2)

            pe.wait_ge(s_xbe, 1 + MAX_BLOCKS)
            pe.wait_ge(s_upc, 2 + MAX_BLOCKS)
            for c in range(EARLY, FC):
                sh_up(SB, c)
            sh_up(SB + 1, 0)
            pe.wait_ge(s_oe, 2 + MAX_BLOCKS)
            sh_down(SB)
            for c in range(1, FC):
                sh_up(SB + 1, c)
            sh_down(SB + 1)


_NAMES = ["x", "ctx_1024", "L0_xattn_Wq", "L0_xattn_bq", "L0_xattn_Wo", "L0_xattn_bo", "L0_ffn_gate_w",
          "L0_ffn_gate_b", "L0_ffn_w1", "L0_ffn_b1", "L0_ffn_w3", "L0_ffn_b3", "L0_ffn_w2", "L0_ffn_b2",
          "L0_ffn_sw1", "L0_ffn_sb1", "L0_ffn_sw3", "L0_ffn_sb3", "L0_ffn_sw2", "L0_ffn_sb2"]


def kernel(**inputs):
    import numpy as _np
    import concourse.bacc as _bacc
    from concourse import mybir as _mybir
    from concourse.bass_utils import run_bass_kernel_spmd as _run

    nc = _bacc.Bacc("TRN2", target_bir_lowering=False, num_devices=1)
    arrays, args = {}, []
    for name in _NAMES:
        a = _np.asarray(inputs[name])
        if name == "L0_ffn_gate_w":
            a = a.T
        if name in ("L0_xattn_Wq", "L0_xattn_bq"):
            a = _np.swapaxes(a.reshape(a.shape[:-1] + (4, 4, 16)), -1, -2).reshape(a.shape)
        a = _np.ascontiguousarray(a)
        arrays[f"in_{name}"] = a
        args.append(nc.dram_tensor(f"in_{name}", a.shape, _mybir.dt.from_np(a.dtype), kind="ExternalInput").ap())
    shape = inputs["x"].shape
    out = nc.dram_tensor("out_x", shape, _mybir.dt.float32, kind="ExternalOutput").ap()
    xattn_moe_kernel(nc, *args, out)
    r = _run(nc, [arrays], core_ids=[0])
    return r.results[0]["out_x"]
```
